# Optimizing a Trainium2 kernel written in Bass

```python
import numpy as np
import jax
import jax.numpy as jnp

def _softmax(x, axis=-1):
    return jax.nn.softmax(x, axis=axis)

def _gelu(x):
    return jax.nn.gelu(x, approximate=True)

def _silu(x):
    return jax.nn.silu(x)

def _sigmoid(x):
    return jax.nn.sigmoid(x)

def _layernorm(x, axis=-1, eps=1e-05):
    m = jnp.mean(x, axis=axis, keepdims=True)
    v = jnp.var(x, axis=axis, keepdims=True)
    return (x - m) / jnp.sqrt(v + eps)

def _scatter_add(tgt, idx, src, axis=0):
    return tgt.at[idx].add(src)

def _segment_sum(src, seg, n):
    return jax.ops.segment_sum(src, seg, n)
kernel_name = 'mk_vit_tower_d1_tok_img1024_r4_6f4315'

def setup_inputs(seed: int=0):
    np.random.seed(seed)
    _w = jnp.asarray

    def _rec_inputs():
        import jax
        import jax.numpy as jnp
        _rk = jax.random.key(seed)
        x = -0.00016672 + 0.999947 * jax.random.normal(jax.random.fold_in(_rk, 1), (64, 3, 96, 96), jnp.float32)
        return x
    x = _rec_inputs()

    def _L0_tok_setup():
        import jax, jax.numpy as jnp
        import numpy as np
        EMBED_DIM = 256
        IMAGE_SIZE = 96
        CHANNELS = 3
        PATCH = 16
        NUM_PATCHES = (IMAGE_SIZE // PATCH) ** 2
        PATCH_DIM = PATCH * PATCH * CHANNELS

        def _patchify(x, patch):
            B, C, H, W = x.shape
            hp, wp = (H // patch, W // patch)
            x = x.reshape(B, C, hp, patch, wp, patch)
            x = x.transpose(0, 2, 4, 1, 3, 5)
            return x.reshape(B, hp * wp, C * patch * patch)
        key = jax.random.key(seed)
        k_x, k_w, k_b, k_cls, k_pos = jax.random.split(key, 5)
        x = jax.random.normal(k_x, (64, CHANNELS, IMAGE_SIZE, IMAGE_SIZE), dtype=jnp.float32)
        W = jax.random.normal(k_w, (EMBED_DIM, PATCH_DIM), dtype=jnp.float32) / np.sqrt(PATCH_DIM)
        b = jax.random.normal(k_b, (EMBED_DIM,), dtype=jnp.float32) * 0.01
        cls_token = jax.random.normal(k_cls, (1, 1, EMBED_DIM), dtype=jnp.float32)
        pos_embedding = jax.random.normal(k_pos, (1, 1 + NUM_PATCHES, EMBED_DIM), dtype=jnp.float32)
        return {'x': x, 'W': W, 'b': b, 'cls_token': cls_token, 'pos_embedding': pos_embedding}
    _L0_tok_all = _L0_tok_setup()
    _L0_tok_in = {k: v for k, v in _L0_tok_all.items() if k in ('W', 'b', 'cls_token', 'pos_embedding')}
    del _L0_tok_all

    def _L0_attn_setup():
        import jax, jax.numpy as jnp
        import numpy as np
        B, S, D = (4, 512, 256)
        H = 16
        HD = D // H
        key = jax.random.key(seed)
        ks = jax.random.split(key, 6)
        s = 1.0 / np.sqrt(D)
        x = jax.random.normal(ks[0], (B, S, D), dtype=jnp.float32)
        Wq = jax.random.uniform(ks[1], (D, D), jnp.float32, -s, s)
        Wk = jax.random.uniform(ks[2], (D, D), jnp.float32, -s, s)
        Wv = jax.random.uniform(ks[3], (D, D), jnp.float32, -s, s)
        Wo = jax.random.uniform(ks[4], (D, D), jnp.float32, -s, s)
        bo = jax.random.uniform(ks[5], (D,), jnp.float32, -s, s)
        return {'x': x, 'Wq': Wq, 'Wk': Wk, 'Wv': Wv, 'Wo': Wo, 'bo': bo}
    _L0_attn_all = _L0_attn_setup()
    _L0_attn_in = {k: v for k, v in _L0_attn_all.items() if k in ('Wq', 'Wk', 'Wv', 'Wo', 'bo')}
    del _L0_attn_all

    def _L0_ffn_setup():
        import jax, jax.numpy as jnp
        import numpy as np
        B, S, D = (1, 512, 256)
        E, K, F = (64, 8, 192)
        SF = 192
        C = 128
        ROUTED_SCALE = 1.0

        def _moe_forward(x, router_w, w_gate, w_up, w_down, ws_gate_up, ws_down):
            T = x.shape[0]
            logits = x.astype(jnp.float32) @ router_w.T
            probs = jax.nn.softmax(logits, axis=-1)
            topk_w, topk_ids = jax.lax.top_k(probs, K)
            topk_w = topk_w / jnp.sum(topk_w, axis=-1, keepdims=True)
            topk_w = topk_w.astype(x.dtype)
            N = T * K
            flat_e = topk_ids.reshape(-1)
            flat_w = topk_w.reshape(-1)
            tok = jnp.arange(N) // K
            onehot = flat_e[:, None] == jnp.arange(E)[None, :]
            pos = jnp.cumsum(onehot, axis=0)[jnp.arange(N), flat_e] - 1
            valid = pos < C
            idx = jnp.where(valid, flat_e * C + pos, E * C)
            x_buf = jnp.zeros((E * C + 1, x.shape[1]), x.dtype).at[idx].set(x[tok])
            xb = x_buf[:E * C].reshape(E, C, -1)
            g = jnp.einsum('ecd,edf->ecf', xb, w_gate)
            u = jnp.einsum('ecd,edf->ecf', xb, w_up)
            h = jax.nn.silu(g) * u
            y = jnp.einsum('ecf,efd->ecd', h, w_down).reshape(E * C, -1)
            safe = jnp.where(valid, idx, 0)
            contrib = y[safe] * (flat_w * valid.astype(flat_w.dtype))[:, None]
            routed = jax.ops.segment_sum(contrib, tok, num_segments=T)
            routed = routed * ROUTED_SCALE
            gu = x @ ws_gate_up
            sg, su = (gu[:, :SF], gu[:, SF:])
            shared = jax.nn.silu(sg) * su @ ws_down
            return routed + shared
        key = jax.random.key(seed)
        ks = jax.random.split(key, 7)
        w = 0.02
        return {'hidden_states': jax.random.normal(ks[0], (B, S, D), jnp.float32), 'router_w': jax.random.normal(ks[1], (E, D), jnp.float32) * w, 'w_gate': jax.random.normal(ks[2], (E, D, F), jnp.float32) * w, 'w_up': jax.random.normal(ks[3], (E, D, F), jnp.float32) * w, 'w_down': jax.random.normal(ks[4], (E, F, D), jnp.float32) * w, 'ws_gate_up': jax.random.normal(ks[5], (D, 2 * SF), jnp.float32) * w, 'ws_down': jax.random.normal(ks[6], (SF, D), jnp.float32) * w}
    _L0_ffn_all = _L0_ffn_setup()
    _L0_ffn_in = {k: v for k, v in _L0_ffn_all.items() if k in ('router_w', 'w_gate', 'w_up', 'w_down', 'ws_gate_up', 'ws_down')}
    del _L0_ffn_all
    return {'x': x, 'L0_tok_W': _L0_tok_in['W'], 'L0_tok_b': _L0_tok_in['b'], 'L0_tok_cls_token': _L0_tok_in['cls_token'], 'L0_tok_pos_embedding': _L0_tok_in['pos_embedding'], 'L0_attn_Wq': _L0_attn_in['Wq'], 'L0_attn_Wk': _L0_attn_in['Wk'], 'L0_attn_Wv': _L0_attn_in['Wv'], 'L0_attn_Wo': _L0_attn_in['Wo'], 'L0_attn_bo': _L0_attn_in['bo'], 'L0_ffn_router_w': _L0_ffn_in['router_w'], 'L0_ffn_w_gate': _L0_ffn_in['w_gate'], 'L0_ffn_w_up': _L0_ffn_in['w_up'], 'L0_ffn_w_down': _L0_ffn_in['w_down'], 'L0_ffn_ws_gate_up': _L0_ffn_in['ws_gate_up'], 'L0_ffn_ws_down': _L0_ffn_in['ws_down']}

def reference(x, L0_tok_W, L0_tok_b, L0_tok_cls_token, L0_tok_pos_embedding, L0_attn_Wq, L0_attn_Wk, L0_attn_Wv, L0_attn_Wo, L0_attn_bo, L0_ffn_router_w, L0_ffn_w_gate, L0_ffn_w_up, L0_ffn_w_down, L0_ffn_ws_gate_up, L0_ffn_ws_down):
    import jax
    import jax.numpy as jnp

    def _L0_tok_ref(x, W, b, cls_token, pos_embedding):
        import jax, jax.numpy as jnp
        import numpy as np
        EMBED_DIM = 256
        IMAGE_SIZE = 96
        CHANNELS = 3
        PATCH = 16
        NUM_PATCHES = (IMAGE_SIZE // PATCH) ** 2
        PATCH_DIM = PATCH * PATCH * CHANNELS

        def _patchify(x, patch):
            B, C, H, W = x.shape
            hp, wp = (H // patch, W // patch)
            x = x.reshape(B, C, hp, patch, wp, patch)
            x = x.transpose(0, 2, 4, 1, 3, 5)
            return x.reshape(B, hp * wp, C * patch * patch)
        B = x.shape[0]
        patches = _patchify(x, PATCH)
        tokens = jnp.einsum('bnd,ed->bne', patches, W) + b
        cls = jnp.broadcast_to(cls_token, (B, 1, EMBED_DIM))
        out = jnp.concatenate([cls, tokens], axis=1)
        return out + pos_embedding

    def _L0_attn_ref(x, Wq, Wk, Wv, Wo, bo):
        import jax, jax.numpy as jnp
        import numpy as np
        B, S, D = (4, 512, 256)
        H = 16
        HD = D // H
        b, n, _ = x.shape
        q = (x @ Wq).reshape(b, n, H, HD).transpose(0, 2, 1, 3)
        k = (x @ Wk).reshape(b, n, H, HD).transpose(0, 2, 1, 3)
        v = (x @ Wv).reshape(b, n, H, HD).transpose(0, 2, 1, 3)
        scores = jnp.einsum('bhqd,bhkd->bhqk', q, k) / np.sqrt(HD).astype(np.float32)
        causal = jnp.tril(jnp.ones((n, n), dtype=bool))
        scores = jnp.where(causal, scores, -jnp.inf)
        attn = jax.nn.softmax(scores, axis=-1)
        ctx = jnp.einsum('bhqk,bhkd->bhqd', attn, v)
        ctx = ctx.transpose(0, 2, 1, 3).reshape(b, n, D)
        return ctx @ Wo + bo

    def _L0_ffn_ref(hidden_states, router_w, w_gate, w_up, w_down, ws_gate_up, ws_down):
        import jax, jax.numpy as jnp
        import numpy as np
        B, S, D = (1, 512, 256)
        E, K, F = (64, 8, 192)
        SF = 192
        C = 128
        ROUTED_SCALE = 1.0

        def _moe_forward(x, router_w, w_gate, w_up, w_down, ws_gate_up, ws_down):
            T = x.shape[0]
            logits = x.astype(jnp.float32) @ router_w.T
            probs = jax.nn.softmax(logits, axis=-1)
            topk_w, topk_ids = jax.lax.top_k(probs, K)
            topk_w = topk_w / jnp.sum(topk_w, axis=-1, keepdims=True)
            topk_w = topk_w.astype(x.dtype)
            N = T * K
            flat_e = topk_ids.reshape(-1)
            flat_w = topk_w.reshape(-1)
            tok = jnp.arange(N) // K
            onehot = flat_e[:, None] == jnp.arange(E)[None, :]
            pos = jnp.cumsum(onehot, axis=0)[jnp.arange(N), flat_e] - 1
            valid = pos < C
            idx = jnp.where(valid, flat_e * C + pos, E * C)
            x_buf = jnp.zeros((E * C + 1, x.shape[1]), x.dtype).at[idx].set(x[tok])
            xb = x_buf[:E * C].reshape(E, C, -1)
            g = jnp.einsum('ecd,edf->ecf', xb, w_gate)
            u = jnp.einsum('ecd,edf->ecf', xb, w_up)
            h = jax.nn.silu(g) * u
            y = jnp.einsum('ecf,efd->ecd', h, w_down).reshape(E * C, -1)
            safe = jnp.where(valid, idx, 0)
            contrib = y[safe] * (flat_w * valid.astype(flat_w.dtype))[:, None]
            routed = jax.ops.segment_sum(contrib, tok, num_segments=T)
            routed = routed * ROUTED_SCALE
            gu = x @ ws_gate_up
            sg, su = (gu[:, :SF], gu[:, SF:])
            shared = jax.nn.silu(sg) * su @ ws_down
            return routed + shared
        b, s, d = hidden_states.shape
        x = hidden_states.reshape(-1, d)
        out = _moe_forward(x, router_w, w_gate, w_up, w_down, ws_gate_up, ws_down)
        return out.reshape(b, s, d)
    h = _L0_tok_ref(x, L0_tok_W, L0_tok_b, L0_tok_cls_token, L0_tok_pos_embedding)
    h = h + _L0_attn_ref(_layernorm(h, axis=-1), L0_attn_Wq, L0_attn_Wk, L0_attn_Wv, L0_attn_Wo, L0_attn_bo)
    h = h + _L0_ffn_ref(_layernorm(h, axis=-1), L0_ffn_router_w, L0_ffn_w_gate, L0_ffn_w_up, L0_ffn_w_down, L0_ffn_ws_gate_up, L0_ffn_ws_down)
    return h

_drawn_inputs = setup_inputs


def setup_inputs(seed=0):
    import zlib

    import numpy as np

    out = dict(_drawn_inputs(seed))
    spreads = {}
    factors = {'L0_tok_b': 7.976,
     'L0_ffn_router_w': 8.0,
     'L0_ffn_w_gate': 8.0,
     'L0_ffn_w_up': 8.0,
     'L0_ffn_w_down': 8.0,
     'L0_ffn_ws_gate_up': 5.561,
     'L0_ffn_ws_down': 5.533}
    for name, (base, spread) in spreads.items():
        noise = np.random.default_rng([zlib.crc32(name.encode()), seed]).standard_normal(out[name].shape)
        drawn = base * np.exp(spread * noise) if base else spread * noise
        out[name] = jnp.asarray(drawn.astype(out[name].dtype))
    for name, factor in factors.items():
        out[name] = (out[name] * factor).astype(out[name].dtype)
    return out
```

```python
from contextlib import ExitStack

import concourse.bass as bass
from concourse import mybir

F32 = mybir.dt.float32
BF16 = mybir.dt.bfloat16
U32 = mybir.dt.uint32
I32 = mybir.dt.int32
ALU = mybir.AluOpType
ACT = mybir.ActivationFunctionType
AX = mybir.AxisListType.X

P = 128
BANK = 512
IMAGES, CH, SIDE, PATCH = 64, 3, 96, 16
PS = SIDE // PATCH
NP = PS * PS
S = NP + 1
D = 256
KD = D // P
H, HD = 16, 16
GI = 3
R = GI * S
GROUPS = -(-IMAGES // GI)
T = IMAGES * S
HC = H // KD
PH = 3
PC = -(-H // PH)
VW = HD + 1
E, TOPK, F, CAP = 64, 8, 192, 128
FC, FP = 2, F // 2
SLOTS = E * CAP
ROW = D + E + 1
NEG = -1e30
EPS = 1e-5
PAIR_ROWS = 2 * GI * CH * PS
PT_C = 2 * GI * S
HALF = 2
XCH = CH * HALF
RING = 16
EW = 2 * KD * F + FC * D


class Group:

    def __init__(self, b, c):
        self.q = 2 * b + c
        self.u = c % 2
        self.pair = b + c // 2
        last = isinstance(self.q, int) and self.q == GROUPS - 1
        self.images = IMAGES - GI * (GROUPS - 1) if last else GI
        self.rows = self.images * S


def vit_kernel(nc, x, W, b, cls, pos, Wq, Wk, Wv, Wo, bo, router_w, w_gate, w_up, w_down, ws_gate_up, ws_down, out):
    ctx = ExitStack()
    with ctx:
        def sb(name, shape, dt=F32):
            return ctx.enter_context(nc.sbuf_tensor(name, shape, dt))

        def sem(name):
            return ctx.enter_context(nc.semaphore(name))

        slots = nc.dram_tensor("slots", [SLOTS, ROW], F32, kind="Internal").ap()
        acc = [nc.dram_tensor(f"acc{i}", [T + P, D], F32, kind="Internal").ap() for i in range(2)]

        ident = sb("ident", [P, P])
        before = sb("before", [P, R], BF16)
        ones = sb("ones", [P, R], BF16)
        headmask = sb("headmask", [P, HC])
        third = sb("third", [P, PC, PH])
        tri = sb("tri", [P, GI, S])
        causal = sb("causal", [P, S])
        posb = sb("posb", [P, D])
        posadd = sb("posadd", [P, D])
        bo_sb = sb("bo_sb", [P, D])
        base = sb("base", [P, E])
        halfneg = sb("halfneg", [P, 1])
        spare = sb("spare", [P, 1])
        empty = sb("empty", [P, ROW])
        wraw = sb("wraw", [P, KD, CH * PATCH * PATCH])
        rraw = sb("rraw", [E, D])
        wT = sb("wT", [P, XCH, D])
        wqk = sb("wqk", [P, KD, 2 * D])
        wv = sb("wv", [P, KD, D])
        wo = sb("wo", [P, KD, D])
        rT = sb("rT", [P, KD, E])
        wsgu = sb("wsgu", [P, KD, 2 * F])
        wsd = sb("wsd", [FP, FC, D])
        xraw = sb("xraw", [PAIR_ROWS, PATCH * SIDE])
        xw = sb("xw", [PAIR_ROWS, PS, PATCH * PATCH])
        pT = sb("pT", [P, XCH, PT_C])
        h = [sb(f"h{u}", [P, D]) for u in range(2)]
        hb = [sb(f"hb{u}", [P, D]) for u in range(2)]
        st1 = sb("st1", [P, 6])
        mv1 = sb("mv1", [P, 2])
        ve1 = sb("ve1", [P, 1])
        rs1 = sb("rs1", [P, 1])
        xn = sb("xn", [P, D])
        xnT = sb("xnT", [P, KD, GI, PH, S])
        qz = sb("qz", [P, KD, GI, R])
        kz = sb("kz", [P, KD, HC, R])
        vz = sb("vz", [R, GI, PC * PH, VW])
        sm = sb("sm", [P, H, S])
        mx = sb("mx", [P, H])
        sx = sb("sx", [P, H, S])
        prob = sb("prob", [P, H * S])
        probT = sb("probT", [P, PC, R])
        ctxsum = sb("ctxsum", [P, PC * PH, VW])
        rden = sb("rden", [P, H])
        cx = sb("cx", [P, H, HD])
        cxT = sb("cxT", [P, KD, R])
        h2 = [sb(f"h2{u}", [P, D]) for u in range(2)]
        st2 = sb("st2", [P, 6])
        mv2 = sb("mv2", [P, 2])
        ve2 = sb("ve2", [P, 1])
        rs2 = sb("rs2", [P, 1])
        xs = [sb(f"xs{u}", [P, ROW]) for u in range(2)]
        xn2T = sb("xn2T", [P, KD, R])
        lg = sb("lg", [P, E])
        top = sb("top", [P, TOPK])
        cut = sb("cut", [P, E])
        shifted = sb("shifted", [P, E])
        chosen = [sb(f"chosen{u}", [P, E], BF16) for u in range(2)]
        earlier = [sb(f"earlier{u}", [P, E], BF16) for u in range(2)]
        ex = sb("ex", [P, E])
        em = sb("em", [P, E])
        wsum = sb("wsum", [P, 1])
        wrec = sb("wrec", [P, 1])
        room = sb("room", [P, E])
        fits = sb("fits", [P, E])
        code = sb("code", [P, E])
        top2 = sb("top2", [P, TOPK])
        idx = [sb(f"idx{u}", [P, TOPK], U32) for u in range(2)]
        th = sb("th", [FP, FC, R])
        g1 = sb("g1", [FP, FC, R])
        hs = sb("hs", [FP, FC, R])
        res = [sb(f"res{u}", [P, D]) for u in range(2)]
        ew = sb("ew", [P, RING, EW])
        xrow = [sb(f"xrow{c}", [P, ROW]) for c in range(4)]
        xT = [sb(f"xT{u}", [P, KD, P]) for u in range(2)]
        sg = [sb(f"sg{u}", [P, F]) for u in range(2)]
        hh = [sb(f"hh{u}", [P, F]) for u in range(2)]
        hT = [sb(f"hT{u}", [FP, FC, P]) for u in range(2)]
        ysc = [sb(f"ysc{u}", [P, D]) for u in range(2)]

        ps = ctx.enter_context(nc.psum_tensor("ps", [P, 8, BANK], F32))

        x_landed = sem("x_landed")
        x_sorted = sem("x_sorted")
        w_landed = sem("w_landed")
        small_landed = sem("small_landed")
        consts_made = sem("consts_made")
        zeros_made = sem("zeros_made")
        masks_made = sem("masks_made")
        posb_made = sem("posb_made")
        dve_const = sem("dve_const")
        slots_cleared = sem("slots_cleared")
        wT_turned = sem("wT_turned")
        wT_copied = sem("wT_copied")
        patches_turned = sem("patches_turned")
        patches_copied = sem("patches_copied")
        embedded = sem("embedded")
        h_ready = sem("h_ready")
        hb_ready = sem("hb_ready")
        ln1_stats = sem("ln1_stats")
        ln1_mean = sem("ln1_mean")
        ln1_var = sem("ln1_var")
        ln1_rstd = sem("ln1_rstd")
        xn_ready = sem("xn_ready")
        xn_turned = sem("xn_turned")
        xnT_ready = sem("xnT_ready")
        qk_done = sem("qk_done")
        q_ready = sem("q_ready")
        k_ready = sem("k_ready")
        v_done = sem("v_done")
        v_ready = sem("v_ready")
        scores_done = sem("scores_done")
        masked = sem("masked")
        max_ready = sem("max_ready")
        lowered = sem("lowered")
        prob_ready = sem("prob_ready")
        prob_turned = sem("prob_turned")
        probT_ready = sem("probT_ready")
        pv_done = sem("pv_done")
        sum_a = sem("sum_a")
        sum_b = sem("sum_b")
        sum_ready = sem("sum_ready")
        rden_ready = sem("rden_ready")
        cx_ready = sem("cx_ready")
        cx_turned = sem("cx_turned")
        cxT_ready = sem("cxT_ready")
        wo_done = sem("wo_done")
        h2_ready = sem("h2_ready")
        ln2_stats = sem("ln2_stats")
        ln2_mean = sem("ln2_mean")
        ln2_var = sem("ln2_var")
        ln2_rstd = sem("ln2_rstd")
        xn2_ready = sem("xn2_ready")
        xn2_turned = sem("xn2_turned")
        xn2T_ready = sem("xn2T_ready")
        router_done = sem("router_done")
        logits_ready = sem("logits_ready")
        top_ready = sem("top_ready")
        cut_ready = sem("cut_ready")
        chosen_ready = sem("chosen_ready")
        shifted_ready = sem("shifted_ready")
        ex_ready = sem("ex_ready")
        em_ready = sem("em_ready")
        wrec_ready = sem("wrec_ready")
        row_ready = sem("row_ready")
        earlier_ready = sem("earlier_ready")
        places_done = sem("places_done")
        room_ready = sem("room_ready")
        fits_ready = sem("fits_ready")
        code_ready = sem("code_ready")
        top2_ready = sem("top2_ready")
        idx_ready = sem("idx_ready")
        scattered = [sem(f"scattered{u}") for u in range(2)]
        gu_done = sem("gu_done")
        tanh_ready = sem("tanh_ready")
        g1_ready = sem("g1_ready")
        hs_ready = sem("hs_ready")
        down_done = sem("down_done")
        res_ready = sem("res_ready")
        res_stored = [sem(f"res_stored{u}") for u in range(2)]
        ew_landed = [sem(f"ew_landed{u}") for u in range(2)]
        row_landed = [sem(f"row_landed{c}") for c in range(4)]
        row_turned = sem("row_turned")
        xT_ready = sem("xT_ready")
        e_gu_done = sem("e_gu_done")
        silu_ready = sem("silu_ready")
        hh_ready = sem("hh_ready")
        hh_turned = sem("hh_turned")
        hT_ready = sem("hT_ready")
        e_down_done = sem("e_down_done")
        ysc_ready = sem("ysc_ready")
        added = [sem(f"added{u}") for u in range(2)]
        waits_carried = sem("waits_carried")
        out_ready = sem("out_ready")
        out_stored = sem("out_stored")

        block = ctx.enter_context(nc.Block())

        CONSTS = 19
        SMALL = 16 * (2 * GI + 2)
        WEIGHTS = 16 * 10
        PAIRS = GROUPS // 2
        EPAIRS = E // 2

        def x_pair(pair, images):
            rows = images * CH * PS
            src = x.rearrange("n c (r i) w -> (n c r) (i w)", i=PATCH)
            return xraw[0:rows, :], src[bass.ds(pair * PAIR_ROWS, rows), :]

        MAIN = T // P
        OUT_PARTS = [(P, r, 6) for r in range(0, MAIN, 6)] + [(T - MAIN * P, MAIN, 1)]
        sums_landed = [sem(f"sums_landed{n}") for n in range(len(OUT_PARTS))]
        flat = ew[:, :, :].rearrange("p a b -> p (a b)")

        def out_tile(k, n):
            parts, at, rows = OUT_PARTS[n]
            lo = (k * (MAIN + 1) + at) * D
            return flat[0:parts, lo:lo + rows * D]

        def out_rows(dram, n):
            parts, at, rows = OUT_PARTS[n]
            if at == MAIN:
                return dram[MAIN * P:T, :]
            return dram[0:MAIN * P, :].rearrange("(p r) d -> p r d", p=P)[:, at:at + rows, :].rearrange("p r d -> p (r d)")

        @block.sync
        def _(sp):
            sp.dma_start(*x_pair(0, 2 * GI)).then_inc(x_landed, 16)
            sp.dma_start(wraw[:, :, :], W.rearrange("(k p) d -> p k d", p=P)).then_inc(w_landed, 16)
            for i in range(GI):
                sp.dma_start(posb[S * i:S * i + S, :], pos[0, :, :]).then_inc(small_landed, 16)
                sp.dma_start(posadd[S * i:S * i + 1, :], cls[0, :, :]).then_inc(small_landed, 16)
                sp.dma_start(posadd[S * i + 1:S * i + S, :],
                             b.rearrange("(o d) -> o d", o=1).broadcast_to([NP, D])).then_inc(w_landed, 16)
            sp.dma_start(wqk[:, :, 0:D], Wq.rearrange("(k p) n -> p k n", p=P)).then_inc(w_landed, 16)
            sp.dma_start(wqk[:, :, D:2 * D], Wk.rearrange("(k p) n -> p k n", p=P)).then_inc(w_landed, 16)
            sp.dma_start(wv[:, :, :], Wv.rearrange("(k p) n -> p k n", p=P)).then_inc(w_landed, 16)
            sp.dma_start(bo_sb[0:R, :], bo.rearrange("(o d) -> o d", o=1).broadcast_to([R, D])).then_inc(small_landed, 16)
            sp.dma_start(rraw[:, :], router_w).then_inc(small_landed, 16)
            sp.dma_start(wo[:, :, :], Wo.rearrange("(k p) n -> p k n", p=P)).then_inc(w_landed, 16)
            sp.dma_start(wsgu[:, :, :], ws_gate_up.rearrange("(k p) n -> p k n", p=P)).then_inc(w_landed, 16)
            sp.dma_start(wsd[:, :, :], ws_down.rearrange("(k p) n -> p k n", p=FP)).then_inc(w_landed, 16)

            def load_x(pair, images=2 * GI):
                sp.wait_ge(x_sorted, pair)
                sp.dma_start(*x_pair(pair, images)).then_inc(x_landed, 16)

            def load_experts(pair, u, slot):
                ring = ew[:, bass.ds(slot, 2), :]
                for w, at, parts, wide in ((w_gate, 0, P, KD * F), (w_up, KD * F, P, KD * F),
                                           (w_down, 2 * KD * F, FP, FC * D)):
                    sp.dma_start(ring[0:parts, :, at:at + wide],
                                 w.rearrange("e (p k) f -> p e (k f)", p=parts)[:, bass.ds(2 * pair, 2), :]
                                 ).then_inc(ew_landed[u], 16)

            def store_res(g):
                sp.wait_ge(res_ready, g.q + 1)
                sp.dma_start(acc[0][bass.ds(g.q * R, g.rows), :], res[g.u][0:g.rows, :]).then_inc(res_stored[g.u], 16)

            load_experts(0, 0, 0)
            load_x(1)
            load_experts(1, 1, 2)
            store_res(Group(0, 0))
            with sp.Fori(1, 4) as j:
                for u in range(2):
                    pair = 2 * j + u
                    load_x(pair)
                    sp.wait_ge(ew_landed[u], 48 * j)
                    load_experts(pair, u, 2 * pair)
                    store_res(Group(pair, -3))
                    store_res(Group(pair, -2))
            for pair in range(RING // 2, PAIRS):
                load_x(pair, min(2 * GI, IMAGES - 2 * GI * pair))
                store_res(Group(0, 2 * pair - 3))
                store_res(Group(0, 2 * pair - 2))
            for q in range(2 * PAIRS - 3, GROUPS):
                store_res(Group(0, q))
            sp.wait_ge(slots_cleared, 48)
            for u in range(2):
                sp.wait_ge(scattered[u], 16 * TOPK * PAIRS)

            def load_row(e, c):
                sp.dma_start(xrow[c][:, :], slots[bass.ds(e * CAP, CAP), :]).then_inc(row_landed[c], 16)

            for e in range(3):
                load_row(e, e)
            load_row(3, 3)

            def more_experts(m, n):
                sp.wait_ge(e_down_done, 4 * m + 2 * n + 2)
                sp.wait_ge(ew_landed[n], 48 * (m + RING // 4))
                load_experts(2 * m + n + RING // 2, n, (4 * m + 2 * n) % RING)

            def next_rows(m, cs):
                for c in cs:
                    sp.wait_ge(added[c % 2], 16 * (2 * m + c // 2 + 1))
                    load_row(4 * m + 4 + c, c)

            with sp.Fori(0, (E - RING) // 4) as m:
                for n in range(2):
                    next_rows(m, (2 * n, 2 * n + 1))
                    more_experts(m, n)
            with sp.Fori((E - RING) // 4, E // 4 - 1) as m:
                next_rows(m, range(4))
            for u in range(2):
                sp.wait_ge(added[u], 16 * E // 2)
                sp.wait_ge(res_stored[u], 16 * PAIRS)
            for n, (parts, at, rows) in enumerate(OUT_PARTS):
                for k in range(2):
                    sp.dma_start(out_tile(k, n), out_rows(acc[k], n)).then_inc(sums_landed[n], 16)
            for n in range(len(OUT_PARTS)):
                sp.wait_ge(out_ready, n + 1)
                sp.dma_start(out_rows(out.rearrange("n s d -> (n s) d"), n), out_tile(0, n)).then_inc(out_stored, 16)
            sp.wait_ge(out_stored, 16 * len(OUT_PARTS))

        @block.gpsimd
        def _(pool):
            made = [0]

            def step(ins):
                made[0] += 1
                ins.then_inc(consts_made, 1)

            def done():
                pool.wait_ge(consts_made, made[0])

            step(pool.memset(ident[:, :], 0.0))
            step(pool.memset(ones[:, :], 1.0))
            step(pool.memset(before[:, :], 1.0))
            step(pool.memset(headmask[:, :], 1.0))
            step(pool.memset(third[:, :, :], 1.0))
            step(pool.memset(tri[:, :, :], 0.0))
            step(pool.memset(halfneg[:, :], -0.5))
            step(pool.memset(empty[:, :], 0.0))
            step(pool.iota(base[:, :], [[-CAP, E]], base=SLOTS, channel_multiplier=0,
                           allow_small_or_imprecise_dtypes=True))
            for u in range(2):
                step(pool.iota(xs[u][:, ROW - 1:ROW].bitcast(I32), [[0, 1]], base=R * u - 2 * R, channel_multiplier=1))
            done()
            step(pool.affine_select(out=ident[:, :], in_=ident[:, :], compare_op=ALU.not_equal, fill=1.0, base=0,
                                    pattern=[[-1, P]], channel_multiplier=1))
            step(pool.affine_select(out=before[:, :], in_=before[:, :], compare_op=ALU.is_gt, fill=0.0, base=0,
                                    pattern=[[1, R]], channel_multiplier=-1))
            step(pool.affine_select(out=headmask[:, :], in_=headmask[:, :], compare_op=ALU.is_ge, fill=0.0, base=0,
                                    pattern=[[-HD, HC]], channel_multiplier=1))
            step(pool.affine_select(out=third[:, :, :], in_=third[:, :, :], compare_op=ALU.is_ge, fill=0.0, base=0,
                                    pattern=[[0, PC], [-S, PH]], channel_multiplier=1))
            step(pool.affine_select(out=tri[:, :, :], in_=tri[:, :, :], compare_op=ALU.is_ge, fill=NEG, base=0,
                                    pattern=[[-S, GI], [-1, S]], channel_multiplier=1))
            step(pool.iota(empty[:, ROW - 1:ROW].bitcast(I32), [[0, 1]], base=T, channel_multiplier=1))
            done()
            step(pool.affine_select(out=headmask[:, :], in_=headmask[:, :], compare_op=ALU.is_ge, fill=0.0,
                                    base=HD - 1, pattern=[[HD, HC]], channel_multiplier=-1))
            step(pool.affine_select(out=third[:, :, :], in_=third[:, :, :], compare_op=ALU.is_ge, fill=0.0,
                                    base=S - 1, pattern=[[0, PC], [S, PH]], channel_multiplier=-1))
            assert made[0] == CONSTS

            def rstd(g, ve, rs, var_ready, ready):
                pool.wait_ge(var_ready, g.q + 1)
                pool.tensor_tensor(rs[0:g.rows, :], ve[0:g.rows, :], halfneg[0:g.rows, :], ALU.pow).then_inc(ready, 1)

            def add_bo(g):
                pool.wait_ge(h_ready, g.q + 1)
                if not (isinstance(g.q, int) and g.q < 2):
                    pool.wait_ge(h2_ready, g.q - 1)
                pool.tensor_tensor(hb[g.u][0:g.rows, :], h[g.u][0:g.rows, :], bo_sb[0:g.rows, :],
                                   ALU.add).then_inc(hb_ready, 1)

            def constant_wait():
                pool.wait_ge(consts_made, CONSTS)

            def scatter(g):
                constant_wait()
                pool.wait_ge(row_ready, g.q + 1)
                pool.wait_ge(idx_ready, g.q + 1)
                for k in range(TOPK):
                    pool.indirect_dma_start(
                        slots, bass.IndirectOffsetOnAxis(ap=idx[g.u][0:g.rows, k:k + 1], axis=0),
                        xs[g.u][0:g.rows, :], None, bounds_check=SLOTS - 1, oob_is_err=False,
                    ).then_inc(scattered[g.u], 16)

            def turn(b, c):
                here = 2 * b + c
                known = isinstance(here, int)
                if not known or 0 <= here - 1 < GROUPS:
                    rstd(Group(b, c - 1), ve2, rs2, ln2_var, ln2_rstd)
                if not known or here + 1 < GROUPS:
                    g = Group(b, c + 1)
                    rstd(g, ve1, rs1, ln1_var, ln1_rstd)
                    add_bo(g)
                if not known or 0 <= here - 2 < GROUPS:
                    if known and here == 2:
                        pool.wait_ge(slots_cleared, 48)
                    scatter(Group(b, c - 2))

            pool.wait_ge(small_landed, SMALL)
            for i in range(-1, 3):
                turn(0, i)
            with pool.Fori(1, PAIRS - 2) as b:
                turn(b, 1)
                turn(b, 2)
            for i in range(GROUPS - 3, GROUPS + 2):
                turn(0, i)

            def add(e, u, c):
                pool.wait_ge(ysc_ready, e + 1)
                if not isinstance(e, int) or e >= 2:
                    pool.wait_ge(added[u], 8 * (e - u))
                if not isinstance(e, int) or e >= 1:
                    pool.wait_ge(waits_carried, e)
                pool.tensor_tensor(spare[:, :], halfneg[:, :], halfneg[:, :], ALU.add).then_inc(waits_carried, 1)
                pool.indirect_dma_start(
                    acc[u], bass.IndirectOffsetOnAxis(ap=xrow[c][:, ROW - 1:ROW].bitcast(U32), axis=0),
                    ysc[u][:, :], None, compute_op=ALU.add,
                ).then_inc(added[u], 16)

            for u in range(2):
                pool.wait_ge(res_stored[u], 16 * PAIRS)
            for c in range(4):
                add(c, c % 2, c)
            with pool.Fori(1, E // 4) as m:
                for c in range(4):
                    add(4 * m + c, c % 2, c)

        @block.scalar
        def _(act):
            act.wait_ge(consts_made, CONSTS)
            act.wait_ge(x_landed, 16)
            act.dma_start(slots.rearrange("(e p) c -> p e c", p=P),
                          empty[:, :].unsqueeze(1).broadcast_to([P, E, ROW])).then_inc(slots_cleared, 16)
            act.dma_start(acc[1].rearrange("(a p) c -> p a c", p=FP),
                          empty[0:FP, 0:D].unsqueeze(1).broadcast_to([FP, (T + P) // FP, D])).then_inc(slots_cleared, 16)
            act.dma_start(acc[0][T:T + P, :], empty[:, 0:D]).then_inc(slots_cleared, 16)
            for n in range(4):
                act.wait_ge(wT_turned, n + 1)
                if n < 3:
                    nc.scalar.activation(wT[:, 2 * n:2 * n + 2, :].rearrange("p a b -> p (a b)"),
                                         ps[:, n, 0:2 * D], ACT.Copy).then_inc(wT_copied, 1)
                else:
                    nc.scalar.activation(rT[:, :, :].rearrange("p a b -> p (a b)"), ps[:, n, 0:KD * E],
                                         ACT.Copy).then_inc(wT_copied, 1)

            def sort_x(pair, images):
                rows = images * CH * PS
                act.wait_ge(x_landed, 16 * (pair + 1))
                if not (isinstance(pair, int) and pair == 0):
                    act.wait_ge(patches_turned, 4 * pair)
                nc.scalar.activation(xw[0:rows, :, :].rearrange("p w (i j) -> p w i j", i=PATCH),
                                     xraw[0:rows, :].rearrange("p (i w j) -> p w i j", i=PATCH, w=PS),
                                     ACT.Copy).then_inc(x_sorted, 1)

            def copy_patches(pair, n, images):
                half, w3 = n // 2, n % 2
                act.wait_ge(patches_turned, 4 * pair + n + 1)
                if not (isinstance(pair, int) and pair == 0):
                    act.wait_ge(embedded, 2 * pair)
                rows = images * CH * PS
                src = ps[:, 7, 0:3 * rows].rearrange("p (w b c r) -> p b c r w", w=3, b=images, c=CH)
                for c in range(CH):
                    dst = pT[:, c * HALF + half, :].rearrange("p (b s) -> p b s", s=S)[:, 0:images, 1:S].rearrange(
                        "p b (r w) -> p b r w", r=PS)
                    ins = nc.scalar.activation(dst[:, :, :, 3 * w3:3 * w3 + 3], src[:, :, c, :, :], ACT.Copy)
                ins.then_inc(patches_copied, 1)

            def copy_xnT(g):
                act.wait_ge(xn_turned, g.q + 1)
                if not (isinstance(g.q, int) and g.q == 0):
                    act.wait_ge(v_done, g.q)
                for k in range(KD):
                    src = ps[:, 1, k * R:k * R + g.rows].rearrange("p (i s) -> p i s", s=S)
                    ins = nc.scalar.activation(xnT[:, k, 0:g.images, :, :],
                                               src.unsqueeze(2).broadcast_to([P, g.images, PH, S]), ACT.Copy)
                ins.then_inc(xnT_ready, 1)

            def copy_q(g):
                act.wait_ge(qk_done, g.q + 1)
                if not (isinstance(g.q, int) and g.q == 0):
                    act.wait_ge(scores_done, g.q)
                qk = ps[:, 0, 0:4 * R].rearrange("p (k r) -> p k r", k=4)
                for c in range(KD):
                    zero_diag = qz[:, c, :, :].rearrange("p i r -> p (i r)")
                    dst = bass.AP(tensor=zero_diag.tensor, offset=zero_diag.offset,
                                  ap=[zero_diag.ap[0], [R + S, g.images], [1, S]])
                    ins = nc.scalar.activation(dst, qk[:, c, 0:g.rows].rearrange("p (i s) -> p i s", i=g.images), ACT.Copy)
                ins.then_inc(q_ready, 1)
                for hd in range(HC):
                    ins = nc.scalar.activation(kz[:, :, hd, 0:g.rows], qk[:, KD:2 * KD, 0:g.rows], ACT.Copy,
                                               scale=headmask[:, hd:hd + 1])
                ins.then_inc(k_ready, 1)

            def copy_cxT(g):
                act.wait_ge(cx_turned, g.q + 1)
                if not (isinstance(g.q, int) and g.q == 0):
                    act.wait_ge(wo_done, g.q)
                nc.scalar.activation(cxT[:, :, 0:g.rows], ps[:, 1, 0:KD * R].rearrange("p (k r) -> p k r", k=KD)[:, :, 0:g.rows],
                                     ACT.Copy).then_inc(cxT_ready, 1)

            def copy_xn2T(g):
                act.wait_ge(xn2_turned, g.q + 1)
                if not (isinstance(g.q, int) and g.q == 0):
                    act.wait_ge(gu_done, g.q)
                nc.scalar.activation(xn2T[:, :, 0:g.rows], ps[:, 1, 0:KD * R].rearrange("p (k r) -> p k r", k=KD)[:, :, 0:g.rows],
                                     ACT.Copy).then_inc(xn2T_ready, 1)

            def exp_probs(g):
                act.wait_ge(lowered, g.q + 1)
                if not (isinstance(g.q, int) and g.q == 0):
                    act.wait_ge(prob_turned, g.q)
                nc.scalar.activation(prob[0:g.rows, :], sx[0:g.rows, :, :].rearrange("p h s -> p (h s)"), ACT.Exp,
                                     scale=float(HD) ** -0.5).then_inc(prob_ready, 1)

            def copy_probT(g):
                act.wait_ge(prob_turned, g.q + 1)
                if not (isinstance(g.q, int) and g.q == 0):
                    act.wait_ge(pv_done, g.q)
                a = ps[:, 2, 0:3 * R].rearrange("p (k r) -> p k r", k=3)
                z = ps[:, 3, 0:3 * R].rearrange("p (k r) -> p k r", k=3)
                nc.scalar.activation(probT[0:R, 0:3, 0:g.rows], a[0:R, :, 0:g.rows], ACT.Copy)
                nc.scalar.activation(probT[0:R, 3:5, 0:g.rows], z[0:R, 0:2, 0:g.rows], ACT.Copy)
                nc.scalar.activation(probT[0:S, 5, 0:g.rows], z[0:S, 2, 0:g.rows], ACT.Copy).then_inc(probT_ready, 1)

            def route_exp(g):
                act.wait_ge(shifted_ready, g.q + 1)
                if not (isinstance(g.q, int) and g.q == 0):
                    act.wait_ge(em_ready, g.q)
                nc.scalar.activation(ex[0:g.rows, :], shifted[0:g.rows, :], ACT.Exp).then_inc(ex_ready, 1)

            def shared_tanh(g):
                act.wait_ge(gu_done, g.q + 1)
                if not (isinstance(g.q, int) and g.q == 0):
                    act.wait_ge(g1_ready, g.q)
                nc.scalar.activation(th[:, :, 0:g.rows], ps[0:FP, 0, 0:2 * R].rearrange("p (k r) -> p k r", k=2)[:, :, 0:g.rows],
                                     ACT.Tanh, scale=0.5).then_inc(tanh_ready, 1)

            def turn(b, c):
                here = 2 * b + c
                known = isinstance(here, int)
                front = not known or here + 1 < GROUPS
                mid = not known or 0 <= here < GROUPS
                back = not known or 0 <= here - 1 < GROUPS
                pair = b + (c + 1) // 2
                images = 2 * GI
                if isinstance(pair, int):
                    images = min(images, IMAGES - 2 * GI * pair)
                turning = c % 2 == 1 and images > 0 and front
                if turning:
                    copy_patches(pair, 0, images)
                if mid:
                    copy_q(Group(b, c))
                if back:
                    copy_cxT(Group(b, c - 1))
                if turning:
                    for n in range(1, 4):
                        copy_patches(pair, n, images)
                if back:
                    copy_xn2T(Group(b, c - 1))
                if mid:
                    exp_probs(Group(b, c))
                if back:
                    shared_tanh(Group(b, c - 1))
                    route_exp(Group(b, c - 1))
                if mid:
                    copy_probT(Group(b, c))
                if front:
                    copy_xnT(Group(b, c + 1))
                if c % 2 == 0 and (not known or 2 * pair + 2 < GROUPS):
                    sort_x(pair + 1, 2 * GI if not known else min(2 * GI, IMAGES - 2 * GI * (pair + 1)))

            act.wait_ge(masks_made, 4)
            sort_x(0, 2 * GI)
            for i in range(-1, 3):
                turn(0, i)
            with act.Fori(1, PAIRS - 2) as b:
                turn(b, 1)
                turn(b, 2)
            for i in range(GROUPS - 3, GROUPS + 1):
                turn(0, i)

            def copy_xT(e, u):
                act.wait_ge(row_turned, e + 1)
                if not isinstance(e, int) or e >= 2:
                    act.wait_ge(e_gu_done, e - 1)
                nc.scalar.activation(xT[u][:, :, :].rearrange("p k r -> p (k r)"), ps[:, 2 + u, 0:KD * P],
                                     ACT.Copy).then_inc(xT_ready, 1)

            def silu(e, u):
                act.wait_ge(e_gu_done, e + 1)
                if not isinstance(e, int) or e >= 2:
                    act.wait_ge(hh_ready, e - 1)
                nc.scalar.activation(sg[u][:, :], ps[:, u, 0:F], ACT.Silu).then_inc(silu_ready, 1)

            def copy_hT(e, u):
                act.wait_ge(hh_turned, e + 1)
                if not isinstance(e, int) or e >= 2:
                    act.wait_ge(e_down_done, e - 1)
                nc.scalar.activation(hT[u][:, :, :].rearrange("p k r -> p (k r)"), ps[0:FP, 4 + u, 0:FC * P],
                                     ACT.Copy).then_inc(hT_ready, 1)

            def expert(e, u, more=True):
                silu(e, u)
                if more:
                    copy_xT(e + 1, 1 - u)
                copy_hT(e, u)

            copy_xT(0, 0)
            expert(0, 0)
            expert(1, 1)
            with act.Fori(1, E // 2 - 1) as m:
                expert(2 * m, 0)
                expert(2 * m + 1, 1)
            expert(E - 2, 0)
            expert(E - 1, 1, more=False)

        @block.tensor
        def _(pe):
            pe.wait_ge(consts_made, CONSTS)
            pe.wait_ge(w_landed, WEIGHTS)
            pe.wait_ge(small_landed, SMALL)
            for n in range(3):
                for dd in range(2):
                    for k in range(KD):
                        ins = nc.tensor.transpose(ps[:, n, dd * D + k * P:dd * D + (k + 1) * P],
                                                  wraw[:, k, (2 * n + dd) * P:(2 * n + dd + 1) * P], ident[:, :])
                ins.then_inc(wT_turned, 1)
            for k in range(KD):
                ins = nc.tensor.transpose(ps[:, 3, k * E:(k + 1) * E], rraw[:, k * P:(k + 1) * P], ident[0:E, 0:E])
            ins.then_inc(wT_turned, 1)
            pe.wait_ge(wT_copied, 4)

            def turn_patches(pair, n, images):
                half, w3 = n // 2, n % 2
                rows = images * CH * PS
                if n == 0:
                    pe.wait_ge(x_sorted, pair + 1)
                    if not (isinstance(pair, int) and pair < 1):
                        pe.wait_ge(res_ready, 2 * pair - 2)
                else:
                    pe.wait_ge(patches_copied, 4 * pair + n)
                for w in range(3):
                    ins = nc.tensor.transpose(ps[:, 7, w * rows:(w + 1) * rows],
                                              xw[0:rows, 3 * w3 + w, half * P:(half + 1) * P], ident[0:rows, 0:rows])
                ins.then_inc(patches_turned, 1)

            def embed(g):
                pe.wait_ge(patches_copied, 4 * g.pair + 4)
                if g.u == 1:
                    if not (isinstance(g.q, int) and g.q < 2):
                        pe.wait_ge(res_ready, g.q - 2)
                    else:
                        pe.wait_ge(h_ready, 1)
                for c in range(CH):
                    for half in range(HALF):
                        ins = nc.tensor.matmul(ps[0:g.rows, 7, 0:D],
                                               pT[:, c * HALF + half, g.u * R:g.u * R + g.rows], wT[:, c * HALF + half, :],
                                               start=(c + half == 0), stop=(c == CH - 1 and half == HALF - 1))
                ins.then_inc(embedded, 1)

            def turn_two(g, src, done):
                for k in range(KD):
                    ins = nc.tensor.transpose(ps[:, 1, k * R:k * R + g.rows], src[0:g.rows, k * P:(k + 1) * P],
                                              ident[0:g.rows, 0:g.rows])
                ins.then_inc(done, 1)

            def turn_xn(g):
                pe.wait_ge(xn_ready, g.q + 1)
                if not (isinstance(g.q, int) and g.q < 2):
                    pe.wait_ge(xn2T_ready, g.q - 1)
                elif g.q == 1:
                    pe.wait_ge(xnT_ready, 1)
                turn_two(g, xn, xn_turned)

            def project_qk(g):
                pe.wait_ge(xnT_ready, g.q + 1)
                if not (isinstance(g.q, int) and g.q < 2):
                    pe.wait_ge(hs_ready, g.q - 1)
                elif g.q == 1:
                    pe.wait_ge(k_ready, 1)
                for c in range(2 * KD):
                    for k in range(KD):
                        ins = nc.tensor.matmul(ps[:, 0, c * R:c * R + g.rows], wqk[:, k, c * P:(c + 1) * P],
                                               xnT[:, k, 0:g.images, 0, :], start=(k == 0), stop=(k == KD - 1))
                ins.then_inc(qk_done, 1)

            def project_v(g):
                if not (isinstance(g.q, int) and g.q == 0):
                    pe.wait_ge(probT_ready, g.q)
                for i in range(g.images):
                    for k in range(KD):
                        ins = nc.tensor.matmul(ps[0:R, 2 + i // 2, (i % 2) * D:(i % 2 + 1) * D],
                                               xnT[:, k, i, :, :].rearrange("p a s -> p (a s)"), wv[:, k, :],
                                               start=(k == 0), stop=(k == KD - 1))
                ins.then_inc(v_done, 1)

            def scores(g, c):
                if c == 0:
                    pe.wait_ge(q_ready, g.q + 1)
                    pe.wait_ge(k_ready, g.q + 1)
                    if not (isinstance(g.q, int) and g.q == 0):
                        pe.wait_ge(sum_ready, g.q)
                for i in range(g.images):
                    ins = nc.tensor.matmul(ps[0:g.rows, 5 + c, 0:HC * S], qz[:, c, i, 0:g.rows],
                                           kz[:, c, :, S * i:S * i + S], start=(i == 0), stop=(i == g.images - 1))
                if c == 1:
                    ins.then_inc(scores_done, 1)

            def turn_probs(g):
                pe.wait_ge(prob_ready, g.q + 1)
                pe.wait_ge(v_ready, g.q + 1)
                for c in range(PC):
                    cols = min(PH * S, H * S - c * PH * S)
                    ins = nc.tensor.transpose(ps[0:cols, 2 + c // 3, (c % 3) * R:(c % 3) * R + g.rows],
                                              prob[0:g.rows, c * PH * S:c * PH * S + cols], ident[0:g.rows, 0:g.rows])
                ins.then_inc(prob_turned, 1)

            def context(g):
                pe.wait_ge(probT_ready, g.q + 1)
                pe.wait_ge(masked, g.q + 1)
                for c in range(PC):
                    rows = min(PH * S, H * S - c * PH * S)
                    wide = PH * VW
                    ins = nc.tensor.matmul(
                        ps[0:g.rows, 5 + c // 3, 0:GI * 3 * wide].rearrange("p (i c w) -> p i c w", i=GI, c=3)[
                            :, 0:g.images, c % 3, :],
                        probT[0:rows, c, 0:g.rows],
                        vz[0:rows, 0:g.images, c * PH:(c + 1) * PH, :].rearrange("p i h d -> p i (h d)"),
                        start=True, stop=True)
                ins.then_inc(pv_done, 1)

            def turn_cx(g):
                pe.wait_ge(cx_ready, g.q + 1)
                if isinstance(g.q, int) and g.q == GROUPS - 1:
                    pe.wait_ge(xnT_ready, GROUPS)
                else:
                    pe.wait_ge(xnT_ready, g.q + 2)
                turn_two(g, cx[:, :, :].rearrange("p h d -> p (h d)"), cx_turned)

            def project_o(g):
                pe.wait_ge(cxT_ready, g.q + 1)
                if not (isinstance(g.q, int) and g.q == 0):
                    pe.wait_ge(room_ready, g.q)
                for k in range(KD):
                    ins = nc.tensor.matmul(ps[0:g.rows, 4, 0:D], cxT[:, k, 0:g.rows], wo[:, k, :],
                                           start=(k == 0), stop=(k == KD - 1))
                ins.then_inc(wo_done, 1)

            def turn_xn2(g):
                pe.wait_ge(xn2_ready, g.q + 1)
                pe.wait_ge(cxT_ready, g.q + 1)
                turn_two(g, xs[g.u], xn2_turned)

            def route(g):
                pe.wait_ge(xn2T_ready, g.q + 1)
                pe.wait_ge(h2_ready, g.q + 1)
                for k in range(KD):
                    ins = nc.tensor.matmul(ps[0:g.rows, 4, 0:E], xn2T[:, k, 0:g.rows], rT[:, k, :],
                                           start=(k == 0), stop=(k == KD - 1))
                ins.then_inc(router_done, 1)

            def shared_up(g):
                if isinstance(g.q, int) and g.q == GROUPS - 1:
                    pe.wait_ge(k_ready, GROUPS)
                else:
                    pe.wait_ge(k_ready, g.q + 2)
                    pe.wait_ge(q_ready, g.q + 2)
                for j in range(2 * FC):
                    for k in range(KD):
                        ins = nc.tensor.matmul(ps[0:FP, 0, j * R:j * R + g.rows], wsgu[:, k, j * FP:(j + 1) * FP],
                                               xn2T[:, k, 0:g.rows], start=(k == 0), stop=(k == KD - 1))
                ins.then_inc(gu_done, 1)

            def shared_down(g):
                pe.wait_ge(hs_ready, g.q + 1)
                pe.wait_ge(h_ready, min(g.q + 3, GROUPS) if isinstance(g.q, int) else g.q + 3)
                for j in range(FC):
                    ins = nc.tensor.matmul(ps[0:g.rows, 7, 0:D], hs[:, j, 0:g.rows], wsd[:, j, :],
                                           start=(j == 0), stop=(j == FC - 1))
                ins.then_inc(down_done, 1)

            def places(g):
                pe.wait_ge(chosen_ready, g.q + 1)
                pe.wait_ge(earlier_ready, g.q + 1)
                pe.wait_ge(logits_ready, g.q + 1)
                nc.tensor.matmul(ps[0:g.rows, 4, 0:E], before[0:g.rows, 0:g.rows], chosen[g.u][0:g.rows, :],
                                 start=True, stop=False)
                nc.tensor.matmul(ps[0:g.rows, 4, 0:E], ones[0:R, 0:g.rows], earlier[g.u][0:R, :],
                                 start=False, stop=True).then_inc(places_done, 1)

            def turn(b, c):
                here = 2 * b + c
                known = isinstance(here, int)
                front = not known or here + 1 < GROUPS
                mid = not known or 0 <= here < GROUPS
                back = not known or 0 <= here - 1 < GROUPS
                pair = b + (c + 1) // 2
                images = 2 * GI
                if isinstance(pair, int):
                    images = min(images, IMAGES - 2 * GI * pair)
                turning = c % 2 == 1 and images > 0 and front
                if turning:
                    turn_patches(pair, 0, images)
                if mid:
                    project_qk(Group(b, c))
                if back:
                    turn_cx(Group(b, c - 1))
                if turning:
                    turn_patches(pair, 1, images)
                if mid:
                    project_v(Group(b, c))
                if turning:
                    turn_patches(pair, 2, images)
                if back:
                    project_o(Group(b, c - 1))
                if mid:
                    scores(Group(b, c), 0)
                if turning:
                    turn_patches(pair, 3, images)
                if mid:
                    scores(Group(b, c), 1)
                if back:
                    turn_xn2(Group(b, c - 1))
                if front:
                    embed(Group(b, c + 1))
                if back:
                    route(Group(b, c - 1))
                    shared_up(Group(b, c - 1))
                if mid:
                    turn_probs(Group(b, c))
                if front:
                    turn_xn(Group(b, c + 1))
                if back:
                    shared_down(Group(b, c - 1))
                    places(Group(b, c - 1))
                if mid:
                    context(Group(b, c))

            for i in range(-1, 3):
                turn(0, i)
            with pe.Fori(1, PAIRS - 2) as b:
                turn(b, 1)
                turn(b, 2)
            for i in range(GROUPS - 3, GROUPS + 1):
                turn(0, i)

            pe.wait_ge(res_ready, GROUPS)
            pe.wait_ge(room_ready, GROUPS)

            def turn_rows(e, c, lap):
                pe.wait_ge(row_landed[c], 16 * (lap + 1))
                if not isinstance(e, int) or e >= 2:
                    pe.wait_ge(xT_ready, e - 1)
                for k in range(KD):
                    ins = nc.tensor.transpose(ps[:, 2 + c % 2, k * P:(k + 1) * P], xrow[c][:, k:D:KD], ident[:, :])
                ins.then_inc(row_turned, 1)

            def gate_up(e, c, lap, slot):
                u = c % 2
                pe.wait_ge(xT_ready, e + 1)
                pe.wait_ge(ew_landed[c // 2], 48 * (lap + 1))
                if not isinstance(e, int) or e >= 2:
                    pe.wait_ge(hh_ready, e - 1)
                w = ew[:, slot, 0:2 * KD * F].rearrange("p (m k f) -> p m k f", m=2, k=KD)
                for k in range(KD):
                    ins = nc.tensor.matmul(ps[:, u, 0:2 * F], xT[u][:, k, :], w[:, :, k, :],
                                           start=(k == 0), stop=(k == KD - 1))
                ins.then_inc(e_gu_done, 1)

            def turn_hidden(e, u):
                pe.wait_ge(hh_ready, e + 1)
                if not isinstance(e, int) or e >= 2:
                    pe.wait_ge(hT_ready, e - 1)
                for k in range(FC):
                    ins = nc.tensor.transpose(ps[0:FP, 4 + u, k * P:(k + 1) * P], hh[u][:, k:F:FC], ident[:, :])
                ins.then_inc(hh_turned, 1)

            def down(e, u, slot):
                pe.wait_ge(hT_ready, e + 1)
                if not isinstance(e, int) or e >= 2:
                    pe.wait_ge(ysc_ready, e - 1)
                for k in range(FC):
                    ins = nc.tensor.matmul(ps[:, 6 + u, 0:D], hT[u][:, k, :],
                                           ew[0:FP, slot, 2 * KD * F + k * D:2 * KD * F + (k + 1) * D],
                                           start=(k == 0), stop=(k == FC - 1))
                ins.then_inc(e_down_done, 1)

            def experts(m, first=False, last=False):
                for c in range(4):
                    e = 4 * m + c
                    gate_up(e, c, m, e % RING)
                    if not (last and c == 3):
                        turn_rows(e + 1, (c + 1) % 4, m + (c + 1) // 4)
                    if not (first and c == 0):
                        down(e - 1, (c - 1) % 2, (e - 1) % RING)
                    turn_hidden(e, c % 2)

            turn_rows(0, 0, 0)
            experts(0, first=True)
            with pe.Fori(1, E // 4 - 1) as m:
                experts(m)
            experts(E // 4 - 1, last=True)
            down(E - 1, 1, (E - 1) % RING)

        @block.vector
        def _(dve):
            V = nc.vector
            V.memset(qz[:, :, :, :], 0.0).then_inc(zeros_made, 1)
            V.memset(vz[:, :, :, :], 0.0).then_inc(zeros_made, 1)
            V.memset(pT[:, :, :], 0.0).then_inc(zeros_made, 1)
            V.memset(earlier[0][:, :], 0.0).then_inc(earlier_ready, 1)
            dve.wait_ge(consts_made, CONSTS)
            dve.wait_ge(zeros_made, 3)
            for i in range(GI):
                V.tensor_copy(vz[:, i, :, HD], third[0:R, :, :].rearrange("p c r -> p (c r)")).then_inc(masks_made, 1)
            V.tensor_scalar(causal[:, :], tri[:, 0, :], third[:, 0, 0:1], None, ALU.mult).then_inc(dve_const, 1)
            for i in range(1, GI):
                dve.wait_ge(dve_const, i)
                V.scalar_tensor_tensor(out=causal[:, :], in0=tri[:, i, :], scalar=third[:, 0, i:i + 1],
                                       in1=causal[:, :], op0=ALU.mult, op1=ALU.add).then_inc(dve_const, 1)
            dve.wait_ge(small_landed, SMALL)
            dve.wait_ge(w_landed, WEIGHTS)
            V.tensor_tensor(posb[0:R, :], posb[0:R, :], posadd[0:R, :], ALU.add).then_inc(masks_made, 1)
            dve.wait_ge(masks_made, 4)
            dve.wait_ge(dve_const, GI)

            def at(g, t):
                return t[0:g.rows]

            def constant_wait():
                dve.wait_ge(consts_made, CONSTS)

            def norm(g, src, st, mv, ve, stats, mean, var):
                V.bn_stats(st[0:g.rows, :], src).then_inc(stats, 1)
                constant_wait()
                dve.wait_ge(stats, g.q + 1)
                V.bn_aggr(mv[0:g.rows, :], st[0:g.rows, :]).then_inc(mean, 1)
                dve.wait_ge(mean, g.q + 1)
                V.tensor_scalar(ve[0:g.rows, :], mv[0:g.rows, 1:2], EPS, None, ALU.add).then_inc(var, 1)

            def tokens(g):
                r = g.rows
                dve.wait_ge(embedded, g.q + 1)
                if not (isinstance(g.q, int) and g.q < 2):
                    dve.wait_ge(hb_ready, g.q - 1)
                V.tensor_tensor(h[g.u][0:r, :], ps[0:r, 7, 0:D], posb[0:r, :], ALU.add).then_inc(h_ready, 1)
                dve.wait_ge(h_ready, g.q + 1)
                norm(g, h[g.u][0:r, :], st1, mv1, ve1, ln1_stats, ln1_mean, ln1_var)

            def normed(g):
                r = g.rows
                dve.wait_ge(ln1_rstd, g.q + 1)
                if not (isinstance(g.q, int) and g.q == 0):
                    dve.wait_ge(xn_turned, g.q)
                V.tensor_scalar(xn[0:r, :], h[g.u][0:r, :], mv1[0:r, 0:1], rs1[0:r, 0:1], ALU.subtract,
                                ALU.mult).then_inc(xn_ready, 1)

            def copy_v(g):
                n = g.images
                dve.wait_ge(v_done, g.q + 1)
                if not (isinstance(g.q, int) and g.q == 0):
                    dve.wait_ge(pv_done, g.q)
                src = ps[0:R, 2:4, :].rearrange("p a b -> p (a b)")[:, 0:n * D].rearrange("p (i h d) -> p i h d", i=n, h=H)
                for i in range(n):
                    ins = V.tensor_tensor(vz[:, i, 0:H, 0:HD], src[:, i],
                                          third[0:R, :, :].rearrange("p c r -> p (c r)")[:, 0:H].unsqueeze(2).broadcast_to([R, H, HD]),
                                          ALU.mult)
                ins.then_inc(v_ready, 1)

            def softmax(g):
                r = g.rows
                dve.wait_ge(scores_done, g.q + 1)
                for c in range(KD):
                    ins = V.tensor_tensor(sm[0:r, c * HC:(c + 1) * HC, :],
                                          ps[0:r, 5 + c, 0:HC * S].rearrange("p (h s) -> p h s", h=HC),
                                          causal[0:r, :].unsqueeze(1).broadcast_to([r, HC, S]), ALU.add)
                ins.then_inc(masked, 1)
                dve.wait_ge(masked, g.q + 1)
                V.tensor_reduce(mx[0:r, :], sm[0:r, :, :], AX, ALU.max).then_inc(max_ready, 1)
                dve.wait_ge(max_ready, g.q + 1)
                if not (isinstance(g.q, int) and g.q == 0):
                    dve.wait_ge(prob_ready, g.q)
                V.tensor_tensor(sx[0:r, :, :], sm[0:r, :, :], mx[0:r, :].unsqueeze(2).broadcast_to([r, H, S]),
                                ALU.subtract).then_inc(lowered, 1)

            def gather_context(g):
                r = g.rows
                dve.wait_ge(pv_done, g.q + 1)
                wide = PH * VW
                o = ps[0:r, 5:7, 0:3 * GI * wide].rearrange("p a (i w) -> p a i w", i=GI)
                s4 = ctxsum[0:r, :, :].rearrange("p (a w) d -> p a (w d)", a=2)
                V.tensor_scalar(s4, o[:, :, 0, :], third[0:r, 0, 0:1], None, ALU.mult).then_inc(sum_a, 1)
                for i in range(1, g.images):
                    dve.wait_ge((sum_a, sum_b)[i - 1], g.q + 1)
                    V.scalar_tensor_tensor(out=s4, in0=o[:, :, i, :], scalar=third[0:r, 0, i:i + 1], in1=s4,
                                           op0=ALU.mult, op1=ALU.add).then_inc((sum_b, sum_ready)[i - 1], 1)
                if g.images == 1:
                    dve.wait_ge(sum_a, g.q + 1)
                    V.tensor_copy(rden[0:r, 0:1], ctxsum[0:r, 0:1, 0]).then_inc(sum_ready, 1)
                dve.wait_ge(sum_ready, g.q + 1)
                V.reciprocal(rden[0:r, :], ctxsum[0:r, 0:H, HD]).then_inc(rden_ready, 1)
                dve.wait_ge(rden_ready, g.q + 1)
                if not (isinstance(g.q, int) and g.q == 0):
                    dve.wait_ge(cx_turned, g.q)
                V.tensor_tensor(cx[0:r, :, :], ctxsum[0:r, 0:H, 0:HD], rden[0:r, :].unsqueeze(2).broadcast_to([r, H, HD]),
                                ALU.mult).then_inc(cx_ready, 1)

            def residual(g):
                r = g.rows
                dve.wait_ge(wo_done, g.q + 1)
                dve.wait_ge(hb_ready, g.q + 1)
                V.tensor_tensor(h2[g.u][0:r, :], ps[0:r, 4, 0:D], hb[g.u][0:r, :], ALU.add).then_inc(h2_ready, 1)
                dve.wait_ge(h2_ready, g.q + 1)
                norm(g, h2[g.u][0:r, :], st2, mv2, ve2, ln2_stats, ln2_mean, ln2_var)
                if not (isinstance(g.q, int) and g.q < 2):
                    dve.wait_ge(scattered[g.u], 16 * TOPK * g.pair)
                ids = xs[g.u][:, ROW - 1:ROW].bitcast(I32)
                V.tensor_scalar(ids, ids, 2.0 * R, None, ALU.add)
                dve.wait_ge(ln2_rstd, g.q + 1)
                V.tensor_scalar(xs[g.u][0:r, 0:D], h2[g.u][0:r, :], mv2[0:r, 0:1], rs2[0:r, 0:1], ALU.subtract,
                                ALU.mult).then_inc(xn2_ready, 1)

            def choose(g):
                r = g.rows
                dve.wait_ge(router_done, g.q + 1)
                V.tensor_copy(lg[0:r, :], ps[0:r, 4, 0:E]).then_inc(logits_ready, 1)
                constant_wait()
                dve.wait_ge(logits_ready, g.q + 1)
                V.max(top[0:r, :], lg[0:r, :]).then_inc(top_ready, 1)
                constant_wait()
                dve.wait_ge(top_ready, g.q + 1)
                V.match_replace(cut[0:r, :], top[0:r, :], lg[0:r, :], NEG).then_inc(cut_ready, 1)
                if not (isinstance(g.q, int) and g.q == 0):
                    dve.wait_ge(ex_ready, g.q)
                V.tensor_scalar(shifted[0:r, :], lg[0:r, :], top[0:r, 0:1], None, ALU.subtract).then_inc(shifted_ready, 1)
                dve.wait_ge(cut_ready, g.q + 1)
                V.tensor_tensor(chosen[g.u][0:r, :], lg[0:r, :], cut[0:r, :], ALU.not_equal).then_inc(chosen_ready, 1)
                dve.wait_ge(chosen_ready, g.q + 1)
                if not (isinstance(g.q, int) and g.q == GROUPS - 1):
                    if not (isinstance(g.q, int) and g.q == 0):
                        dve.wait_ge(places_done, g.q)
                    V.tensor_tensor(earlier[1 - g.u][0:R, :], earlier[g.u][0:R, :], chosen[g.u][0:R, :],
                                    ALU.add).then_inc(earlier_ready, 1)

            def weigh(g):
                r = g.rows
                dve.wait_ge(ex_ready, g.q + 1)
                V.tensor_tensor_reduce(em[0:r, :], ex[0:r, :], chosen[g.u][0:r, :], 1.0, 0.0, ALU.mult, ALU.add,
                                       wsum[0:r, :]).then_inc(em_ready, 1)
                dve.wait_ge(em_ready, g.q + 1)
                V.reciprocal(wrec[0:r, :], wsum[0:r, :]).then_inc(wrec_ready, 1)
                dve.wait_ge(wrec_ready, g.q + 1)
                V.tensor_scalar(xs[g.u][0:r, D:D + E], em[0:r, :], wrec[0:r, 0:1], None, ALU.mult).then_inc(row_ready, 1)

            def place(g):
                r = g.rows
                dve.wait_ge(places_done, g.q + 1)
                V.tensor_tensor(room[0:r, :], base[0:r, :], ps[0:r, 4, 0:E], ALU.subtract)
                V.scalar_tensor_tensor(out=fits[0:r, :], in0=ps[0:r, 4, 0:E], scalar=float(CAP),
                                       in1=chosen[g.u][0:r, :], op0=ALU.is_lt, op1=ALU.mult).then_inc(room_ready, 1)
                dve.wait_ge(room_ready, g.q + 1)
                V.tensor_tensor(code[0:r, :], room[0:r, :], fits[0:r, :], ALU.mult).then_inc(code_ready, 1)
                constant_wait()
                dve.wait_ge(code_ready, g.q + 1)
                V.max(top2[0:r, :], code[0:r, :]).then_inc(top2_ready, 1)
                dve.wait_ge(top2_ready, g.q + 1)
                V.tensor_scalar(idx[g.u][0:r, :], top2[0:r, :], -1.0, float(SLOTS), ALU.mult, ALU.add).then_inc(idx_ready, 1)

            def shared_gate(g):
                r = g.rows
                gu = ps[0:FP, 0, 0:4 * R].rearrange("p (k r) -> p k r", k=4)
                dve.wait_ge(tanh_ready, g.q + 1)
                V.scalar_tensor_tensor(out=g1[:, :, 0:r], in0=th[:, :, 0:r], scalar=1.0, in1=gu[:, 0:2, 0:r],
                                       op0=ALU.add, op1=ALU.mult).then_inc(g1_ready, 1)
                dve.wait_ge(g1_ready, g.q + 1)
                if not (isinstance(g.q, int) and g.q == 0):
                    dve.wait_ge(down_done, g.q)
                V.scalar_tensor_tensor(out=hs[:, :, 0:r], in0=g1[:, :, 0:r], scalar=0.5, in1=gu[:, 2:4, 0:r],
                                       op0=ALU.mult, op1=ALU.mult).then_inc(hs_ready, 1)

            def shared_add(g):
                r = g.rows
                dve.wait_ge(down_done, g.q + 1)
                if not (isinstance(g.q, int) and g.q < 2):
                    dve.wait_ge(res_stored[g.u], 16 * g.pair)
                V.tensor_tensor(res[g.u][0:r, :], ps[0:r, 7, 0:D], h2[g.u][0:r, :], ALU.add).then_inc(res_ready, 1)

            def turn(b, c):
                here = 2 * b + c
                known = isinstance(here, int)
                front = not known or here + 1 < GROUPS
                mid = not known or 0 <= here < GROUPS
                back = not known or 0 <= here - 1 < GROUPS
                if mid:
                    copy_v(Group(b, c))
                if back:
                    residual(Group(b, c - 1))
                if mid:
                    softmax(Group(b, c))
                if front:
                    tokens(Group(b, c + 1))
                if back:
                    choose(Group(b, c - 1))
                if front:
                    normed(Group(b, c + 1))
                if back:
                    shared_gate(Group(b, c - 1))
                    weigh(Group(b, c - 1))
                    shared_add(Group(b, c - 1))
                    place(Group(b, c - 1))
                if mid:
                    gather_context(Group(b, c))

            for i in range(-1, 3):
                turn(0, i)
            with dve.Fori(1, PAIRS - 2) as b:
                turn(b, 1)
                turn(b, 2)
            for i in range(GROUPS - 3, GROUPS + 1):
                turn(0, i)

            def hidden(e, u):
                dve.wait_ge(silu_ready, e + 1)
                if not isinstance(e, int) or e >= 2:
                    dve.wait_ge(hh_turned, e - 1)
                V.tensor_tensor(hh[u][:, :], sg[u][:, :], ps[:, u, F:2 * F], ALU.mult).then_inc(hh_ready, 1)

            def weighed(e, u, c, lap):
                dve.wait_ge(e_down_done, e + 1)
                if not isinstance(e, int) or e >= 2:
                    dve.wait_ge(added[u], 8 * (e - u))
                V.tensor_scalar(ysc[u][:, :], ps[:, 6 + u, 0:D], xrow[c][:, bass.ds(D + e, 1)], None,
                                ALU.mult).then_inc(ysc_ready, 1)

            def experts(m, first=False):
                for c in range(4):
                    e = 4 * m + c
                    hidden(e, c % 2)
                    if not (first and c == 0):
                        weighed(e - 1, (c - 1) % 2, (c - 1) % 4, m)

            experts(0, first=True)
            with dve.Fori(1, E // 4) as m:
                experts(m)
            weighed(E - 1, 1, 3, E // 4 - 1)
            for n in range(len(OUT_PARTS)):
                dve.wait_ge(sums_landed[n], 32)
                V.tensor_tensor(out_tile(0, n), out_tile(0, n), out_tile(1, n), ALU.add).then_inc(out_ready, 1)


_INS = ['x', 'L0_tok_W', 'L0_tok_b', 'L0_tok_cls_token', 'L0_tok_pos_embedding', 'L0_attn_Wq', 'L0_attn_Wk',
        'L0_attn_Wv', 'L0_attn_Wo', 'L0_attn_bo', 'L0_ffn_router_w', 'L0_ffn_w_gate', 'L0_ffn_w_up',
        'L0_ffn_w_down', 'L0_ffn_ws_gate_up', 'L0_ffn_ws_down']
_OUTS = [((IMAGES, S, D), 'float32')]


def kernel(**inputs):
    import numpy as _np
    import concourse.bacc as _bacc
    from concourse import mybir as _mybir
    from concourse.bass_utils import run_bass_kernel_spmd as _run

    nc = _bacc.Bacc("TRN2", target_bir_lowering=False, num_devices=1)
    arrays, args = {}, []
    for name in _INS:
        a = _np.ascontiguousarray(inputs[name])
        arrays[f"in_{name}_dram"] = a
        args.append(nc.dram_tensor(f"in_{name}_dram", a.shape, _mybir.dt.from_np(a.dtype), kind="ExternalInput").ap())
    for i, (shape, dtype) in enumerate(_OUTS):
        dt = _mybir.dt.from_np(_np.dtype(dtype))
        args.append(nc.dram_tensor(f"out_{i}_dram", shape, dt, kind="ExternalOutput").ap())
    vit_kernel(nc, *args)
    r = _run(nc, [arrays], core_ids=[0])
    got = tuple(r.results[0][f"out_{i}_dram"] for i in range(len(_OUTS)))
    return got[0]
```

```python
from contextlib import ExitStack

import concourse.bass as bass
from concourse import mybir

F32 = mybir.dt.float32
BF16 = mybir.dt.bfloat16
U32 = mybir.dt.uint32
I32 = mybir.dt.int32
ALU = mybir.AluOpType
ACT = mybir.ActivationFunctionType
AX = mybir.AxisListType.X

P = 128
BANK = 512
IMAGES, CH, SIDE, PATCH = 64, 3, 96, 16
PS = SIDE // PATCH
NP = PS * PS
S = NP + 1
D = 256
KD = D // P
H, HD = 16, 16
GI = 3
R = GI * S
GROUPS = -(-IMAGES // GI)
T = IMAGES * S
HC = H // KD
HA = 4
PH = 3
PC = -(-H // PH)
VW = HD + 1
E, TOPK, F, CAP = 64, 8, 192, 128
FC, FP = 2, F // 2
SLOTS = E * CAP
ROW = D + E
NEG = -1e30
EPS = 1e-5
PAIR_ROWS = 2 * GI * CH * PS
PT_C = 2 * GI * S
HALF = 2
XCH = CH * HALF
RING = 20
EW = 2 * KD * F + FC * D


class Group:

    def __init__(self, b, c):
        self.q = 2 * b + c
        self.u = c % 2
        self.pair = b + c // 2
        last = isinstance(self.q, int) and self.q == GROUPS - 1
        self.images = IMAGES - GI * (GROUPS - 1) if last else GI
        self.rows = self.images * S


def vit_kernel(nc, x, W, b, cls, pos, Wq, Wk, Wv, Wo, bo, router_w, w_gate, w_up, w_down, ws_gate_up, ws_down, out):
    ctx = ExitStack()
    with ctx:
        def sb(name, shape, dt=F32):
            return ctx.enter_context(nc.sbuf_tensor(name, shape, dt))

        def sem(name):
            return ctx.enter_context(nc.semaphore(name))

        slots = nc.dram_tensor("slots", [SLOTS, 1], I32, kind="Internal").ap()
        table = nc.dram_tensor("table", [T + P, ROW], F32, kind="Internal").ap()
        acc = [nc.dram_tensor(f"acc{i}", [T + P, D], F32, kind="Internal").ap() for i in range(2)]

        ident = sb("ident", [P, P])
        before = sb("before", [P, R], BF16)
        ones = sb("ones", [P, R], BF16)
        headmask = sb("headmask", [P, HC])
        third = sb("third", [P, PC, PH])
        tri = sb("tri", [P, GI, S])
        causal = sb("causal", [P, S])
        posb = sb("posb", [P, D])
        posadd = sb("posadd", [P, D])
        bo_sb = sb("bo_sb", [P, D])
        base = sb("base", [P, E])
        halfneg = sb("halfneg", [P, 1])
        zero = sb("zero", [P, ROW])
        nobody = sb("nobody", [P, E], I32)
        wraw = sb("wraw", [P, KD, CH * PATCH * PATCH])
        rraw = sb("rraw", [E, D])
        wT = sb("wT", [P, XCH, D])
        wqk = sb("wqk", [P, KD, 2 * D])
        wv = sb("wv", [P, KD, D])
        wo = sb("wo", [P, KD, D])
        rT = sb("rT", [P, KD, E])
        wsgu = sb("wsgu", [P, KD, 2 * F])
        wsd = sb("wsd", [FP, FC, D])
        xraw = sb("xraw", [PAIR_ROWS, PATCH * SIDE])
        xw = sb("xw", [PAIR_ROWS, PS, PATCH * PATCH])
        pT = sb("pT", [P, XCH, PT_C])
        h = [sb(f"h{u}", [P, D]) for u in range(2)]
        hb = [sb(f"hb{u}", [P, D]) for u in range(2)]
        st1 = sb("st1", [P, 6])
        mv1 = sb("mv1", [P, 2])
        ve1 = sb("ve1", [P, 1])
        rs1 = sb("rs1", [P, 1])
        xn = sb("xn", [P, D])
        xnT = sb("xnT", [P, KD, GI, PH, S])
        qz = sb("qz", [P, KD, GI, R])
        keys = sb("keys", [P, KD, R])
        kz = sb("kz", [P, KD, HC, R])
        vz = sb("vz", [R, GI, PC * PH, VW])
        sm = sb("sm", [P, H, S])
        mx = sb("mx", [P, H])
        sx = sb("sx", [P, H, S])
        prob = sb("prob", [P, H * S])
        probT = sb("probT", [P, PC, R])
        ctxsum = sb("ctxsum", [P, PC * PH, VW])
        rden = sb("rden", [P, H])
        cx = sb("cx", [P, H, HD])
        cxT = sb("cxT", [P, KD, R])
        h2 = [sb(f"h2{u}", [P, D]) for u in range(2)]
        st2 = sb("st2", [P, 6])
        mv2 = sb("mv2", [P, 2])
        ve2 = sb("ve2", [P, 1])
        rs2 = sb("rs2", [P, 1])
        xs = [sb(f"xs{u}", [P, ROW]) for u in range(2)]
        xn2T = sb("xn2T", [P, KD, R])
        number = [sb(f"number{u}", [P, 1], I32) for u in range(2)]
        lg = sb("lg", [P, E])
        top = sb("top", [P, TOPK])
        cut = sb("cut", [P, E])
        shifted = sb("shifted", [P, E])
        chosen = [sb(f"chosen{u}", [P, E], BF16) for u in range(2)]
        earlier = [sb(f"earlier{u}", [P, E], BF16) for u in range(2)]
        ex = sb("ex", [P, E])
        em = sb("em", [P, E])
        wsum = sb("wsum", [P, 1])
        wrec = sb("wrec", [P, 1])
        room = sb("room", [P, E])
        fits = sb("fits", [P, E])
        code = sb("code", [P, E])
        top2 = sb("top2", [P, TOPK])
        idx = [sb(f"idx{u}", [P, TOPK], U32) for u in range(2)]
        th = sb("th", [FP, FC, R])
        g1 = sb("g1", [FP, FC, R])
        hs = sb("hs", [FP, FC, R])
        res = [sb(f"res{u}", [P, D]) for u in range(2)]
        ew = sb("ew", [P, RING, EW])
        slot_tok = sb("slot_tok", [P, E], I32)
        tok = [sb(f"tok{c}", [P, 1], I32) for c in range(8)]
        xrow = [t.rearrange(dims)[:, c * ROW:(c + 1) * ROW] for t, dims in
                ((wT[:, :, :], "p a b -> p (a b)"), (kz[:, :, :, :], "p a b c -> p (a b c)")) for c in range(4)]
        xT = [sb(f"xT{u}", [P, KD, P]) for u in range(2)]
        sg = [sb(f"sg{u}", [P, F]) for u in range(2)]
        hh = [sb(f"hh{u}", [P, F]) for u in range(2)]
        hT = [sb(f"hT{u}", [FP, FC, P]) for u in range(2)]
        ysc = [pT[:, :, :].rearrange("p a b -> p (a b)")[:, c * D:(c + 1) * D] for c in range(4)]

        ps = ctx.enter_context(nc.psum_tensor("ps", [P, 8, BANK], F32))

        x_landed = sem("x_landed")
        x_sorted = sem("x_sorted")
        w_landed = sem("w_landed")
        router_landed = sem("router_landed")
        pos_landed = sem("pos_landed")
        qk_landed = sem("qk_landed")
        v_landed = sem("v_landed")
        bo_landed = sem("bo_landed")
        wo_landed = sem("wo_landed")
        shared_landed = sem("shared_landed")
        consts_made = sem("consts_made")
        zeros_made = sem("zeros_made")
        masks_made = sem("masks_made")
        posb_made = sem("posb_made")
        dve_const = sem("dve_const")
        slots_cleared = sem("slots_cleared")
        rows_cleared = sem("rows_cleared")
        wT_turned = sem("wT_turned")
        wT_copied = sem("wT_copied")
        patches_turned = sem("patches_turned")
        patches_copied = sem("patches_copied")
        embedded = sem("embedded")
        h_ready = sem("h_ready")
        hb_ready = sem("hb_ready")
        ln1_stats = sem("ln1_stats")
        ln1_mean = sem("ln1_mean")
        ln1_var = sem("ln1_var")
        ln1_rstd = sem("ln1_rstd")
        xn_ready = sem("xn_ready")
        xn_turned = sem("xn_turned")
        xnT_ready = sem("xnT_ready")
        qk_done = sem("qk_done")
        q_ready = sem("q_ready")
        keys_ready = sem("keys_ready")
        k_ready = sem("k_ready")
        k_more_ready = sem("k_more_ready")
        v_done = sem("v_done")
        v_ready = sem("v_ready")
        scores_done = [sem(f"scores_done{c}") for c in range(KD)]
        masked = [sem(f"masked{c}") for c in range(KD)]
        max_ready = [sem(f"max_ready{c}") for c in range(KD)]
        lowered = [sem(f"lowered{c}") for c in range(KD)]
        prob_ready = [sem(f"prob_ready{c}") for c in range(KD)]
        prob_turned = sem("prob_turned")
        probT_ready = sem("probT_ready")
        pv_done = sem("pv_done")
        sum_a = sem("sum_a")
        sum_b = sem("sum_b")
        sum_ready = sem("sum_ready")
        rden_ready = sem("rden_ready")
        cx_ready = sem("cx_ready")
        cx_turned = sem("cx_turned")
        cxT_ready = sem("cxT_ready")
        wo_done = sem("wo_done")
        h2_ready = sem("h2_ready")
        ln2_stats = sem("ln2_stats")
        ln2_mean = sem("ln2_mean")
        ln2_var = sem("ln2_var")
        ln2_rstd = sem("ln2_rstd")
        xn2_ready = sem("xn2_ready")
        xn2_turned = sem("xn2_turned")
        xn2T_ready = sem("xn2T_ready")
        router_done = sem("router_done")
        logits_ready = sem("logits_ready")
        top_ready = sem("top_ready")
        cut_ready = sem("cut_ready")
        chosen_ready = sem("chosen_ready")
        shifted_ready = sem("shifted_ready")
        ex_ready = sem("ex_ready")
        em_ready = sem("em_ready")
        wrec_ready = sem("wrec_ready")
        row_ready = sem("row_ready")
        number_ready = sem("number_ready")
        earlier_ready = sem("earlier_ready")
        places_done = sem("places_done")
        room_ready = sem("room_ready")
        fits_ready = sem("fits_ready")
        code_ready = sem("code_ready")
        top2_ready = sem("top2_ready")
        idx_ready = sem("idx_ready")
        scattered = [sem(f"scattered{u}") for u in range(2)]
        gu_done = sem("gu_done")
        tanh_ready = sem("tanh_ready")
        g1_ready = sem("g1_ready")
        hs_ready = sem("hs_ready")
        down_done = sem("down_done")
        res_ready = sem("res_ready")
        res_stored = [sem(f"res_stored{u}") for u in range(2)]
        row_stored = [sem(f"row_stored{u}") for u in range(2)]
        slot_tok_landed = sem("slot_tok_landed")
        ew_landed = [sem(f"ew_landed{u}") for u in range(2)]
        row_landed = [sem(f"row_landed{c}") for c in range(8)]
        row_turned = sem("row_turned")
        xT_ready = sem("xT_ready")
        e_gu_done = sem("e_gu_done")
        silu_ready = sem("silu_ready")
        hh_ready = sem("hh_ready")
        hh_turned = sem("hh_turned")
        hT_ready = sem("hT_ready")
        e_down_done = sem("e_down_done")
        ysc_ready = sem("ysc_ready")
        added = [sem(f"added{u}") for u in range(2)]
        tok_ready = sem("tok_ready")
        out_ready = sem("out_ready")
        out_stored = sem("out_stored")

        block = ctx.enter_context(nc.Block())

        CONSTS = 19
        PAIRS = GROUPS // 2
        EPAIRS = E // 2

        def x_pair(pair, images):
            rows = images * CH * PS
            src = x.rearrange("n c (r i) w -> (n c r) (i w)", i=PATCH)
            return xraw[0:rows, :], src[bass.ds(pair * PAIR_ROWS, rows), :]

        MAIN = T // P
        OUT_PARTS = [(P, r, 6) for r in range(0, MAIN, 6)] + [(T - MAIN * P, MAIN, 1)]
        sums_landed = [sem(f"sums_landed{n}") for n in range(len(OUT_PARTS))]
        flat = ew[:, :, :].rearrange("p a b -> p (a b)")

        def out_tile(k, n):
            parts, at, rows = OUT_PARTS[n]
            lo = (k * (MAIN + 1) + at) * D
            return flat[0:parts, lo:lo + rows * D]

        def out_rows(dram, n):
            parts, at, rows = OUT_PARTS[n]
            if at == MAIN:
                return dram[MAIN * P:T, :]
            return dram[0:MAIN * P, :].rearrange("(p r) d -> p r d", p=P)[:, at:at + rows, :].rearrange("p r d -> p (r d)")

        @block.sync
        def _(sp):
            sp.dma_start(*x_pair(0, 2 * GI)).then_inc(x_landed, 16)
            sp.dma_start(wraw[:, :, :], W.rearrange("(k p) d -> p k d", p=P)).then_inc(w_landed, 16)
            sp.dma_start(rraw[:, :], router_w).then_inc(router_landed, 16)
            for i in range(GI):
                sp.dma_start(posb[S * i:S * i + S, :], pos[0, :, :]).then_inc(pos_landed, 16)
                sp.dma_start(posadd[S * i:S * i + 1, :], cls[0, :, :]).then_inc(pos_landed, 16)
                sp.dma_start(posadd[S * i + 1:S * i + S, :],
                             b.rearrange("(o d) -> o d", o=1).broadcast_to([NP, D])).then_inc(pos_landed, 16)
            sp.dma_start(wqk[:, :, 0:D], Wq.rearrange("(k p) n -> p k n", p=P)).then_inc(qk_landed, 16)
            sp.dma_start(wqk[:, :, D:2 * D], Wk.rearrange("(k p) n -> p k n", p=P)).then_inc(qk_landed, 16)
            sp.dma_start(wv[:, :, :], Wv.rearrange("(k p) n -> p k n", p=P)).then_inc(v_landed, 16)
            sp.dma_start(bo_sb[0:R, :], bo.rearrange("(o d) -> o d", o=1).broadcast_to([R, D])).then_inc(bo_landed, 16)
            sp.dma_start(wo[:, :, :], Wo.rearrange("(k p) n -> p k n", p=P)).then_inc(wo_landed, 16)
            sp.dma_start(wsgu[:, :, :], ws_gate_up.rearrange("(k p) n -> p k n", p=P)).then_inc(shared_landed, 16)
            sp.dma_start(wsd[:, :, :], ws_down.rearrange("(k p) n -> p k n", p=FP)).then_inc(shared_landed, 16)
            sp.wait_ge(consts_made, CONSTS)
            sp.dma_start(slots.rearrange("(p e) o -> p (e o)", p=P), nobody[:, :]).then_inc(slots_cleared, 16)
            sp.dma_start(table[T:T + P, :], zero[:, :]).then_inc(rows_cleared, 16)

            def load_x(pair, images=2 * GI):
                sp.wait_ge(x_sorted, pair)
                sp.dma_start(*x_pair(pair, images)).then_inc(x_landed, 16)

            def load_experts(pair, u, slot):
                ring = ew[:, bass.ds(slot, 2), :]
                for w, at, parts, wide in ((w_gate, 0, P, KD * F), (w_up, KD * F, P, KD * F),
                                           (w_down, 2 * KD * F, FP, FC * D)):
                    sp.dma_start(ring[0:parts, :, at:at + wide],
                                 w.rearrange("e (p k) f -> p e (k f)", p=parts)[:, bass.ds(2 * pair, 2), :]
                                 ).then_inc(ew_landed[u], 16)

            def store_rows(g):
                sp.wait_ge(row_ready, g.q + 1)
                sp.dma_start(table[bass.ds(g.q * R, g.rows), :], xs[g.u][0:g.rows, :]).then_inc(row_stored[g.u], 16)
                sp.wait_ge(res_ready, g.q + 1)
                sp.dma_start(acc[0][bass.ds(g.q * R, g.rows), :], res[g.u][0:g.rows, :]).then_inc(res_stored[g.u], 16)

            load_experts(0, 0, 0)
            load_x(1)
            sp.dma_start(acc[1].rearrange("(a p) c -> p a c", p=FP),
                         zero[0:FP, 0:D].unsqueeze(1).broadcast_to([FP, (T + P) // FP, D])).then_inc(rows_cleared, 16)
            sp.dma_start(acc[0][T:T + P, :], zero[:, 0:D]).then_inc(rows_cleared, 16)
            load_experts(1, 1, 2)
            store_rows(Group(0, 0))
            with sp.Fori(1, PAIRS // 2) as j:
                for u in range(2):
                    pair = 2 * j + u
                    load_x(pair)
                    sp.wait_ge(ew_landed[u], 48 * j)
                    load_experts(pair, u, 2 * pair)
                    store_rows(Group(pair, -3))
                    store_rows(Group(pair, -2))
            load_x(PAIRS - 1, IMAGES - 2 * GI * (PAIRS - 1))
            for pair in range(PAIRS - 1, RING // 2):
                sp.wait_ge(ew_landed[pair % 2], 48 * (pair // 2))
                load_experts(pair, pair % 2, 2 * pair)
            for q in range(2 * PAIRS - 5, GROUPS):
                store_rows(Group(0, q))
            for u in range(2):
                sp.wait_ge(scattered[u], 16 * TOPK * PAIRS)
            sp.dma_start(slot_tok[:, :], slots.rearrange("(p e) o -> p (e o)", p=P)).then_inc(slot_tok_landed, 16)

            def more_experts(m, n):
                sp.wait_ge(e_down_done, 4 * m + 2 * n + 2)
                sp.wait_ge(ew_landed[n], 48 * (m + RING // 4))
                load_experts(2 * m + n + RING // 2, n, (4 * m + 2 * n) % RING)

            with sp.Fori(0, (E - RING) // 4) as m:
                for n in range(2):
                    more_experts(m, n)
            for u in range(2):
                sp.wait_ge(added[u], 16 * E // 2)
                sp.wait_ge(res_stored[u], 16 * PAIRS)
            for n, (parts, at, rows) in enumerate(OUT_PARTS):
                for k in range(2):
                    sp.dma_start(out_tile(k, n), out_rows(acc[k], n)).then_inc(sums_landed[n], 16)
            for n in range(len(OUT_PARTS)):
                sp.wait_ge(out_ready, n + 1)
                sp.dma_start(out_rows(out.rearrange("n s d -> (n s) d"), n), out_tile(0, n)).then_inc(out_stored, 16)
            sp.wait_ge(out_stored, 16 * len(OUT_PARTS))

        @block.gpsimd
        def _(pool):
            made = [0]

            def step(ins):
                made[0] += 1
                ins.then_inc(consts_made, 1)

            def done():
                pool.wait_ge(consts_made, made[0])

            step(pool.memset(ident[:, :], 0.0))
            step(pool.memset(ones[:, :], 1.0))
            step(pool.memset(before[:, :], 1.0))
            step(pool.memset(headmask[:, :], 1.0))
            step(pool.memset(third[:, :, :], 1.0))
            step(pool.memset(tri[:, :, :], 0.0))
            step(pool.memset(halfneg[:, :], -0.5))
            step(pool.memset(zero[:, :], 0.0))
            step(pool.iota(nobody[:, :], [[0, E]], base=T, channel_multiplier=1))
            step(pool.iota(base[:, :], [[-1, E]], base=SLOTS, channel_multiplier=0,
                           allow_small_or_imprecise_dtypes=True))
            for u in range(2):
                step(pool.iota(number[u][:, :], [[0, 1]], base=R * u - 2 * R, channel_multiplier=1))
            done()
            step(pool.affine_select(out=ident[:, :], in_=ident[:, :], compare_op=ALU.not_equal, fill=1.0, base=0,
                                    pattern=[[-1, P]], channel_multiplier=1))
            step(pool.affine_select(out=before[:, :], in_=before[:, :], compare_op=ALU.is_gt, fill=0.0, base=0,
                                    pattern=[[1, R]], channel_multiplier=-1))
            step(pool.affine_select(out=headmask[:, :], in_=headmask[:, :], compare_op=ALU.is_ge, fill=0.0, base=0,
                                    pattern=[[-HD, HC]], channel_multiplier=1))
            step(pool.affine_select(out=third[:, :, :], in_=third[:, :, :], compare_op=ALU.is_ge, fill=0.0, base=0,
                                    pattern=[[0, PC], [-S, PH]], channel_multiplier=1))
            step(pool.affine_select(out=tri[:, :, :], in_=tri[:, :, :], compare_op=ALU.is_ge, fill=NEG, base=0,
                                    pattern=[[-S, GI], [-1, S]], channel_multiplier=1))
            done()
            step(pool.affine_select(out=headmask[:, :], in_=headmask[:, :], compare_op=ALU.is_ge, fill=0.0,
                                    base=HD - 1, pattern=[[HD, HC]], channel_multiplier=-1))
            step(pool.affine_select(out=third[:, :, :], in_=third[:, :, :], compare_op=ALU.is_ge, fill=0.0,
                                    base=S - 1, pattern=[[0, PC], [S, PH]], channel_multiplier=-1))
            assert made[0] == CONSTS

            def rstd(g, ve, rs, var_ready, ready):
                pool.wait_ge(var_ready, g.q + 1)
                pool.tensor_tensor(rs[0:g.rows, :], ve[0:g.rows, :], halfneg[0:g.rows, :], ALU.pow).then_inc(ready, 1)

            def add_bo(g):
                if isinstance(g.q, int) and g.q == 0:
                    pool.wait_ge(bo_landed, 16)
                pool.wait_ge(h_ready, g.q + 1)
                if not (isinstance(g.q, int) and g.q < 2):
                    pool.wait_ge(h2_ready, g.q - 1)
                pool.tensor_tensor(hb[g.u][0:g.rows, :], h[g.u][0:g.rows, :], bo_sb[0:g.rows, :],
                                   ALU.add).then_inc(hb_ready, 1)

            def constant_wait():
                pool.wait_ge(consts_made, CONSTS)

            def scatter(g):
                constant_wait()
                pool.wait_ge(idx_ready, g.q + 1)
                pool.wait_ge(number_ready, g.q + 1)
                for k in range(TOPK):
                    pool.indirect_dma_start(
                        slots, bass.IndirectOffsetOnAxis(ap=idx[g.u][0:g.rows, k:k + 1], axis=0),
                        number[g.u][0:g.rows, :], None, bounds_check=SLOTS - 1, oob_is_err=False,
                    ).then_inc(scattered[g.u], 16)

            def turn(b, c):
                here = 2 * b + c
                known = isinstance(here, int)
                if not known or 0 <= here - 1 < GROUPS:
                    rstd(Group(b, c - 1), ve2, rs2, ln2_var, ln2_rstd)
                if not known or here + 1 < GROUPS:
                    g = Group(b, c + 1)
                    rstd(g, ve1, rs1, ln1_var, ln1_rstd)
                    add_bo(g)
                if not known or 0 <= here - 2 < GROUPS:
                    if known and here == 2:
                        pool.wait_ge(slots_cleared, 16)
                    scatter(Group(b, c - 2))

            for i in range(-1, 3):
                turn(0, i)
            with pool.Fori(1, PAIRS - 2) as b:
                turn(b, 1)
                turn(b, 2)
            for i in range(GROUPS - 3, GROUPS + 2):
                turn(0, i)

            def take_tok(e, c):
                pool.tensor_copy(tok[c % 8][:, :], slot_tok[:, bass.ds(e, 1)]).then_inc(tok_ready, 1)

            def gather(c):
                pool.indirect_dma_start(
                    xrow[c % 8][:, :], None, table, bass.IndirectOffsetOnAxis(ap=tok[c % 8][:, :].bitcast(U32), axis=0),
                    bounds_check=T + P - 1, oob_is_err=False,
                ).then_inc(row_landed[c % 8], 16)

            def add(c):
                pool.indirect_dma_start(
                    acc[c % 2], bass.IndirectOffsetOnAxis(ap=tok[c % 8][:, :].bitcast(U32), axis=0),
                    ysc[c % 4][:, :], None, compute_op=ALU.add,
                ).then_inc(added[c % 2], 16)

            def step_two(e, c):
                known = isinstance(e, int)
                u = (c - 1) % 2
                if not known or e >= 1:
                    pool.wait_ge(ysc_ready, e)
                if not known or e >= 3:
                    pool.wait_ge(added[u], 8 * (e - 1 - u))
                pool.wait_ge(tok_ready, e + 5 if not known else min(e + 5, E))
                if not known or e + 5 < E:
                    take_tok(e + 5, c + 5)
                if not known or e >= 1:
                    add(c - 1)
                if not known or e + 4 < E:
                    gather(c + 4)

            pool.wait_ge(slot_tok_landed, 16)
            for u in range(2):
                pool.wait_ge(row_stored[u], 16 * PAIRS)
                pool.wait_ge(res_stored[u], 16 * PAIRS)
            pool.wait_ge(rows_cleared, 48)
            for e in range(5):
                take_tok(e, e)
            pool.wait_ge(tok_ready, 5)
            for e in range(4):
                gather(e)
            for e in range(8):
                step_two(e, e)
            with pool.Fori(1, E // 8 - 1) as m:
                for c in range(8):
                    step_two(8 * m + c, c)
            for e in range(E - 8, E + 1):
                step_two(e, e)

        @block.scalar
        def _(act):
            def sort_x(pair, images):
                rows = images * CH * PS
                act.wait_ge(x_landed, 16 * (pair + 1))
                if not (isinstance(pair, int) and pair == 0):
                    act.wait_ge(patches_turned, 4 * pair)
                nc.scalar.activation(xw[0:rows, :, :].rearrange("p w (i j) -> p w i j", i=PATCH),
                                     xraw[0:rows, :].rearrange("p (i w j) -> p w i j", i=PATCH, w=PS),
                                     ACT.Copy).then_inc(x_sorted, 1)

            sort_x(0, 2 * GI)
            for n in range(4):
                act.wait_ge(wT_turned, n + 1)
                if n < 3:
                    nc.scalar.activation(wT[:, 2 * n:2 * n + 2, :].rearrange("p a b -> p (a b)"),
                                         ps[:, n, 0:2 * D], ACT.Copy).then_inc(wT_copied, 1)
                else:
                    nc.scalar.activation(rT[:, :, :].rearrange("p a b -> p (a b)"), ps[:, n, 0:KD * E],
                                         ACT.Copy).then_inc(wT_copied, 1)

            def copy_patches(pair, n, images):
                half, w3 = n // 2, n % 2
                act.wait_ge(patches_turned, 4 * pair + n + 1)
                if not (isinstance(pair, int) and pair == 0):
                    act.wait_ge(embedded, 2 * pair)
                rows = images * CH * PS
                src = ps[:, 7, 0:3 * rows].rearrange("p (w b c r) -> p b c r w", w=3, b=images, c=CH)
                for c in range(CH):
                    dst = pT[:, c * HALF + half, :].rearrange("p (b s) -> p b s", s=S)[:, 0:images, 1:S].rearrange(
                        "p b (r w) -> p b r w", r=PS)
                    ins = nc.scalar.activation(dst[:, :, :, 3 * w3:3 * w3 + 3], src[:, :, c, :, :], ACT.Copy)
                ins.then_inc(patches_copied, 1)

            def copy_xnT(g):
                act.wait_ge(xn_turned, g.q + 1)
                if not (isinstance(g.q, int) and g.q == 0):
                    act.wait_ge(v_done, g.q)
                for k in range(KD):
                    src = ps[:, 1, k * R:k * R + g.rows].rearrange("p (i s) -> p i s", s=S)
                    ins = nc.scalar.activation(xnT[:, k, 0:g.images, :, :],
                                               src.unsqueeze(2).broadcast_to([P, g.images, PH, S]), ACT.Copy)
                ins.then_inc(xnT_ready, 1)

            def copy_q(g):
                act.wait_ge(keys_ready, g.q + 1)
                if not (isinstance(g.q, int) and g.q == 0):
                    act.wait_ge(scores_done[1], g.q)
                q = ps[:, 0, 0:KD * R].rearrange("p (k r) -> p k r", k=KD)
                for c in range(KD):
                    zero_diag = qz[:, c, :, :].rearrange("p i r -> p (i r)")
                    dst = bass.AP(tensor=zero_diag.tensor, offset=zero_diag.offset,
                                  ap=[zero_diag.ap[0], [R + S, g.images], [1, S]])
                    ins = nc.scalar.activation(dst, q[:, c, 0:g.rows].rearrange("p (i s) -> p i s", i=g.images), ACT.Copy)
                ins.then_inc(q_ready, 1)
                for hd in range(HA):
                    ins = nc.scalar.activation(kz[:, :, hd, 0:g.rows], keys[:, :, 0:g.rows], ACT.Copy,
                                               scale=headmask[:, hd:hd + 1])
                ins.then_inc(k_ready, 1)

            def copy_cxT(g):
                act.wait_ge(cx_turned, g.q + 1)
                if not (isinstance(g.q, int) and g.q == 0):
                    act.wait_ge(wo_done, g.q)
                nc.scalar.activation(cxT[:, :, 0:g.rows], ps[:, 1, 0:KD * R].rearrange("p (k r) -> p k r", k=KD)[:, :, 0:g.rows],
                                     ACT.Copy).then_inc(cxT_ready, 1)

            def copy_xn2T(g):
                act.wait_ge(xn2_turned, g.q + 1)
                if not (isinstance(g.q, int) and g.q == 0):
                    act.wait_ge(gu_done, g.q)
                nc.scalar.activation(xn2T[:, :, 0:g.rows], ps[:, 1, 0:KD * R].rearrange("p (k r) -> p k r", k=KD)[:, :, 0:g.rows],
                                     ACT.Copy).then_inc(xn2T_ready, 1)

            def exp_probs(g, c):
                act.wait_ge(lowered[c], g.q + 1)
                if not (isinstance(g.q, int) and g.q == 0):
                    act.wait_ge(prob_turned, g.q)
                nc.scalar.activation(prob[0:g.rows, c * HC * S:(c + 1) * HC * S],
                                     sx[0:g.rows, c * HC:(c + 1) * HC, :].rearrange("p h s -> p (h s)"), ACT.Exp,
                                     scale=float(HD) ** -0.5).then_inc(prob_ready[c], 1)

            def copy_probT(g):
                act.wait_ge(prob_turned, g.q + 1)
                if not (isinstance(g.q, int) and g.q == 0):
                    act.wait_ge(pv_done, g.q)
                a = ps[:, 2, 0:3 * R].rearrange("p (k r) -> p k r", k=3)
                z = ps[:, 3, 0:3 * R].rearrange("p (k r) -> p k r", k=3)
                nc.scalar.activation(probT[0:R, 0:3, 0:g.rows], a[0:R, :, 0:g.rows], ACT.Copy)
                nc.scalar.activation(probT[0:R, 3:5, 0:g.rows], z[0:R, 0:2, 0:g.rows], ACT.Copy)
                nc.scalar.activation(probT[0:S, 5, 0:g.rows], z[0:S, 2, 0:g.rows], ACT.Copy).then_inc(probT_ready, 1)

            def route_exp(g):
                act.wait_ge(shifted_ready, g.q + 1)
                if not (isinstance(g.q, int) and g.q == 0):
                    act.wait_ge(em_ready, g.q)
                nc.scalar.activation(ex[0:g.rows, :], shifted[0:g.rows, :], ACT.Exp).then_inc(ex_ready, 1)

            def shared_tanh(g):
                act.wait_ge(gu_done, g.q + 1)
                if not (isinstance(g.q, int) and g.q == 0):
                    act.wait_ge(g1_ready, g.q)
                nc.scalar.activation(th[:, :, 0:g.rows], ps[0:FP, 0, 0:2 * R].rearrange("p (k r) -> p k r", k=2)[:, :, 0:g.rows],
                                     ACT.Tanh, scale=0.5).then_inc(tanh_ready, 1)

            def turn(b, c):
                here = 2 * b + c
                known = isinstance(here, int)
                front = not known or here + 1 < GROUPS
                mid = not known or 0 <= here < GROUPS
                back = not known or 0 <= here - 1 < GROUPS
                pair = b + (c + 1) // 2
                images = 2 * GI
                if isinstance(pair, int):
                    images = min(images, IMAGES - 2 * GI * pair)
                turning = c % 2 == 1 and images > 0 and front
                if turning:
                    copy_patches(pair, 0, images)
                if mid:
                    copy_q(Group(b, c))
                if turning:
                    copy_patches(pair, 1, images)
                if back:
                    copy_cxT(Group(b, c - 1))
                if turning:
                    copy_patches(pair, 2, images)
                if mid:
                    exp_probs(Group(b, c), 0)
                if turning:
                    copy_patches(pair, 3, images)
                if mid:
                    exp_probs(Group(b, c), 1)
                if back:
                    copy_xn2T(Group(b, c - 1))
                if mid:
                    copy_probT(Group(b, c))
                if back:
                    shared_tanh(Group(b, c - 1))
                    route_exp(Group(b, c - 1))
                if front:
                    copy_xnT(Group(b, c + 1))
                if c % 2 == 0 and (not known or 2 * pair + 2 < GROUPS):
                    sort_x(pair + 1, 2 * GI if not known else min(2 * GI, IMAGES - 2 * GI * (pair + 1)))

            act.wait_ge(consts_made, CONSTS)
            act.wait_ge(masks_made, 4)
            for i in range(-1, 3):
                turn(0, i)
            with act.Fori(1, PAIRS - 2) as b:
                turn(b, 1)
                turn(b, 2)
            for i in range(GROUPS - 3, GROUPS + 1):
                turn(0, i)

            def copy_xT(e, u):
                act.wait_ge(row_turned, e + 1)
                if not isinstance(e, int) or e >= 2:
                    act.wait_ge(e_gu_done, e - 1)
                nc.scalar.activation(xT[u][:, :, :].rearrange("p k r -> p (k r)"), ps[:, 2 + u, 0:KD * P],
                                     ACT.Copy).then_inc(xT_ready, 1)

            def silu(e, u):
                act.wait_ge(e_gu_done, e + 1)
                if not isinstance(e, int) or e >= 2:
                    act.wait_ge(hh_ready, e - 1)
                nc.scalar.activation(sg[u][:, :], ps[:, u, 0:F], ACT.Silu).then_inc(silu_ready, 1)

            def copy_hT(e, u):
                act.wait_ge(hh_turned, e + 1)
                if not isinstance(e, int) or e >= 2:
                    act.wait_ge(e_down_done, e - 1)
                nc.scalar.activation(hT[u][:, :, :].rearrange("p k r -> p (k r)"), ps[0:FP, 4 + u, 0:FC * P],
                                     ACT.Copy).then_inc(hT_ready, 1)

            def expert(e, u, more=True):
                silu(e, u)
                if more:
                    copy_xT(e + 1, 1 - u)
                copy_hT(e, u)

            copy_xT(0, 0)
            expert(0, 0)
            expert(1, 1)
            with act.Fori(1, E // 2 - 1) as m:
                expert(2 * m, 0)
                expert(2 * m + 1, 1)
            expert(E - 2, 0)
            expert(E - 1, 1, more=False)

        @block.tensor
        def _(pe):
            pe.wait_ge(consts_made, CONSTS)
            pe.wait_ge(w_landed, 16)
            for n in range(3):
                for dd in range(2):
                    for k in range(KD):
                        ins = nc.tensor.transpose(ps[:, n, dd * D + k * P:dd * D + (k + 1) * P],
                                                  wraw[:, k, (2 * n + dd) * P:(2 * n + dd + 1) * P], ident[:, :])
                ins.then_inc(wT_turned, 1)
            pe.wait_ge(router_landed, 16)
            for k in range(KD):
                ins = nc.tensor.transpose(ps[:, 3, k * E:(k + 1) * E], rraw[:, k * P:(k + 1) * P], ident[0:E, 0:E])
            ins.then_inc(wT_turned, 1)
            pe.wait_ge(wT_copied, 4)

            def turn_patches(pair, n, images):
                half, w3 = n // 2, n % 2
                rows = images * CH * PS
                if n == 0:
                    pe.wait_ge(x_sorted, pair + 1)
                    if not (isinstance(pair, int) and pair < 1):
                        pe.wait_ge(res_ready, 2 * pair - 2)
                else:
                    pe.wait_ge(patches_copied, 4 * pair + n)
                for w in range(3):
                    ins = nc.tensor.transpose(ps[:, 7, w * rows:(w + 1) * rows],
                                              xw[0:rows, 3 * w3 + w, half * P:(half + 1) * P], ident[0:rows, 0:rows])
                ins.then_inc(patches_turned, 1)

            def embed(g):
                pe.wait_ge(patches_copied, 4 * g.pair + 4)
                if g.u == 1:
                    if not (isinstance(g.q, int) and g.q < 2):
                        pe.wait_ge(res_ready, g.q - 2)
                    else:
                        pe.wait_ge(h_ready, 1)
                for c in range(CH):
                    for half in range(HALF):
                        ins = nc.tensor.matmul(ps[0:g.rows, 7, 0:D],
                                               pT[:, c * HALF + half, g.u * R:g.u * R + g.rows], wT[:, c * HALF + half, :],
                                               start=(c + half == 0), stop=(c == CH - 1 and half == HALF - 1))
                ins.then_inc(embedded, 1)

            def turn_two(g, src, done):
                for k in range(KD):
                    ins = nc.tensor.transpose(ps[:, 1, k * R:k * R + g.rows], src[0:g.rows, k * P:(k + 1) * P],
                                              ident[0:g.rows, 0:g.rows])
                ins.then_inc(done, 1)

            def turn_xn(g):
                pe.wait_ge(xn_ready, g.q + 1)
                if not (isinstance(g.q, int) and g.q < 2):
                    pe.wait_ge(xn2T_ready, g.q - 1)
                elif g.q == 1:
                    pe.wait_ge(xnT_ready, 1)
                turn_two(g, xn, xn_turned)

            def project_qk(g):
                if isinstance(g.q, int) and g.q == 0:
                    pe.wait_ge(qk_landed, 32)
                pe.wait_ge(xnT_ready, g.q + 1)
                if not (isinstance(g.q, int) and g.q < 2):
                    pe.wait_ge(hs_ready, g.q - 1)
                elif g.q == 1:
                    pe.wait_ge(q_ready, 1)
                for c in range(2 * KD):
                    for k in range(KD):
                        ins = nc.tensor.matmul(ps[:, 0, c * R:c * R + g.rows], wqk[:, k, c * P:(c + 1) * P],
                                               xnT[:, k, 0:g.images, 0, :], start=(k == 0), stop=(k == KD - 1))
                ins.then_inc(qk_done, 1)

            def project_v(g):
                if isinstance(g.q, int) and g.q == 0:
                    pe.wait_ge(v_landed, 16)
                if not (isinstance(g.q, int) and g.q == 0):
                    pe.wait_ge(probT_ready, g.q)
                for i in range(g.images):
                    for k in range(KD):
                        ins = nc.tensor.matmul(ps[0:R, 2 + i // 2, (i % 2) * D:(i % 2 + 1) * D],
                                               xnT[:, k, i, :, :].rearrange("p a s -> p (a s)"), wv[:, k, :],
                                               start=(k == 0), stop=(k == KD - 1))
                ins.then_inc(v_done, 1)

            def scores(g, c):
                if c == 0:
                    pe.wait_ge(q_ready, g.q + 1)
                    pe.wait_ge(k_ready, g.q + 1)
                    pe.wait_ge(k_more_ready, g.q + 1)
                    if not (isinstance(g.q, int) and g.q == 0):
                        pe.wait_ge(sum_ready, g.q)
                for i in range(g.images):
                    ins = nc.tensor.matmul(ps[0:g.rows, 5 + c, 0:HC * S], qz[:, c, i, 0:g.rows],
                                           kz[:, c, :, S * i:S * i + S], start=(i == 0), stop=(i == g.images - 1))
                ins.then_inc(scores_done[c], 1)

            def turn_probs(g):
                for c in range(KD):
                    pe.wait_ge(prob_ready[c], g.q + 1)
                pe.wait_ge(v_ready, g.q + 1)
                for c in range(PC):
                    cols = min(PH * S, H * S - c * PH * S)
                    ins = nc.tensor.transpose(ps[0:cols, 2 + c // 3, (c % 3) * R:(c % 3) * R + g.rows],
                                              prob[0:g.rows, c * PH * S:c * PH * S + cols], ident[0:g.rows, 0:g.rows])
                ins.then_inc(prob_turned, 1)

            def context(g):
                pe.wait_ge(probT_ready, g.q + 1)
                for c in range(KD):
                    pe.wait_ge(masked[c], g.q + 1)
                for c in range(PC):
                    rows = min(PH * S, H * S - c * PH * S)
                    wide = PH * VW
                    ins = nc.tensor.matmul(
                        ps[0:g.rows, 5 + c // 3, 0:GI * 3 * wide].rearrange("p (i c w) -> p i c w", i=GI, c=3)[
                            :, 0:g.images, c % 3, :],
                        probT[0:rows, c, 0:g.rows],
                        vz[0:rows, 0:g.images, c * PH:(c + 1) * PH, :].rearrange("p i h d -> p i (h d)"),
                        start=True, stop=True)
                ins.then_inc(pv_done, 1)

            def turn_cx(g):
                pe.wait_ge(cx_ready, g.q + 1)
                if isinstance(g.q, int) and g.q == GROUPS - 1:
                    pe.wait_ge(xnT_ready, GROUPS)
                else:
                    pe.wait_ge(xnT_ready, g.q + 2)
                turn_two(g, cx[:, :, :].rearrange("p h d -> p (h d)"), cx_turned)

            def project_o(g):
                if isinstance(g.q, int) and g.q == 0:
                    pe.wait_ge(wo_landed, 16)
                pe.wait_ge(cxT_ready, g.q + 1)
                if not (isinstance(g.q, int) and g.q == 0):
                    pe.wait_ge(room_ready, g.q)
                for k in range(KD):
                    ins = nc.tensor.matmul(ps[0:g.rows, 4, 0:D], cxT[:, k, 0:g.rows], wo[:, k, :],
                                           start=(k == 0), stop=(k == KD - 1))
                ins.then_inc(wo_done, 1)

            def turn_xn2(g):
                pe.wait_ge(xn2_ready, g.q + 1)
                pe.wait_ge(cxT_ready, g.q + 1)
                turn_two(g, xs[g.u], xn2_turned)

            def route(g):
                pe.wait_ge(xn2T_ready, g.q + 1)
                pe.wait_ge(h2_ready, g.q + 1)
                for k in range(KD):
                    ins = nc.tensor.matmul(ps[0:g.rows, 4, 0:E], xn2T[:, k, 0:g.rows], rT[:, k, :],
                                           start=(k == 0), stop=(k == KD - 1))
                ins.then_inc(router_done, 1)

            def shared_up(g):
                if isinstance(g.q, int) and g.q == 0:
                    pe.wait_ge(shared_landed, 32)
                behind = GROUPS if isinstance(g.q, int) and g.q == GROUPS - 1 else g.q + 2
                pe.wait_ge(q_ready, behind)
                for j in range(2 * FC):
                    for k in range(KD):
                        ins = nc.tensor.matmul(ps[0:FP, 0, j * R:j * R + g.rows], wsgu[:, k, j * FP:(j + 1) * FP],
                                               xn2T[:, k, 0:g.rows], start=(k == 0), stop=(k == KD - 1))
                ins.then_inc(gu_done, 1)

            def shared_down(g):
                pe.wait_ge(hs_ready, g.q + 1)
                pe.wait_ge(h_ready, min(g.q + 3, GROUPS) if isinstance(g.q, int) else g.q + 3)
                for j in range(FC):
                    ins = nc.tensor.matmul(ps[0:g.rows, 7, 0:D], hs[:, j, 0:g.rows], wsd[:, j, :],
                                           start=(j == 0), stop=(j == FC - 1))
                ins.then_inc(down_done, 1)

            def places(g):
                pe.wait_ge(chosen_ready, g.q + 1)
                pe.wait_ge(earlier_ready, g.q + 1)
                pe.wait_ge(logits_ready, g.q + 1)
                nc.tensor.matmul(ps[0:g.rows, 4, 0:E], before[0:g.rows, 0:g.rows], chosen[g.u][0:g.rows, :],
                                 start=True, stop=False)
                nc.tensor.matmul(ps[0:g.rows, 4, 0:E], ones[0:R, 0:g.rows], earlier[g.u][0:R, :],
                                 start=False, stop=True).then_inc(places_done, 1)

            def turn(b, c):
                here = 2 * b + c
                known = isinstance(here, int)
                front = not known or here + 1 < GROUPS
                mid = not known or 0 <= here < GROUPS
                back = not known or 0 <= here - 1 < GROUPS
                pair = b + (c + 1) // 2
                images = 2 * GI
                if isinstance(pair, int):
                    images = min(images, IMAGES - 2 * GI * pair)
                turning = c % 2 == 1 and images > 0 and front
                if mid:
                    project_qk(Group(b, c))
                if turning:
                    turn_patches(pair, 0, images)
                if mid:
                    project_v(Group(b, c))
                if turning:
                    turn_patches(pair, 1, images)
                if back:
                    turn_cx(Group(b, c - 1))
                if mid:
                    scores(Group(b, c), 0)
                if turning:
                    turn_patches(pair, 2, images)
                if back:
                    project_o(Group(b, c - 1))
                if turning:
                    turn_patches(pair, 3, images)
                if mid:
                    scores(Group(b, c), 1)
                if front:
                    embed(Group(b, c + 1))
                if back:
                    turn_xn2(Group(b, c - 1))
                if mid:
                    turn_probs(Group(b, c))
                if back:
                    route(Group(b, c - 1))
                    shared_up(Group(b, c - 1))
                if mid:
                    context(Group(b, c))
                if front:
                    turn_xn(Group(b, c + 1))
                if back:
                    shared_down(Group(b, c - 1))
                    places(Group(b, c - 1))

            for i in range(-1, 3):
                turn(0, i)
            with pe.Fori(1, PAIRS - 2) as b:
                turn(b, 1)
                turn(b, 2)
            for i in range(GROUPS - 3, GROUPS + 1):
                turn(0, i)

            pe.wait_ge(res_ready, GROUPS)
            pe.wait_ge(room_ready, GROUPS)

            def turn_rows(e, c, lap):
                pe.wait_ge(row_landed[c], 16 * (lap + 1))
                if not isinstance(e, int) or e >= 2:
                    pe.wait_ge(xT_ready, e - 1)
                for k in range(KD):
                    ins = nc.tensor.transpose(ps[:, 2 + c % 2, k * P:(k + 1) * P], xrow[c][:, k:D:KD], ident[:, :])
                ins.then_inc(row_turned, 1)

            def gate_up(e, c, slot):
                u = c % 2
                pe.wait_ge(xT_ready, e + 1)
                pe.wait_ge(ew_landed[c // 2 % 2], 12 * (e - c % 4) + 48)
                if not isinstance(e, int) or e >= 2:
                    pe.wait_ge(hh_ready, e - 1)
                w = ew[:, slot, 0:2 * KD * F].rearrange("p (m k f) -> p m k f", m=2, k=KD)
                for k in range(KD):
                    ins = nc.tensor.matmul(ps[:, u, 0:2 * F], xT[u][:, k, :], w[:, :, k, :],
                                           start=(k == 0), stop=(k == KD - 1))
                ins.then_inc(e_gu_done, 1)

            def turn_hidden(e, u):
                pe.wait_ge(hh_ready, e + 1)
                if not isinstance(e, int) or e >= 2:
                    pe.wait_ge(hT_ready, e - 1)
                for k in range(FC):
                    ins = nc.tensor.transpose(ps[0:FP, 4 + u, k * P:(k + 1) * P], hh[u][:, k:F:FC], ident[:, :])
                ins.then_inc(hh_turned, 1)

            def down(e, u, slot):
                pe.wait_ge(hT_ready, e + 1)
                if not isinstance(e, int) or e >= 2:
                    pe.wait_ge(ysc_ready, e - 1)
                for k in range(FC):
                    ins = nc.tensor.matmul(ps[:, 6 + u, 0:D], hT[u][:, k, :],
                                           ew[0:FP, slot, 2 * KD * F + k * D:2 * KD * F + (k + 1) * D],
                                           start=(k == 0), stop=(k == FC - 1))
                ins.then_inc(e_down_done, 1)

            def experts(m, first=False, last=False):
                for c in range(8):
                    e = 8 * m + c
                    gate_up(e, c, e % RING)
                    if not (last and c == 7):
                        turn_rows(e + 1, (c + 1) % 8, m + (c + 1) // 8)
                    if not (first and c == 0):
                        down(e - 1, (c - 1) % 2, (e - 1) % RING)
                    turn_hidden(e, c % 2)

            turn_rows(0, 0, 0)
            experts(0, first=True)
            with pe.Fori(1, E // 8 - 1) as m:
                experts(m)
            experts(E // 8 - 1, last=True)
            down(E - 1, 1, (E - 1) % RING)

        @block.vector
        def _(dve):
            V = nc.vector
            V.memset(qz[:, :, :, :], 0.0).then_inc(zeros_made, 1)
            V.memset(vz[:, :, :, :], 0.0).then_inc(zeros_made, 1)
            V.memset(pT[:, :, :], 0.0).then_inc(zeros_made, 1)
            V.memset(earlier[0][:, :], 0.0).then_inc(earlier_ready, 1)
            dve.wait_ge(consts_made, CONSTS)
            dve.wait_ge(zeros_made, 3)
            for i in range(GI):
                V.tensor_copy(vz[:, i, :, HD], third[0:R, :, :].rearrange("p c r -> p (c r)")).then_inc(masks_made, 1)
            V.tensor_scalar(causal[:, :], tri[:, 0, :], third[:, 0, 0:1], None, ALU.mult).then_inc(dve_const, 1)
            for i in range(1, GI):
                dve.wait_ge(dve_const, i)
                V.scalar_tensor_tensor(out=causal[:, :], in0=tri[:, i, :], scalar=third[:, 0, i:i + 1],
                                       in1=causal[:, :], op0=ALU.mult, op1=ALU.add).then_inc(dve_const, 1)
            dve.wait_ge(pos_landed, 16 * 3 * GI)
            V.tensor_tensor(posb[0:R, :], posb[0:R, :], posadd[0:R, :], ALU.add).then_inc(masks_made, 1)
            dve.wait_ge(masks_made, 4)
            dve.wait_ge(dve_const, GI)

            def at(g, t):
                return t[0:g.rows]

            def constant_wait():
                dve.wait_ge(consts_made, CONSTS)

            def norm(g, src, st, mv, ve, stats, mean, var):
                V.bn_stats(st[0:g.rows, :], src).then_inc(stats, 1)
                constant_wait()
                dve.wait_ge(stats, g.q + 1)
                V.bn_aggr(mv[0:g.rows, :], st[0:g.rows, :]).then_inc(mean, 1)
                dve.wait_ge(mean, g.q + 1)
                V.tensor_scalar(ve[0:g.rows, :], mv[0:g.rows, 1:2], EPS, None, ALU.add).then_inc(var, 1)

            def tokens(g):
                r = g.rows
                dve.wait_ge(embedded, g.q + 1)
                if not (isinstance(g.q, int) and g.q < 2):
                    dve.wait_ge(hb_ready, g.q - 1)
                V.tensor_tensor(h[g.u][0:r, :], ps[0:r, 7, 0:D], posb[0:r, :], ALU.add).then_inc(h_ready, 1)
                dve.wait_ge(h_ready, g.q + 1)
                norm(g, h[g.u][0:r, :], st1, mv1, ve1, ln1_stats, ln1_mean, ln1_var)

            def normed(g):
                r = g.rows
                dve.wait_ge(ln1_rstd, g.q + 1)
                if not (isinstance(g.q, int) and g.q == 0):
                    dve.wait_ge(xn_turned, g.q)
                V.tensor_scalar(xn[0:r, :], h[g.u][0:r, :], mv1[0:r, 0:1], rs1[0:r, 0:1], ALU.subtract,
                                ALU.mult).then_inc(xn_ready, 1)

            def copy_v(g):
                n = g.images
                dve.wait_ge(v_done, g.q + 1)
                if not (isinstance(g.q, int) and g.q == 0):
                    dve.wait_ge(pv_done, g.q)
                src = ps[0:R, 2:4, :].rearrange("p a b -> p (a b)")[:, 0:n * D].rearrange("p (i h d) -> p i h d", i=n, h=H)
                for i in range(n):
                    ins = V.tensor_tensor(vz[:, i, 0:H, 0:HD], src[:, i],
                                          third[0:R, :, :].rearrange("p c r -> p (c r)")[:, 0:H].unsqueeze(2).broadcast_to([R, H, HD]),
                                          ALU.mult)
                ins.then_inc(v_ready, 1)

            def more_keys(g):
                dve.wait_ge(qk_done, g.q + 1)
                if not (isinstance(g.q, int) and g.q == 0):
                    dve.wait_ge(k_ready, g.q)
                k = ps[:, 0, KD * R:2 * KD * R].rearrange("p (k r) -> p k r", k=KD)
                V.tensor_copy(keys[:, :, 0:g.rows], k[:, :, 0:g.rows]).then_inc(keys_ready, 1)
                dve.wait_ge(keys_ready, g.q + 1)
                if not (isinstance(g.q, int) and g.q == 0):
                    dve.wait_ge(scores_done[1], g.q)
                for hd in range(HA, HC):
                    ins = V.tensor_scalar(kz[:, :, hd, 0:g.rows], keys[:, :, 0:g.rows], headmask[:, hd:hd + 1], None, ALU.mult)
                ins.then_inc(k_more_ready, 1)

            def softmax(g, c):
                r = g.rows
                hs_c = slice(c * HC, (c + 1) * HC)
                dve.wait_ge(scores_done[c], g.q + 1)
                V.tensor_tensor(sm[0:r, hs_c, :], ps[0:r, 5 + c, 0:HC * S].rearrange("p (h s) -> p h s", h=HC),
                                causal[0:r, :].unsqueeze(1).broadcast_to([r, HC, S]), ALU.add).then_inc(masked[c], 1)
                dve.wait_ge(masked[c], g.q + 1)
                V.tensor_reduce(mx[0:r, hs_c], sm[0:r, hs_c, :], AX, ALU.max).then_inc(max_ready[c], 1)
                dve.wait_ge(max_ready[c], g.q + 1)
                if not (isinstance(g.q, int) and g.q == 0):
                    dve.wait_ge(prob_ready[c], g.q)
                V.tensor_tensor(sx[0:r, hs_c, :], sm[0:r, hs_c, :], mx[0:r, hs_c].unsqueeze(2).broadcast_to([r, HC, S]),
                                ALU.subtract).then_inc(lowered[c], 1)

            def gather_context(g):
                r = g.rows
                dve.wait_ge(pv_done, g.q + 1)
                wide = PH * VW
                o = ps[0:r, 5:7, 0:3 * GI * wide].rearrange("p a (i w) -> p a i w", i=GI)
                s4 = ctxsum[0:r, :, :].rearrange("p (a w) d -> p a (w d)", a=2)
                V.tensor_scalar(s4, o[:, :, 0, :], third[0:r, 0, 0:1], None, ALU.mult).then_inc(sum_a, 1)
                for i in range(1, g.images):
                    dve.wait_ge((sum_a, sum_b)[i - 1], g.q + 1)
                    V.scalar_tensor_tensor(out=s4, in0=o[:, :, i, :], scalar=third[0:r, 0, i:i + 1], in1=s4,
                                           op0=ALU.mult, op1=ALU.add).then_inc((sum_b, sum_ready)[i - 1], 1)
                if g.images == 1:
                    dve.wait_ge(sum_a, g.q + 1)
                    V.tensor_copy(rden[0:r, 0:1], ctxsum[0:r, 0:1, 0]).then_inc(sum_ready, 1)
                dve.wait_ge(sum_ready, g.q + 1)
                V.reciprocal(rden[0:r, :], ctxsum[0:r, 0:H, HD]).then_inc(rden_ready, 1)
                dve.wait_ge(rden_ready, g.q + 1)
                if not (isinstance(g.q, int) and g.q == 0):
                    dve.wait_ge(cx_turned, g.q)
                V.tensor_tensor(cx[0:r, :, :], ctxsum[0:r, 0:H, 0:HD], rden[0:r, :].unsqueeze(2).broadcast_to([r, H, HD]),
                                ALU.mult).then_inc(cx_ready, 1)

            def residual(g):
                r = g.rows
                dve.wait_ge(wo_done, g.q + 1)
                dve.wait_ge(hb_ready, g.q + 1)
                V.tensor_tensor(h2[g.u][0:r, :], ps[0:r, 4, 0:D], hb[g.u][0:r, :], ALU.add).then_inc(h2_ready, 1)
                dve.wait_ge(h2_ready, g.q + 1)
                norm(g, h2[g.u][0:r, :], st2, mv2, ve2, ln2_stats, ln2_mean, ln2_var)

            def normed_two(g):
                r = g.rows
                if not (isinstance(g.q, int) and g.q < 2):
                    dve.wait_ge(scattered[g.u], 16 * TOPK * g.pair)
                V.tensor_scalar(number[g.u][:, :], number[g.u][:, :], 2.0 * R, None, ALU.add).then_inc(number_ready, 1)
                if not (isinstance(g.q, int) and g.q < 2):
                    dve.wait_ge(row_stored[g.u], 16 * g.pair)
                dve.wait_ge(ln2_rstd, g.q + 1)
                V.tensor_scalar(xs[g.u][0:r, 0:D], h2[g.u][0:r, :], mv2[0:r, 0:1], rs2[0:r, 0:1], ALU.subtract,
                                ALU.mult).then_inc(xn2_ready, 1)

            def choose(g):
                r = g.rows
                dve.wait_ge(router_done, g.q + 1)
                V.tensor_copy(lg[0:r, :], ps[0:r, 4, 0:E]).then_inc(logits_ready, 1)
                constant_wait()
                dve.wait_ge(logits_ready, g.q + 1)
                V.max(top[0:r, :], lg[0:r, :]).then_inc(top_ready, 1)
                constant_wait()
                dve.wait_ge(top_ready, g.q + 1)
                V.match_replace(cut[0:r, :], top[0:r, :], lg[0:r, :], NEG).then_inc(cut_ready, 1)
                if not (isinstance(g.q, int) and g.q == 0):
                    dve.wait_ge(ex_ready, g.q)
                V.tensor_scalar(shifted[0:r, :], lg[0:r, :], top[0:r, 0:1], None, ALU.subtract).then_inc(shifted_ready, 1)
                dve.wait_ge(cut_ready, g.q + 1)
                V.tensor_tensor(chosen[g.u][0:r, :], lg[0:r, :], cut[0:r, :], ALU.not_equal).then_inc(chosen_ready, 1)
                dve.wait_ge(chosen_ready, g.q + 1)
                if not (isinstance(g.q, int) and g.q == GROUPS - 1):
                    if not (isinstance(g.q, int) and g.q == 0):
                        dve.wait_ge(places_done, g.q)
                    V.tensor_tensor(earlier[1 - g.u][0:R, :], earlier[g.u][0:R, :], chosen[g.u][0:R, :],
                                    ALU.add).then_inc(earlier_ready, 1)

            def weigh(g):
                r = g.rows
                dve.wait_ge(ex_ready, g.q + 1)
                V.tensor_tensor_reduce(em[0:r, :], ex[0:r, :], chosen[g.u][0:r, :], 1.0, 0.0, ALU.mult, ALU.add,
                                       wsum[0:r, :]).then_inc(em_ready, 1)
                dve.wait_ge(em_ready, g.q + 1)
                V.reciprocal(wrec[0:r, :], wsum[0:r, :]).then_inc(wrec_ready, 1)
                dve.wait_ge(wrec_ready, g.q + 1)
                V.tensor_scalar(xs[g.u][0:r, D:D + E], em[0:r, :], wrec[0:r, 0:1], None, ALU.mult).then_inc(row_ready, 1)

            def place(g):
                r = g.rows
                dve.wait_ge(places_done, g.q + 1)
                V.scalar_tensor_tensor(out=room[0:r, :], in0=ps[0:r, 4, 0:E], scalar=float(-E), in1=base[0:r, :],
                                       op0=ALU.mult, op1=ALU.add)
                V.scalar_tensor_tensor(out=fits[0:r, :], in0=ps[0:r, 4, 0:E], scalar=float(CAP),
                                       in1=chosen[g.u][0:r, :], op0=ALU.is_lt, op1=ALU.mult).then_inc(room_ready, 1)
                dve.wait_ge(room_ready, g.q + 1)
                V.tensor_tensor(code[0:r, :], room[0:r, :], fits[0:r, :], ALU.mult).then_inc(code_ready, 1)
                constant_wait()
                dve.wait_ge(code_ready, g.q + 1)
                V.max(top2[0:r, :], code[0:r, :]).then_inc(top2_ready, 1)
                dve.wait_ge(top2_ready, g.q + 1)
                V.tensor_scalar(idx[g.u][0:r, :], top2[0:r, :], -1.0, float(SLOTS), ALU.mult, ALU.add).then_inc(idx_ready, 1)

            def shared_gate(g):
                r = g.rows
                gu = ps[0:FP, 0, 0:4 * R].rearrange("p (k r) -> p k r", k=4)
                dve.wait_ge(tanh_ready, g.q + 1)
                V.scalar_tensor_tensor(out=g1[:, :, 0:r], in0=th[:, :, 0:r], scalar=1.0, in1=gu[:, 0:2, 0:r],
                                       op0=ALU.add, op1=ALU.mult).then_inc(g1_ready, 1)
                dve.wait_ge(g1_ready, g.q + 1)
                if not (isinstance(g.q, int) and g.q == 0):
                    dve.wait_ge(down_done, g.q)
                V.scalar_tensor_tensor(out=hs[:, :, 0:r], in0=g1[:, :, 0:r], scalar=0.5, in1=gu[:, 2:4, 0:r],
                                       op0=ALU.mult, op1=ALU.mult).then_inc(hs_ready, 1)

            def shared_add(g):
                r = g.rows
                dve.wait_ge(down_done, g.q + 1)
                if not (isinstance(g.q, int) and g.q < 2):
                    dve.wait_ge(res_stored[g.u], 16 * g.pair)
                V.tensor_tensor(res[g.u][0:r, :], ps[0:r, 7, 0:D], h2[g.u][0:r, :], ALU.add).then_inc(res_ready, 1)

            def turn(b, c):
                here = 2 * b + c
                known = isinstance(here, int)
                front = not known or here + 1 < GROUPS
                mid = not known or 0 <= here < GROUPS
                back = not known or 0 <= here - 1 < GROUPS
                if mid:
                    more_keys(Group(b, c))
                if not known or 0 <= here - 2 < GROUPS:
                    place(Group(b, c - 2))
                if mid:
                    copy_v(Group(b, c))
                    softmax(Group(b, c), 0)
                if back:
                    residual(Group(b, c - 1))
                if mid:
                    softmax(Group(b, c), 1)
                if back:
                    normed_two(Group(b, c - 1))
                if front:
                    tokens(Group(b, c + 1))
                if back:
                    choose(Group(b, c - 1))
                if front:
                    normed(Group(b, c + 1))
                if back:
                    shared_gate(Group(b, c - 1))
                    weigh(Group(b, c - 1))
                if mid:
                    gather_context(Group(b, c))
                if back:
                    shared_add(Group(b, c - 1))

            for i in range(-1, 3):
                turn(0, i)
            with dve.Fori(1, PAIRS - 2) as b:
                turn(b, 1)
                turn(b, 2)
            for i in range(GROUPS - 3, GROUPS + 2):
                turn(0, i)

            def hidden(e, u):
                dve.wait_ge(silu_ready, e + 1)
                if not isinstance(e, int) or e >= 2:
                    dve.wait_ge(hh_turned, e - 1)
                V.tensor_tensor(hh[u][:, :], sg[u][:, :], ps[:, u, F:2 * F], ALU.mult).then_inc(hh_ready, 1)

            def weighed(e, u, c):
                dve.wait_ge(e_down_done, e + 1)
                if not isinstance(e, int) or e >= 4:
                    dve.wait_ge(added[u], 8 * (e - u) - 16)
                V.tensor_scalar(ysc[c % 4][:, :], ps[:, 6 + u, 0:D], xrow[c][:, bass.ds(D + e, 1)], None,
                                ALU.mult).then_inc(ysc_ready, 1)

            def experts(m, first=False):
                for c in range(8):
                    e = 8 * m + c
                    hidden(e, c % 2)
                    if not (first and c == 0):
                        weighed(e - 1, (c - 1) % 2, (c - 1) % 8)

            experts(0, first=True)
            with dve.Fori(1, E // 8) as m:
                experts(m)
            weighed(E - 1, 1, 7)
            for n in range(len(OUT_PARTS)):
                dve.wait_ge(sums_landed[n], 32)
                V.tensor_tensor(out_tile(0, n), out_tile(0, n), out_tile(1, n), ALU.add).then_inc(out_ready, 1)


_INS = ['x', 'L0_tok_W', 'L0_tok_b', 'L0_tok_cls_token', 'L0_tok_pos_embedding', 'L0_attn_Wq', 'L0_attn_Wk',
        'L0_attn_Wv', 'L0_attn_Wo', 'L0_attn_bo', 'L0_ffn_router_w', 'L0_ffn_w_gate', 'L0_ffn_w_up',
        'L0_ffn_w_down', 'L0_ffn_ws_gate_up', 'L0_ffn_ws_down']
_OUTS = [((IMAGES, S, D), 'float32')]


def kernel(**inputs):
    import numpy as _np
    import concourse.bacc as _bacc
    from concourse import mybir as _mybir
    from concourse.bass_utils import run_bass_kernel_spmd as _run

    nc = _bacc.Bacc("TRN2", target_bir_lowering=False, num_devices=1)
    arrays, args = {}, []
    for name in _INS:
        a = _np.ascontiguousarray(inputs[name])
        arrays[f"in_{name}_dram"] = a
        args.append(nc.dram_tensor(f"in_{name}_dram", a.shape, _mybir.dt.from_np(a.dtype), kind="ExternalInput").ap())
    for i, (shape, dtype) in enumerate(_OUTS):
        dt = _mybir.dt.from_np(_np.dtype(dtype))
        args.append(nc.dram_tensor(f"out_{i}_dram", shape, dt, kind="ExternalOutput").ap())
    vit_kernel(nc, *args)
    r = _run(nc, [arrays], core_ids=[0])
    got = tuple(r.results[0][f"out_{i}_dram"] for i in range(len(_OUTS)))
    return got[0]
```

```python
from contextlib import ExitStack

import numpy as np

import concourse.bass as bass
from concourse import mybir

F32 = mybir.dt.float32
F32R = mybir.dt.float32r
BF16 = mybir.dt.bfloat16
U32 = mybir.dt.uint32
I32 = mybir.dt.int32
ALU = mybir.AluOpType
ACT = mybir.ActivationFunctionType
AX = mybir.AxisListType.X

P = 128
BANK = 512
IMAGES, CH, SIDE, PATCH = 64, 3, 96, 16
PS = SIDE // PATCH
NP = PS * PS
S = NP + 1
D = 256
KD = D // P
H, HD = 16, 16
GI = 3
R = GI * S
GROUPS = -(-IMAGES // GI)
T = IMAGES * S
HC = H // KD
HA = 2
PH = 3
PC = -(-H // PH)
VW = HD + 1
E, TOPK, F, CAP = 64, 8, 192, 128
FC, FP = 2, F // 2
SLOTS = E * CAP
ROW = D + E
NEG = -1e30
EPS = 1e-5
PAIR_ROWS = 2 * GI * CH * PS
PT_C = 2 * GI * S
HALF = 2
XCH = CH * HALF
RING = 20
EW = 2 * KD * F + FC * D
LATE = 8


class Group:

    def __init__(self, b, c):
        self.q = 2 * b + c
        self.u = c % 2
        self.pair = b + c // 2
        last = isinstance(self.q, int) and self.q == GROUPS - 1
        self.images = IMAGES - GI * (GROUPS - 1) if last else GI
        self.rows = self.images * S


def vit_kernel(nc, x, W, b, cls, pos, Wq, Wk, Wv, Wo, bo, router_w, w_gate, w_up, w_down, ws_gate_up, ws_down, out):
    ctx = ExitStack()
    with ctx:
        def sb(name, shape, dt=F32):
            return ctx.enter_context(nc.sbuf_tensor(name, shape, dt))

        def sem(name):
            return ctx.enter_context(nc.semaphore(name))

        slots = nc.dram_tensor("slots", [SLOTS, 1], I32, kind="Internal").ap()
        table = nc.dram_tensor("table", [T + P, ROW], F32, kind="Internal").ap()
        acc = [out.rearrange("n s d -> (n s) d"), nc.dram_tensor("acc", [T, D], F32, kind="Internal").ap()]

        ident = sb("ident", [P, P])
        before = sb("before", [P, R], BF16)
        ones = sb("ones", [P, R], BF16)
        headmask = sb("headmask", [P, HC])
        third = sb("third", [P, PC, PH])
        tri = sb("tri", [P, GI, S])
        causal = sb("causal", [P, S])
        posb = sb("posb", [P, D])
        posadd = sb("posadd", [P, D])
        bo_sb = sb("bo_sb", [P, D])
        base = sb("base", [P, E])
        halfneg = sb("halfneg", [P, 1])
        zero = sb("zero", [P, ROW])
        silu_warm = sb("silu_warm", [P, 1])
        nobody = sb("nobody", [P, E], I32)
        wraw = sb("wraw", [P, KD, CH * PATCH * PATCH])
        rraw = sb("rraw", [E, D])
        wT_hi, wT_lo = (sb(f"wT_{part}", [P, XCH, D], F32R) for part in ("hi", "lo"))
        wqk = sb("wqk", [P, KD, 2 * D])
        wv = sb("wv", [P, KD, D])
        wo = sb("wo", [P, KD, D])
        rT = sb("rT", [P, KD, E])
        wsgu = sb("wsgu", [P, KD, 2 * F])
        wsd = sb("wsd", [FP, FC, D])
        ew = sb("ew", [P, RING, EW])
        taken = [0]

        def late(parts, *dims):
            size = int(np.prod(dims))
            lo = taken[0]
            taken[0] += size
            assert taken[0] <= LATE * EW
            flat = ew[0:parts, RING - LATE:RING, :].rearrange("p a b -> p (a b)")[:, lo:lo + size]
            if len(dims) == 1:
                return flat
            names = "abcd"[:len(dims)]
            return flat.rearrange("p (" + " ".join(names) + ") -> p " + " ".join(names), **dict(zip(names, dims)))

        xraw = late(PAIR_ROWS, PATCH * SIDE)
        xw = late(PAIR_ROWS, PS, PATCH * PATCH)
        pT = sb("pT", [P, XCH, PT_C])
        pT_hi, pT_lo = (sb(f"pT_{part}", [P, XCH, PT_C], F32R) for part in ("hi", "lo"))
        h = [sb(f"h{u}", [P, D]) for u in range(2)]
        hb = [sb(f"hb{u}", [P, D]) for u in range(2)]
        st1 = sb("st1", [P, 6])
        mv1 = sb("mv1", [P, 2])
        ve1 = sb("ve1", [P, 1])
        rs1 = sb("rs1", [P, 1])
        xn = sb("xn", [P, D])
        xnT = late(P, KD, R)
        vT = late(P, KD, GI, PH, S)
        qz = late(P, KD, GI, R)
        keys = sb("keys", [P, KD, R])
        kz = late(P, KD, HC, R)
        vz = late(R, GI, PC * PH, VW)
        sm = late(P, H, S)
        mx = sb("mx", [P, H])
        sx = late(P, H, S)
        prob = late(P, H * S)
        probT = late(P, PC, R)
        ctxsum = late(P, PC * PH, VW)
        rden = sb("rden", [P, H])
        cx = sb("cx", [P, H, HD])
        cxT = sb("cxT", [P, KD, R])
        h2 = [sb(f"h2{u}", [P, D]) for u in range(2)]
        st2 = sb("st2", [P, 6])
        mv2 = sb("mv2", [P, 2])
        ve2 = sb("ve2", [P, 1])
        rs2 = sb("rs2", [P, 1])
        xs = [sb(f"xs{u}", [P, ROW]) for u in range(2)]
        xn2T = sb("xn2T", [P, KD, R])
        number = [sb(f"number{u}", [P, 1], I32) for u in range(2)]
        lg = sb("lg", [P, E])
        top = sb("top", [P, TOPK])
        cut = sb("cut", [P, E])
        shifted = sb("shifted", [P, E])
        chosen = [sb(f"chosen{u}", [P, E], BF16) for u in range(2)]
        earlier = [sb(f"earlier{u}", [P, E], BF16) for u in range(2)]
        ex = sb("ex", [P, E])
        em = sb("em", [P, E])
        wsum = sb("wsum", [P, 1])
        wrec = sb("wrec", [P, 1])
        room = sb("room", [P, E])
        fits = sb("fits", [P, E])
        code = sb("code", [P, E])
        top2 = sb("top2", [P, TOPK])
        idx = [sb(f"idx{u}", [P, TOPK], U32) for u in range(2)]
        th = sb("th", [FP, FC, R])
        g1 = sb("g1", [FP, FC, R])
        hs = sb("hs", [FP, FC, R])
        res = [sb(f"res{u}", [P, D]) for u in range(2)]
        slot_tok = sb("slot_tok", [P, E], I32)
        tok = [sb(f"tok{c}", [P, 1], I32) for c in range(16)]
        xrow = [sb(f"xrow{c}", [P, ROW]) for c in range(8)]
        GU = 2 * KD * F
        w_hi, w_lo = ([sb(f"w_{part}{u}", [P, GU], F32R) for u in range(2)] for part in ("hi", "lo"))
        x_hi, x_lo = ([sb(f"x_{part}{u}", [P, KD * P], F32R) for u in range(2)] for part in ("hi", "lo"))
        sg = [sb(f"sg{u}", [P, F]) for u in range(2)]
        hh = [sb(f"hh{u}", [P, F]) for u in range(2)]
        hT = [sb(f"hT{u}", [FP, FC, P]) for u in range(2)]
        ysc = [pT[:, :, :].rearrange("p a b -> p (a b)")[:, c * D:(c + 1) * D] for c in range(4)]

        ps = ctx.enter_context(nc.psum_tensor("ps", [P, 8, BANK], F32))

        x_landed = sem("x_landed")
        x_sorted = sem("x_sorted")
        w_landed = sem("w_landed")
        router_landed = sem("router_landed")
        pos_landed = sem("pos_landed")
        qk_landed = sem("qk_landed")
        v_landed = sem("v_landed")
        bo_landed = sem("bo_landed")
        wo_landed = sem("wo_landed")
        shared_landed = sem("shared_landed")
        consts_made = sem("consts_made")
        zeros_made = sem("zeros_made")
        masks_made = sem("masks_made")
        posb_made = sem("posb_made")
        dve_const = sem("dve_const")
        slots_cleared = sem("slots_cleared")
        rows_cleared = sem("rows_cleared")
        wT_turned = sem("wT_turned")
        wT_copied = sem("wT_copied")
        wT_low = sem("wT_low")
        patches_turned = sem("patches_turned")
        patches_copied = sem("patches_copied")
        pT_hi_ready = sem("pT_hi_ready")
        pT_lo_ready = sem("pT_lo_ready")
        embedded = sem("embedded")
        h_ready = sem("h_ready")
        hb_ready = sem("hb_ready")
        ln1_stats = sem("ln1_stats")
        ln1_mean = sem("ln1_mean")
        ln1_var = sem("ln1_var")
        ln1_rstd = sem("ln1_rstd")
        xn_ready = sem("xn_ready")
        xn_turned = sem("xn_turned")
        xnT_ready = sem("xnT_ready")
        qk_done = sem("qk_done")
        q_ready = sem("q_ready")
        keys_ready = sem("keys_ready")
        k_ready = sem("k_ready")
        k_more_ready = sem("k_more_ready")
        vT_done = sem("vT_done")
        vT_ready = sem("vT_ready")
        v_turned = sem("v_turned")
        v_ready = sem("v_ready")
        scores_done = [sem(f"scores_done{c}") for c in range(KD)]
        masked = [sem(f"masked{c}") for c in range(KD)]
        max_ready = [sem(f"max_ready{c}") for c in range(KD)]
        lowered = [sem(f"lowered{c}") for c in range(KD)]
        prob_ready = [sem(f"prob_ready{c}") for c in range(KD)]
        prob_turned = sem("prob_turned")
        probT_ready = sem("probT_ready")
        pv_done = sem("pv_done")
        sum_a = sem("sum_a")
        sum_b = sem("sum_b")
        sum_ready = sem("sum_ready")
        rden_ready = sem("rden_ready")
        cx_ready = sem("cx_ready")
        cx_turned = sem("cx_turned")
        cxT_ready = sem("cxT_ready")
        wo_done = sem("wo_done")
        h2_ready = sem("h2_ready")
        ln2_stats = sem("ln2_stats")
        ln2_mean = sem("ln2_mean")
        ln2_var = sem("ln2_var")
        ln2_rstd = sem("ln2_rstd")
        xn2_ready = sem("xn2_ready")
        xn2_turned = sem("xn2_turned")
        xn2T_ready = sem("xn2T_ready")
        router_done = sem("router_done")
        logits_ready = sem("logits_ready")
        top_ready = sem("top_ready")
        cut_ready = sem("cut_ready")
        chosen_ready = sem("chosen_ready")
        shifted_ready = sem("shifted_ready")
        ex_ready = sem("ex_ready")
        em_ready = sem("em_ready")
        wrec_ready = sem("wrec_ready")
        row_ready = sem("row_ready")
        number_ready = sem("number_ready")
        earlier_ready = sem("earlier_ready")
        places_done = sem("places_done")
        room_ready = sem("room_ready")
        fits_ready = sem("fits_ready")
        code_ready = sem("code_ready")
        top2_ready = sem("top2_ready")
        idx_ready = sem("idx_ready")
        scattered = [sem(f"scattered{u}") for u in range(2)]
        gu_done = sem("gu_done")
        tanh_ready = sem("tanh_ready")
        g1_ready = sem("g1_ready")
        hs_ready = sem("hs_ready")
        down_done = sem("down_done")
        res_ready = sem("res_ready")
        res_stored = [sem(f"res_stored{u}") for u in range(2)]
        row_stored = [sem(f"row_stored{u}") for u in range(2)]
        slot_tok_landed = sem("slot_tok_landed")
        ew_landed = [sem(f"ew_landed{u}") for u in range(2)]
        row_landed = [sem(f"row_landed{c}") for c in range(8)]
        row_turned = sem("row_turned")
        x_hi_ready = sem("x_hi_ready")
        x_lo_ready = sem("x_lo_ready")
        w_hi_ready = sem("w_hi_ready")
        w_lo_ready = sem("w_lo_ready")
        e_gu_done = sem("e_gu_done")
        silu_ready = sem("silu_ready")
        hh_ready = sem("hh_ready")
        hh_turned = sem("hh_turned")
        hT_ready = sem("hT_ready")
        e_down_done = sem("e_down_done")
        ysc_ready = sem("ysc_ready")
        added = [sem(f"added{u}") for u in range(2)]
        tok_ready = sem("tok_ready")
        out_stored = sem("out_stored")

        block = ctx.enter_context(nc.Block())

        CONSTS = 19
        PAIRS = GROUPS // 2
        EPAIRS = E // 2

        def x_pair(pair, images):
            rows = images * CH * PS
            src = x.rearrange("n c (r i) w -> (n c r) (i w)", i=PATCH)
            return xraw[0:rows, :], src[bass.ds(pair * PAIR_ROWS, rows), :]

        @block.sync
        def _(sp):
            sp.dma_start(*x_pair(0, 2 * GI)).then_inc(x_landed, 16)
            sp.dma_start(wraw[:, :, :], W.rearrange("(k p) d -> p k d", p=P)).then_inc(w_landed, 16)
            sp.dma_start(rraw[:, :], router_w).then_inc(router_landed, 16)
            for i in range(GI):
                sp.dma_start(posb[S * i:S * i + S, :], pos[0, :, :]).then_inc(pos_landed, 16)
                sp.dma_start(posadd[S * i:S * i + 1, :], cls[0, :, :]).then_inc(pos_landed, 16)
                sp.dma_start(posadd[S * i + 1:S * i + S, :],
                             b.rearrange("(o d) -> o d", o=1).broadcast_to([NP, D])).then_inc(pos_landed, 16)
            sp.dma_start(wqk[:, :, 0:D], Wq.rearrange("(k p) n -> p k n", p=P)).then_inc(qk_landed, 16)
            sp.dma_start(wqk[:, :, D:2 * D], Wk.rearrange("(k p) n -> p k n", p=P)).then_inc(qk_landed, 16)
            sp.dma_start(wv[:, :, :], Wv.rearrange("(k p) n -> p k n", p=P)).then_inc(v_landed, 16)
            sp.dma_start(bo_sb[0:R, :], bo.rearrange("(o d) -> o d", o=1).broadcast_to([R, D])).then_inc(bo_landed, 16)
            sp.dma_start(wo[:, :, :], Wo.rearrange("(k p) n -> p k n", p=P)).then_inc(wo_landed, 16)
            sp.dma_start(wsgu[:, :, :], ws_gate_up.rearrange("(k p) n -> p k n", p=P)).then_inc(shared_landed, 16)
            sp.dma_start(wsd[:, :, :], ws_down.rearrange("(k p) n -> p k n", p=FP)).then_inc(shared_landed, 16)
            sp.wait_ge(consts_made, CONSTS)
            sp.dma_start(slots.rearrange("(p e) o -> p (e o)", p=P), nobody[:, :]).then_inc(slots_cleared, 16)
            sp.dma_start(table[T:T + P, :], zero[:, :]).then_inc(rows_cleared, 16)

            def load_x(pair, images=2 * GI):
                sp.wait_ge(x_sorted, pair)
                sp.dma_start(*x_pair(pair, images)).then_inc(x_landed, 16)

            def load_experts(pair, u, slot):
                ring = ew[:, bass.ds(slot, 2), :]
                for w, at, parts, wide in ((w_gate, 0, P, KD * F), (w_up, KD * F, P, KD * F),
                                           (w_down, 2 * KD * F, FP, FC * D)):
                    sp.dma_start(ring[0:parts, :, at:at + wide],
                                 w.rearrange("e (p k) f -> p e (k f)", p=parts)[:, bass.ds(2 * pair, 2), :]
                                 ).then_inc(ew_landed[u], 16)

            def store_rows(g):
                sp.wait_ge(row_ready, g.q + 1)
                sp.dma_start(table[bass.ds(g.q * R, g.rows), :], xs[g.u][0:g.rows, :]).then_inc(row_stored[g.u], 16)
                sp.wait_ge(res_ready, g.q + 1)
                sp.dma_start(acc[0][bass.ds(g.q * R, g.rows), :], res[g.u][0:g.rows, :]).then_inc(res_stored[g.u], 16)

            load_experts(0, 0, 0)
            load_x(1)
            sp.dma_start(acc[1].rearrange("(a p) c -> p a c", p=IMAGES),
                         zero[0:IMAGES, 0:D].unsqueeze(1).broadcast_to([IMAGES, S, D])).then_inc(rows_cleared, 16)
            load_experts(1, 1, 2)
            EARLY = (RING - LATE) // 4
            load_x(2)
            sp.wait_ge(ew_landed[0], 48)
            load_experts(2, 0, 4)
            store_rows(Group(0, 0))
            load_x(3)
            sp.wait_ge(ew_landed[1], 48)
            load_experts(3, 1, 6)
            store_rows(Group(0, 1))
            store_rows(Group(0, 2))
            with sp.Fori(2, EARLY) as j:
                for u in range(2):
                    pair = 2 * j + u
                    load_x(pair)
                    sp.wait_ge(ew_landed[u], 48 * j)
                    load_experts(pair, u, 2 * pair)
                    store_rows(Group(pair, -5))
                    store_rows(Group(pair, -4))
            with sp.Fori(EARLY, PAIRS // 2) as j:
                for u in range(2):
                    pair = 2 * j + u
                    load_x(pair)
                    store_rows(Group(pair, -5))
                    store_rows(Group(pair, -4))
            load_x(PAIRS - 1, IMAGES - 2 * GI * (PAIRS - 1))
            for q in range(2 * PAIRS - 7, GROUPS - 4):
                store_rows(Group(0, q))

            def load_late(pairs):
                for pair in pairs:
                    sp.wait_ge(ew_landed[pair % 2], 48 * (pair // 2))
                    load_experts(pair, pair % 2, 2 * pair)

            LATE_PAIR = (RING - LATE) // 2
            sp.wait_ge(patches_turned, 4 * PAIRS)
            load_late([LATE_PAIR])
            for q in range(GROUPS - 4, GROUPS - 1):
                store_rows(Group(0, q))
            sp.wait_ge(cx_ready, GROUPS)
            load_late(range(LATE_PAIR + 1, LATE_PAIR + 4))
            store_rows(Group(0, GROUPS - 1))
            for u in range(2):
                sp.wait_ge(scattered[u], 16 * TOPK * PAIRS)
            sp.dma_start(slot_tok[:, :], slots.rearrange("(p e) o -> p (e o)", p=P)).then_inc(slot_tok_landed, 16)
            load_late(range(LATE_PAIR + 4, RING // 2))

            def more_experts(m, n):
                sp.wait_ge(e_down_done, 4 * m + 2 * n + 2)
                sp.wait_ge(ew_landed[n], 48 * (m + RING // 4))
                load_experts(2 * m + n + RING // 2, n, (4 * m + 2 * n) % RING)

            with sp.Fori(0, (E - RING) // 4) as m:
                for n in range(2):
                    more_experts(m, n)

        @block.gpsimd
        def _(pool):
            made = [0]

            def step(ins):
                made[0] += 1
                ins.then_inc(consts_made, 1)

            def done():
                pool.wait_ge(consts_made, made[0])

            step(pool.memset(ident[:, :], 0.0))
            step(pool.memset(ones[:, :], 1.0))
            step(pool.memset(before[:, :], 1.0))
            step(pool.memset(headmask[:, :], 1.0))
            step(pool.memset(third[:, :, :], 1.0))
            step(pool.memset(tri[:, :, :], 0.0))
            step(pool.memset(halfneg[:, :], -0.5))
            step(pool.memset(zero[:, :], 0.0))
            step(pool.iota(nobody[:, :], [[0, E]], base=T, channel_multiplier=1))
            step(pool.iota(base[:, :], [[-1, E]], base=SLOTS, channel_multiplier=0,
                           allow_small_or_imprecise_dtypes=True))
            for u in range(2):
                step(pool.iota(number[u][:, :], [[0, 1]], base=R * u - 2 * R, channel_multiplier=1))
            done()
            step(pool.affine_select(out=ident[:, :], in_=ident[:, :], compare_op=ALU.not_equal, fill=1.0, base=0,
                                    pattern=[[-1, P]], channel_multiplier=1))
            step(pool.affine_select(out=before[:, :], in_=before[:, :], compare_op=ALU.is_gt, fill=0.0, base=0,
                                    pattern=[[1, R]], channel_multiplier=-1))
            step(pool.affine_select(out=headmask[:, :], in_=headmask[:, :], compare_op=ALU.is_ge, fill=0.0, base=0,
                                    pattern=[[-HD, HC]], channel_multiplier=1))
            step(pool.affine_select(out=third[:, :, :], in_=third[:, :, :], compare_op=ALU.is_ge, fill=0.0, base=0,
                                    pattern=[[0, PC], [-S, PH]], channel_multiplier=1))
            step(pool.affine_select(out=tri[:, :, :], in_=tri[:, :, :], compare_op=ALU.is_ge, fill=NEG, base=0,
                                    pattern=[[-S, GI], [-1, S]], channel_multiplier=1))
            done()
            step(pool.affine_select(out=headmask[:, :], in_=headmask[:, :], compare_op=ALU.is_ge, fill=0.0,
                                    base=HD - 1, pattern=[[HD, HC]], channel_multiplier=-1))
            step(pool.affine_select(out=third[:, :, :], in_=third[:, :, :], compare_op=ALU.is_ge, fill=0.0,
                                    base=S - 1, pattern=[[0, PC], [S, PH]], channel_multiplier=-1))
            assert made[0] == CONSTS

            def rstd(g, ve, rs, var_ready, ready):
                pool.wait_ge(var_ready, g.q + 1)
                pool.tensor_tensor(rs[0:g.rows, :], ve[0:g.rows, :], halfneg[0:g.rows, :], ALU.pow).then_inc(ready, 1)

            def add_bo(g):
                if isinstance(g.q, int) and g.q == 0:
                    pool.wait_ge(bo_landed, 16)
                pool.wait_ge(h_ready, g.q + 1)
                if not (isinstance(g.q, int) and g.q < 2):
                    pool.wait_ge(h2_ready, g.q - 1)
                pool.tensor_tensor(hb[g.u][0:g.rows, :], h[g.u][0:g.rows, :], bo_sb[0:g.rows, :],
                                   ALU.add).then_inc(hb_ready, 1)

            def constant_wait():
                pool.wait_ge(consts_made, CONSTS)

            def scatter(g, columns):
                constant_wait()
                pool.wait_ge(idx_ready, g.q + 1)
                pool.wait_ge(number_ready, g.q + 1)
                for k in columns:
                    pool.indirect_dma_start(
                        slots, bass.IndirectOffsetOnAxis(ap=idx[g.u][0:g.rows, k:k + 1], axis=0),
                        number[g.u][0:g.rows, :], None, bounds_check=SLOTS - 1, oob_is_err=False,
                    ).then_inc(scattered[g.u], 16)

            def turn(b, c):
                here = 2 * b + c
                known = isinstance(here, int)
                scattering = not known or 0 <= here - 2 < GROUPS
                if not known or 0 <= here - 1 < GROUPS:
                    rstd(Group(b, c - 1), ve2, rs2, ln2_var, ln2_rstd)
                if scattering:
                    if known and here == 2:
                        pool.wait_ge(slots_cleared, 16)
                    scatter(Group(b, c - 2), range(TOPK // 2))
                if not known or here + 1 < GROUPS:
                    g = Group(b, c + 1)
                    rstd(g, ve1, rs1, ln1_var, ln1_rstd)
                    add_bo(g)
                if scattering:
                    scatter(Group(b, c - 2), range(TOPK // 2, TOPK))

            for i in range(-1, 3):
                turn(0, i)
            with pool.Fori(1, PAIRS - 2) as b:
                turn(b, 1)
                turn(b, 2)
            for i in range(GROUPS - 3, GROUPS):
                turn(0, i)
            behind, last = Group(0, GROUPS - 2), Group(0, GROUPS - 1)
            scatter(behind, range(3))
            rstd(last, ve2, rs2, ln2_var, ln2_rstd)
            scatter(behind, range(3, TOPK))
            scatter(last, range(TOPK))

            def take_tok(e, c):
                pool.tensor_copy(tok[c % 16][:, :], slot_tok[:, bass.ds(e, 1)]).then_inc(tok_ready, 1)

            def gather(c):
                pool.indirect_dma_start(
                    xrow[c % 8][:, :], None, table, bass.IndirectOffsetOnAxis(ap=tok[c % 16][:, :].bitcast(U32), axis=0),
                    bounds_check=T + P - 1, oob_is_err=False,
                ).then_inc(row_landed[c % 8], 16)

            def add(c):
                pool.indirect_dma_start(
                    acc[c % 2], bass.IndirectOffsetOnAxis(ap=tok[c % 16][:, :].bitcast(U32), axis=0),
                    ysc[c % 4][:, :], None, compute_op=ALU.add, bounds_check=T - 1, oob_is_err=False,
                ).then_inc(added[c % 2], 16)

            def step_two(e, c):
                known = isinstance(e, int)
                u = (c - 1) % 2
                if not known or e >= 1:
                    pool.wait_ge(ysc_ready, e)
                if not known or e >= 3:
                    pool.wait_ge(added[u], 8 * (e - 1 - u))
                pool.wait_ge(tok_ready, e + 7 if not known else min(e + 7, E))
                if not known or e + 7 < E:
                    take_tok(e + 7, c + 7)
                if not known or e >= 1:
                    add(c - 1)
                if not known or e + 6 < E:
                    gather(c + 6)

            pool.wait_ge(slot_tok_landed, 16)
            for u in range(2):
                pool.wait_ge(row_stored[u], 16 * PAIRS)
                pool.wait_ge(res_stored[u], 16 * PAIRS)
            pool.wait_ge(rows_cleared, 32)
            take_tok(0, 0)
            pool.wait_ge(tok_ready, 1)
            gather(0)
            for e in range(1, 7):
                take_tok(e, e)
            pool.wait_ge(tok_ready, 7)
            for e in range(1, 6):
                gather(e)
            for e in range(4):
                step_two(e, e)
            with pool.Fori(0, (E - 16) // 16) as m:
                for c in range(4, 20):
                    step_two(16 * m + c, c)
            for e in range(E - 12, E + 1):
                step_two(e, e)
            for u in range(2):
                pool.wait_ge(added[u], 8 * E)
            pool.dma_start(acc[0], acc[1], accum_op=ALU.add, max_dma_last_dim=4 * BANK * 2).then_inc(out_stored, 16)
            pool.wait_ge(out_stored, 16)

        @block.scalar
        def _(act):
            def sort_x(pair, images):
                rows = images * CH * PS
                act.wait_ge(x_landed, 16 * (pair + 1))
                if not (isinstance(pair, int) and pair == 0):
                    act.wait_ge(patches_turned, 4 * pair)
                nc.scalar.activation(xw[0:rows, :, :].rearrange("p w (i j) -> p w i j", i=PATCH),
                                     xraw[0:rows, :].rearrange("p (i w j) -> p w i j", i=PATCH, w=PS),
                                     ACT.Copy).then_inc(x_sorted, 1)

            sort_x(0, 2 * GI)

            def copy_patches(pair, n, images):
                half, w3 = n // 2, n % 2
                act.wait_ge(patches_turned, 4 * pair + n + 1)
                if not (isinstance(pair, int) and pair == 0):
                    act.wait_ge(pT_lo_ready, 2 * pair)
                rows = images * CH * PS
                src = ps[:, 7, 0:3 * rows].rearrange("p (w b c r) -> p b c r w", w=3, b=images, c=CH)
                for c in range(CH):
                    dst = pT[:, c * HALF + half, :].rearrange("p (b s) -> p b s", s=S)[:, 0:images, 1:S].rearrange(
                        "p b (r w) -> p b r w", r=PS)
                    ins = nc.scalar.activation(dst[:, :, :, 3 * w3:3 * w3 + 3], src[:, :, c, :, :], ACT.Copy)
                ins.then_inc(patches_copied, 1)

            def patches_high(pair, half):
                act.wait_ge(patches_copied, 4 * pair + 2 * half + 2)
                if not (isinstance(pair, int) and pair == 0):
                    act.wait_ge(embedded, 2 * pair)
                nc.scalar.activation(pT_hi[:, half::HALF, :], pT[:, half::HALF, :], ACT.Copy).then_inc(pT_hi_ready, 1)

            def copy_xnT(g):
                act.wait_ge(xn_turned, g.q + 1)
                if not (isinstance(g.q, int) and g.q == 0):
                    act.wait_ge(vT_done, g.q)
                nc.scalar.activation(xnT[:, :, 0:g.rows], ps[:, 1, 0:KD * R].rearrange("p (k r) -> p k r", k=KD)[:, :, 0:g.rows],
                                     ACT.Copy).then_inc(xnT_ready, 1)

            def copy_vT(g):
                act.wait_ge(vT_done, g.q + 1)
                if not (isinstance(g.q, int) and g.q == 0):
                    act.wait_ge(v_turned, g.q)
                for k in range(KD):
                    src = ps[:, 3, D + k * R:D + k * R + g.rows].rearrange("p (i s) -> p i s", s=S)
                    ins = nc.scalar.activation(vT[:, k, 0:g.images, :, :],
                                               src.unsqueeze(2).broadcast_to([P, g.images, PH, S]), ACT.Copy)
                ins.then_inc(vT_ready, 1)

            def copy_q(g):
                act.wait_ge(keys_ready, g.q + 1)
                if not (isinstance(g.q, int) and g.q == 0):
                    act.wait_ge(scores_done[1], g.q)
                q = ps[:, 0, 0:KD * R].rearrange("p (k r) -> p k r", k=KD)
                for c in range(KD):
                    zero_diag = qz[:, c, :, :].rearrange("p i r -> p (i r)")
                    dst = bass.AP(tensor=zero_diag.tensor, offset=zero_diag.offset,
                                  ap=[zero_diag.ap[0], [R + S, g.images], [1, S]])
                    ins = nc.scalar.activation(dst, q[:, c, 0:g.rows].rearrange("p (i s) -> p i s", i=g.images), ACT.Copy)
                ins.then_inc(q_ready, 1)

            def copy_k(g):
                act.wait_ge(keys_ready, g.q + 1)
                if not (isinstance(g.q, int) and g.q == 0):
                    act.wait_ge(scores_done[1], g.q)
                for hd in range(HA):
                    ins = nc.scalar.activation(kz[:, :, hd, 0:g.rows], keys[:, :, 0:g.rows], ACT.Copy,
                                               scale=headmask[:, hd:hd + 1])
                ins.then_inc(k_ready, 1)

            def copy_v(g):
                act.wait_ge(v_turned, g.q + 1)
                if not (isinstance(g.q, int) and g.q == 0):
                    act.wait_ge(pv_done, g.q)
                n = g.images
                src = ps[0:R, 2:4, :].rearrange("p a b -> p (a b)")[:, 0:n * D].rearrange("p (i h d) -> p i h d", i=n, h=H)
                for t in range(PH):
                    ins = nc.scalar.activation(vz[:, 0:n, t:H:PH, 0:HD], src[:, :, t:H:PH, :], ACT.Copy,
                                               scale=third[0:R, 0, t:t + 1])
                ins.then_inc(v_ready, 1)

            def copy_cxT(g):
                act.wait_ge(cx_turned, g.q + 1)
                if not (isinstance(g.q, int) and g.q == 0):
                    act.wait_ge(wo_done, g.q)
                nc.scalar.activation(cxT[:, :, 0:g.rows], ps[:, 1, 0:KD * R].rearrange("p (k r) -> p k r", k=KD)[:, :, 0:g.rows],
                                     ACT.Copy).then_inc(cxT_ready, 1)

            def copy_xn2T(g):
                act.wait_ge(xn2_turned, g.q + 1)
                if not (isinstance(g.q, int) and g.q == 0):
                    act.wait_ge(gu_done, g.q)
                nc.scalar.activation(xn2T[:, :, 0:g.rows], ps[:, 1, 0:KD * R].rearrange("p (k r) -> p k r", k=KD)[:, :, 0:g.rows],
                                     ACT.Copy).then_inc(xn2T_ready, 1)

            def exp_probs(g, c):
                act.wait_ge(lowered[c], g.q + 1)
                if not (isinstance(g.q, int) and g.q == 0):
                    act.wait_ge(prob_turned, g.q)
                nc.scalar.activation(prob[0:g.rows, c * HC * S:(c + 1) * HC * S],
                                     sx[0:g.rows, c * HC:(c + 1) * HC, :].rearrange("p h s -> p (h s)"), ACT.Exp,
                                     scale=float(HD) ** -0.5).then_inc(prob_ready[c], 1)

            def copy_probT(g):
                act.wait_ge(prob_turned, g.q + 1)
                if not (isinstance(g.q, int) and g.q == 0):
                    act.wait_ge(pv_done, g.q)
                a = ps[:, 2, 0:3 * R].rearrange("p (k r) -> p k r", k=3)
                z = ps[:, 3, 0:3 * R].rearrange("p (k r) -> p k r", k=3)
                nc.scalar.activation(probT[0:R, 0:3, 0:g.rows], a[0:R, :, 0:g.rows], ACT.Copy)
                nc.scalar.activation(probT[0:R, 3:5, 0:g.rows], z[0:R, 0:2, 0:g.rows], ACT.Copy)
                nc.scalar.activation(probT[0:S, 5, 0:g.rows], z[0:S, 2, 0:g.rows], ACT.Copy).then_inc(probT_ready, 1)

            def route_exp(g):
                act.wait_ge(shifted_ready, g.q + 1)
                if not (isinstance(g.q, int) and g.q == 0):
                    act.wait_ge(em_ready, g.q)
                nc.scalar.activation(ex[0:g.rows, :], shifted[0:g.rows, :], ACT.Exp).then_inc(ex_ready, 1)

            def shared_tanh(g):
                act.wait_ge(gu_done, g.q + 1)
                if not (isinstance(g.q, int) and g.q == 0):
                    act.wait_ge(g1_ready, g.q)
                nc.scalar.activation(th[:, :, 0:g.rows], ps[0:FP, 0, 0:2 * R].rearrange("p (k r) -> p k r", k=2)[:, :, 0:g.rows],
                                     ACT.Tanh, scale=0.5).then_inc(tanh_ready, 1)

            def turn(b, c):
                here = 2 * b + c
                known = isinstance(here, int)
                front = not known or 0 <= here + 1 < GROUPS
                mid = not known or 0 <= here < GROUPS
                back = not known or 0 <= here - 1 < GROUPS
                placing = not known or 0 <= here - 2 < GROUPS
                pair, half = b + (c + 2) // 2, c % 2
                images = 2 * GI if not known else min(2 * GI, IMAGES - 2 * GI * pair)
                turning = images > 0
                if turning:
                    copy_patches(pair, 2 * half, images)
                if mid:
                    copy_q(Group(b, c))
                if back:
                    copy_cxT(Group(b, c - 1))
                if mid:
                    copy_k(Group(b, c))
                    copy_vT(Group(b, c))
                if turning:
                    copy_patches(pair, 2 * half + 1, images)
                if turning and half == 1:
                    patches_high(pair, 1)
                if mid:
                    exp_probs(Group(b, c), 0)
                if back:
                    copy_xn2T(Group(b, c - 1))
                if mid:
                    copy_v(Group(b, c))
                    exp_probs(Group(b, c), 1)
                    copy_probT(Group(b, c))
                if turning and half == 0:
                    patches_high(pair, 0)
                if back:
                    shared_tanh(Group(b, c - 1))
                    route_exp(Group(b, c - 1))
                if front:
                    copy_xnT(Group(b, c + 1))
                if half == 1 and (not known or pair + 1 < PAIRS):
                    sort_x(pair + 1, 2 * GI if not known else min(2 * GI, IMAGES - 2 * GI * (pair + 1)))

            act.wait_ge(zeros_made, 3)
            act.wait_ge(masks_made, GI)
            turn(0, -2)
            for n in range(4):
                act.wait_ge(wT_turned, n + 1)
                if n < 3:
                    nc.scalar.activation(wT_hi[:, 2 * n:2 * n + 2, :].rearrange("p a b -> p (a b)"),
                                         ps[:, n, 0:2 * D], ACT.Copy).then_inc(wT_copied, 1)
                else:
                    nc.scalar.activation(rT[:, :, :].rearrange("p a b -> p (a b)"), ps[:, n, 0:KD * E],
                                         ACT.Copy).then_inc(wT_copied, 1)
            for i in range(-1, 3):
                turn(0, i)
            with act.Fori(1, PAIRS - 2) as b:
                turn(b, 1)
                turn(b, 2)
            for i in range(GROUPS - 3, GROUPS + 1):
                turn(0, i)

            def x_high(e, u):
                act.wait_ge(row_turned, e + 1)
                if not isinstance(e, int) or e >= 2:
                    act.wait_ge(e_gu_done, e - 1)
                nc.scalar.activation(x_hi[u][:, :], ps[:, 2 + u, 0:KD * P], ACT.Copy).then_inc(x_hi_ready, 1)

            def w_high(e, c):
                act.wait_ge(ew_landed[c // 2 % 2], 12 * (e - c % 4) + 48)
                if not isinstance(e, int) or e >= 2:
                    act.wait_ge(e_gu_done, e - 1)
                nc.scalar.activation(w_hi[c % 2][:, :], ew[:, bass.ds(e % RING, 1), 0:GU].rearrange("p a b -> p (a b)"),
                                     ACT.Copy).then_inc(w_hi_ready, 1)

            def silu(e, u):
                act.wait_ge(e_gu_done, e + 1)
                if not isinstance(e, int) or e >= 2:
                    act.wait_ge(hh_ready, e - 1)
                nc.scalar.activation(sg[u][:, :], ps[:, u, 0:F], ACT.Silu).then_inc(silu_ready, 1)

            def copy_hT(e, u):
                act.wait_ge(hh_turned, e + 1)
                if not isinstance(e, int) or e >= 2:
                    act.wait_ge(e_down_done, e - 1)
                nc.scalar.activation(hT[u][:, :, :].rearrange("p k r -> p (k r)"), ps[0:FP, 4 + u, 0:FC * P],
                                     ACT.Copy).then_inc(hT_ready, 1)

            def experts(m, last=False):
                for c in range(4):
                    e = 4 * m + c
                    silu(e, c % 2)
                    if not (last and c >= 2):
                        w_high(e + 2, c + 2)
                    copy_hT(e, c % 2)
                    if not (last and c >= 2):
                        x_high(e + 2, c % 2)

            nc.scalar.activation(silu_warm[:, :], halfneg[:, :], ACT.Silu)
            for e in range(2):
                w_high(e, e)
                x_high(e, e)
            experts(0)
            with act.Fori(1, E // 4 - 1) as m:
                experts(m)
            experts(E // 4 - 1, last=True)

        @block.tensor
        def _(pe):
            pe.wait_ge(consts_made, CONSTS)

            def turn_patches(here, pair, n, images):
                half, w3 = n // 2, n % 2
                rows = images * CH * PS
                known = isinstance(here, int)
                if n == 0:
                    pe.wait_ge(x_sorted, pair + 1)
                if w3 == 0:
                    if not known or here >= 0:
                        pe.wait_ge(h_ready, here + 1)
                    elif n > 0:
                        pe.wait_ge(patches_copied, 4 * pair + n)
                else:
                    pe.wait_ge(patches_copied, 4 * pair + n)
                    if not known or here >= 2:
                        pe.wait_ge(res_ready, here - 1)
                for w in range(3):
                    ins = nc.tensor.transpose(ps[:, 7, w * rows:(w + 1) * rows],
                                              xw[0:rows, 3 * w3 + w, half * P:(half + 1) * P], ident[0:rows, 0:rows])
                ins.then_inc(patches_turned, 1)

            def embed(g, pieces):
                if isinstance(g.q, int) and g.q == 0:
                    pe.wait_ge(wT_copied, 4)
                    pe.wait_ge(wT_low, 3)
                pe.wait_ge(pT_lo_ready, 2 * g.pair + 2)
                if pieces is not None:
                    pe.wait_ge(patches_copied, pieces)
                else:
                    pe.wait_ge(res_ready, g.q - 2)
                parts = [(a, w, k) for a, w in ((pT_hi, wT_hi), (pT_hi, wT_lo), (pT_lo, wT_hi)) for k in range(XCH)]
                for n, (a, w, k) in enumerate(parts):
                    ins = nc.tensor.matmul(ps[0:g.rows, 7, 0:D], a[:, k, g.u * R:g.u * R + g.rows], w[:, k, :],
                                           start=(n == 0), stop=(n == len(parts) - 1))
                ins.then_inc(embedded, 1)

            def turn_two(g, src, done):
                for k in range(KD):
                    ins = nc.tensor.transpose(ps[:, 1, k * R:k * R + g.rows], src[0:g.rows, k * P:(k + 1) * P],
                                              ident[0:g.rows, 0:g.rows])
                ins.then_inc(done, 1)

            def turn_xn(g):
                pe.wait_ge(xn_ready, g.q + 1)
                if not (isinstance(g.q, int) and g.q < 2):
                    pe.wait_ge(xn2T_ready, g.q - 1)
                elif g.q == 1:
                    pe.wait_ge(xnT_ready, 1)
                turn_two(g, xn, xn_turned)

            def project_qk(g):
                if isinstance(g.q, int) and g.q == 0:
                    pe.wait_ge(qk_landed, 32)
                pe.wait_ge(xnT_ready, g.q + 1)
                if not (isinstance(g.q, int) and g.q < 2):
                    pe.wait_ge(hs_ready, g.q - 1)
                elif g.q == 1:
                    pe.wait_ge(q_ready, 1)
                for c in range(2 * KD):
                    for k in range(KD):
                        ins = nc.tensor.matmul(ps[:, 0, c * R:c * R + g.rows], wqk[:, k, c * P:(c + 1) * P],
                                               xnT[:, k, 0:g.rows], start=(k == 0), stop=(k == KD - 1))
                ins.then_inc(qk_done, 1)

            def project_v(g):
                if isinstance(g.q, int) and g.q == 0:
                    pe.wait_ge(v_landed, 16)
                if not (isinstance(g.q, int) and g.q == 0):
                    pe.wait_ge(probT_ready, g.q)
                for c in range(KD):
                    for k in range(KD):
                        ins = nc.tensor.matmul(ps[:, 3, D + c * R:D + c * R + g.rows], wv[:, k, c * P:(c + 1) * P],
                                               xnT[:, k, 0:g.rows], start=(k == 0), stop=(k == KD - 1))
                ins.then_inc(vT_done, 1)

            def turn_v(g):
                pe.wait_ge(vT_ready, g.q + 1)
                for i in range(g.images):
                    for k in range(KD):
                        at = (i % 2) * D + k * P
                        ins = nc.tensor.transpose(ps[0:R, 2 + i // 2, at:at + P],
                                                  vT[:, k, i, :, :].rearrange("p a s -> p (a s)"), ident[:, :])
                ins.then_inc(v_turned, 1)

            def scores(g, c):
                if c == 0:
                    pe.wait_ge(q_ready, g.q + 1)
                    pe.wait_ge(k_ready, g.q + 1)
                    pe.wait_ge(k_more_ready, g.q + 1)
                    if not (isinstance(g.q, int) and g.q == 0):
                        pe.wait_ge(sum_ready, g.q)
                for i in range(g.images):
                    ins = nc.tensor.matmul(ps[0:g.rows, 5 + c, 0:HC * S], qz[:, c, i, 0:g.rows],
                                           kz[:, c, :, S * i:S * i + S], start=(i == 0), stop=(i == g.images - 1))
                ins.then_inc(scores_done[c], 1)

            def turn_probs(g):
                for c in range(KD):
                    pe.wait_ge(prob_ready[c], g.q + 1)
                pe.wait_ge(v_ready, g.q + 1)
                for c in range(PC):
                    cols = min(PH * S, H * S - c * PH * S)
                    ins = nc.tensor.transpose(ps[0:cols, 2 + c // 3, (c % 3) * R:(c % 3) * R + g.rows],
                                              prob[0:g.rows, c * PH * S:c * PH * S + cols], ident[0:g.rows, 0:g.rows])
                ins.then_inc(prob_turned, 1)

            def context(g, chunks):
                pe.wait_ge(probT_ready, g.q + 1)
                for c in range(KD):
                    pe.wait_ge(masked[c], g.q + 1)
                for c in chunks:
                    rows = min(PH * S, H * S - c * PH * S)
                    wide = PH * VW
                    ins = nc.tensor.matmul(
                        ps[0:g.rows, 5 + c // 3, 0:GI * 3 * wide].rearrange("p (i c w) -> p i c w", i=GI, c=3)[
                            :, 0:g.images, c % 3, :],
                        probT[0:rows, c, 0:g.rows],
                        vz[0:rows, 0:g.images, c * PH:(c + 1) * PH, :].rearrange("p i h d -> p i (h d)"),
                        start=True, stop=True)
                if PC - 1 in chunks:
                    ins.then_inc(pv_done, 1)

            def turn_cx(g):
                pe.wait_ge(cx_ready, g.q + 1)
                if isinstance(g.q, int) and g.q == GROUPS - 1:
                    pe.wait_ge(xnT_ready, GROUPS)
                else:
                    pe.wait_ge(xnT_ready, g.q + 2)
                turn_two(g, cx[:, :, :].rearrange("p h d -> p (h d)"), cx_turned)

            def project_o(g):
                if isinstance(g.q, int) and g.q == 0:
                    pe.wait_ge(wo_landed, 16)
                pe.wait_ge(cxT_ready, g.q + 1)
                if not (isinstance(g.q, int) and g.q == 0):
                    pe.wait_ge(room_ready, g.q)
                for k in range(KD):
                    ins = nc.tensor.matmul(ps[0:g.rows, 4, 0:D], cxT[:, k, 0:g.rows], wo[:, k, :],
                                           start=(k == 0), stop=(k == KD - 1))
                ins.then_inc(wo_done, 1)

            def turn_xn2(g):
                pe.wait_ge(xn2_ready, g.q + 1)
                pe.wait_ge(cxT_ready, g.q + 1)
                turn_two(g, xs[g.u], xn2_turned)

            def route(g):
                pe.wait_ge(xn2T_ready, g.q + 1)
                pe.wait_ge(h2_ready, g.q + 1)
                for k in range(KD):
                    ins = nc.tensor.matmul(ps[0:g.rows, 4, 0:E], xn2T[:, k, 0:g.rows], rT[:, k, :],
                                           start=(k == 0), stop=(k == KD - 1))
                ins.then_inc(router_done, 1)

            def shared_up(g):
                if isinstance(g.q, int) and g.q == 0:
                    pe.wait_ge(shared_landed, 32)
                behind = GROUPS if isinstance(g.q, int) and g.q == GROUPS - 1 else g.q + 2
                pe.wait_ge(q_ready, behind)
                for j in range(2 * FC):
                    for k in range(KD):
                        ins = nc.tensor.matmul(ps[0:FP, 0, j * R:j * R + g.rows], wsgu[:, k, j * FP:(j + 1) * FP],
                                               xn2T[:, k, 0:g.rows], start=(k == 0), stop=(k == KD - 1))
                ins.then_inc(gu_done, 1)

            def shared_down(g, pieces):
                pe.wait_ge(hs_ready, g.q + 1)
                if pieces is not None:
                    pe.wait_ge(patches_copied, pieces)
                pe.wait_ge(h_ready, min(g.q + 3, GROUPS) if isinstance(g.q, int) else g.q + 3)
                for j in range(FC):
                    ins = nc.tensor.matmul(ps[0:g.rows, 7, 0:D], hs[:, j, 0:g.rows], wsd[:, j, :],
                                           start=(j == 0), stop=(j == FC - 1))
                ins.then_inc(down_done, 1)

            def places(g):
                pe.wait_ge(chosen_ready, g.q + 1)
                pe.wait_ge(earlier_ready, g.q + 1)
                pe.wait_ge(logits_ready, g.q + 1)
                nc.tensor.matmul(ps[0:g.rows, 4, 0:E], before[0:g.rows, 0:g.rows], chosen[g.u][0:g.rows, :],
                                 start=True, stop=False)
                nc.tensor.matmul(ps[0:g.rows, 4, 0:E], ones[0:R, 0:g.rows], earlier[g.u][0:R, :],
                                 start=False, stop=True).then_inc(places_done, 1)

            def turn(b, c):
                here = 2 * b + c
                known = isinstance(here, int)
                front = not known or 0 <= here + 1 < GROUPS
                mid = not known or 0 <= here < GROUPS
                back = not known or 0 <= here - 1 < GROUPS
                placing = not known or 0 <= here - 2 < GROUPS
                pair, half = b + (c + 2) // 2, c % 2
                images = 2 * GI if not known else min(2 * GI, IMAGES - 2 * GI * pair)
                turning = images > 0
                if mid:
                    project_qk(Group(b, c))
                if turning:
                    turn_patches(here, pair, 2 * half, images)
                if mid:
                    project_v(Group(b, c))
                if back:
                    turn_cx(Group(b, c - 1))
                if placing:
                    shared_down(Group(b, c - 2), 4 * pair + 2 * half + 1 if turning else None)
                if back:
                    project_o(Group(b, c - 1))
                if mid:
                    scores(Group(b, c), 0)
                if turning:
                    turn_patches(here, pair, 2 * half + 1, images)
                if mid:
                    scores(Group(b, c), 1)
                    turn_v(Group(b, c))
                if back:
                    turn_xn2(Group(b, c - 1))
                if front:
                    embed(Group(b, c + 1), 4 * pair + 2 * half + 2 if turning else None)
                if back:
                    route(Group(b, c - 1))
                if mid:
                    turn_probs(Group(b, c))
                if back:
                    shared_up(Group(b, c - 1))
                if mid:
                    context(Group(b, c), range(PC - 2))
                if front:
                    turn_xn(Group(b, c + 1))
                if mid:
                    context(Group(b, c), range(PC - 2, PC))
                if back:
                    places(Group(b, c - 1))

            turn(0, -2)
            pe.wait_ge(w_landed, 16)
            for n in range(3):
                for dd in range(2):
                    for k in range(KD):
                        ins = nc.tensor.transpose(ps[:, n, dd * D + k * P:dd * D + (k + 1) * P],
                                                  wraw[:, k, (2 * n + dd) * P:(2 * n + dd + 1) * P], ident[:, :])
                ins.then_inc(wT_turned, 1)
            pe.wait_ge(router_landed, 16)
            for k in range(KD):
                ins = nc.tensor.transpose(ps[:, 3, k * E:(k + 1) * E], rraw[:, k * P:(k + 1) * P], ident[0:E, 0:E])
            ins.then_inc(wT_turned, 1)
            for i in range(-1, 3):
                turn(0, i)
            with pe.Fori(1, PAIRS - 2) as b:
                turn(b, 1)
                turn(b, 2)
            for i in range(GROUPS - 3, GROUPS):
                turn(0, i)
            behind, last = Group(0, GROUPS - 2), Group(0, GROUPS - 1)
            turn_cx(last)
            project_o(last)
            shared_down(behind, None)
            turn_xn2(last)
            route(last)
            places(last)
            shared_up(last)
            shared_down(last, None)

            pe.wait_ge(res_ready, GROUPS)
            pe.wait_ge(room_ready, GROUPS)

            def turn_rows(e, c, lap):
                pe.wait_ge(row_landed[c], 16 * (lap + 1))
                if not isinstance(e, int) or e >= 2:
                    pe.wait_ge(x_lo_ready, e - 1)
                for k in range(KD):
                    ins = nc.tensor.transpose(ps[:, 2 + c % 2, k * P:(k + 1) * P], xrow[c][:, k:D:KD], ident[:, :])
                ins.then_inc(row_turned, 1)

            def gate_up(e, u):
                pe.wait_ge(x_lo_ready, e + 1)
                pe.wait_ge(w_lo_ready, e + 1)
                if not isinstance(e, int) or e >= 2:
                    pe.wait_ge(hh_ready, e - 1)
                parts = [(a, w, k) for a, w in ((x_hi, w_hi), (x_hi, w_lo), (x_lo, w_hi)) for k in range(KD)]
                for n, (a, w, k) in enumerate(parts):
                    ins = nc.tensor.matmul(ps[:, u, 0:2 * F], a[u][:, k * P:(k + 1) * P],
                                           w[u][:, :].rearrange("p (m k f) -> p m k f", m=2, k=KD)[:, :, k, :],
                                           start=(n == 0), stop=(n == len(parts) - 1))
                ins.then_inc(e_gu_done, 1)

            def turn_hidden(e, u):
                pe.wait_ge(hh_ready, e + 1)
                if not isinstance(e, int) or e >= 2:
                    pe.wait_ge(hT_ready, e - 1)
                for k in range(FC):
                    ins = nc.tensor.transpose(ps[0:FP, 4 + u, k * P:(k + 1) * P], hh[u][:, k:F:FC], ident[:, :])
                ins.then_inc(hh_turned, 1)

            def down(e, u, slot):
                pe.wait_ge(hT_ready, e + 1)
                if not isinstance(e, int) or e >= 2:
                    pe.wait_ge(ysc_ready, e - 1)
                for k in range(FC):
                    ins = nc.tensor.matmul(ps[:, 6 + u, 0:D], hT[u][:, k, :],
                                           ew[0:FP, slot, 2 * KD * F + k * D:2 * KD * F + (k + 1) * D],
                                           start=(k == 0), stop=(k == FC - 1))
                ins.then_inc(e_down_done, 1)

            def experts(m, first=False, last=False):
                for c in range(8):
                    e = 8 * m + c
                    gate_up(e, c % 2)
                    if not (first and c == 0):
                        down(e - 1, (c - 1) % 2, (e - 1) % RING)
                    if not (last and c >= 6):
                        turn_rows(e + 2, (c + 2) % 8, m + (c + 2) // 8)
                    turn_hidden(e, c % 2)

            for e in range(2):
                turn_rows(e, e, 0)
            experts(0, first=True)
            with pe.Fori(1, E // 8 - 1) as m:
                experts(m)
            experts(E // 8 - 1, last=True)
            down(E - 1, 1, (E - 1) % RING)

        @block.vector
        def _(dve):
            V = nc.vector
            V.memset(qz[:, :, :, :], 0.0).then_inc(zeros_made, 1)
            V.memset(vz[:, :, :, :], 0.0).then_inc(zeros_made, 1)
            V.memset(pT[:, :, :], 0.0).then_inc(zeros_made, 1)
            V.memset(earlier[0][:, :], 0.0).then_inc(earlier_ready, 1)
            dve.wait_ge(consts_made, CONSTS)
            dve.wait_ge(zeros_made, 3)
            for i in range(GI):
                V.tensor_copy(vz[:, i, :, HD], third[0:R, :, :].rearrange("p c r -> p (c r)")).then_inc(masks_made, 1)
            V.tensor_scalar(causal[:, :], tri[:, 0, :], third[:, 0, 0:1], None, ALU.mult).then_inc(dve_const, 1)
            for i in range(1, GI):
                dve.wait_ge(dve_const, i)
                V.scalar_tensor_tensor(out=causal[:, :], in0=tri[:, i, :], scalar=third[:, 0, i:i + 1],
                                       in1=causal[:, :], op0=ALU.mult, op1=ALU.add).then_inc(dve_const, 1)
            dve.wait_ge(pos_landed, 16 * 3 * GI)
            V.tensor_tensor(posb[0:R, :], posb[0:R, :], posadd[0:R, :], ALU.add).then_inc(masks_made, 1)
            dve.wait_ge(masks_made, 4)
            dve.wait_ge(dve_const, GI)

            def at(g, t):
                return t[0:g.rows]

            def constant_wait():
                dve.wait_ge(consts_made, CONSTS)

            def norm(g, src, st, mv, ve, stats, mean, var):
                V.bn_stats(st[0:g.rows, :], src).then_inc(stats, 1)
                constant_wait()
                dve.wait_ge(stats, g.q + 1)
                V.bn_aggr(mv[0:g.rows, :], st[0:g.rows, :]).then_inc(mean, 1)
                dve.wait_ge(mean, g.q + 1)
                V.tensor_scalar(ve[0:g.rows, :], mv[0:g.rows, 1:2], EPS, None, ALU.add).then_inc(var, 1)

            def patches_low(pair, half):
                dve.wait_ge(pT_hi_ready, 2 * pair + half + 1)
                if not (isinstance(pair, int) and pair == 0):
                    dve.wait_ge(embedded, 2 * pair)
                V.tensor_tensor(pT_lo[:, half::HALF, :], pT[:, half::HALF, :], pT_hi[:, half::HALF, :].bitcast(F32),
                                ALU.subtract).then_inc(pT_lo_ready, 1)

            def tokens(g):
                r = g.rows
                dve.wait_ge(embedded, g.q + 1)
                if not (isinstance(g.q, int) and g.q < 2):
                    dve.wait_ge(hb_ready, g.q - 1)
                V.tensor_tensor(h[g.u][0:r, :], ps[0:r, 7, 0:D], posb[0:r, :], ALU.add).then_inc(h_ready, 1)
                dve.wait_ge(h_ready, g.q + 1)
                norm(g, h[g.u][0:r, :], st1, mv1, ve1, ln1_stats, ln1_mean, ln1_var)

            def normed(g):
                r = g.rows
                dve.wait_ge(ln1_rstd, g.q + 1)
                if not (isinstance(g.q, int) and g.q == 0):
                    dve.wait_ge(xn_turned, g.q)
                V.tensor_scalar(xn[0:r, :], h[g.u][0:r, :], mv1[0:r, 0:1], rs1[0:r, 0:1], ALU.subtract,
                                ALU.mult).then_inc(xn_ready, 1)

            def copy_keys(g):
                dve.wait_ge(qk_done, g.q + 1)
                if not (isinstance(g.q, int) and g.q == 0):
                    dve.wait_ge(k_ready, g.q)
                k = ps[:, 0, KD * R:2 * KD * R].rearrange("p (k r) -> p k r", k=KD)
                V.tensor_copy(keys[:, :, 0:g.rows], k[:, :, 0:g.rows]).then_inc(keys_ready, 1)

            def more_keys(g):
                dve.wait_ge(keys_ready, g.q + 1)
                if not (isinstance(g.q, int) and g.q == 0):
                    dve.wait_ge(scores_done[1], g.q)
                for hd in range(HA, HC):
                    ins = V.tensor_scalar(kz[:, :, hd, 0:g.rows], keys[:, :, 0:g.rows], headmask[:, hd:hd + 1], None, ALU.mult)
                ins.then_inc(k_more_ready, 1)

            def softmax(g, c):
                r = g.rows
                hs_c = slice(c * HC, (c + 1) * HC)
                dve.wait_ge(scores_done[c], g.q + 1)
                V.tensor_tensor(sm[0:r, hs_c, :], ps[0:r, 5 + c, 0:HC * S].rearrange("p (h s) -> p h s", h=HC),
                                causal[0:r, :].unsqueeze(1).broadcast_to([r, HC, S]), ALU.add).then_inc(masked[c], 1)
                dve.wait_ge(masked[c], g.q + 1)
                V.tensor_reduce(mx[0:r, hs_c], sm[0:r, hs_c, :], AX, ALU.max).then_inc(max_ready[c], 1)
                dve.wait_ge(max_ready[c], g.q + 1)
                if not (isinstance(g.q, int) and g.q == 0):
                    dve.wait_ge(prob_ready[c], g.q)
                V.tensor_tensor(sx[0:r, hs_c, :], sm[0:r, hs_c, :], mx[0:r, hs_c].unsqueeze(2).broadcast_to([r, HC, S]),
                                ALU.subtract).then_inc(lowered[c], 1)

            def gather_context(g):
                r = g.rows
                dve.wait_ge(pv_done, g.q + 1)
                wide = PH * VW
                o = ps[0:r, 5:7, 0:3 * GI * wide].rearrange("p a (i w) -> p a i w", i=GI)
                s4 = ctxsum[0:r, :, :].rearrange("p (a w) d -> p a (w d)", a=2)
                V.tensor_scalar(s4, o[:, :, 0, :], third[0:r, 0, 0:1], None, ALU.mult).then_inc(sum_a, 1)

            def gather_image(g, i):
                r = g.rows
                wide = PH * VW
                o = ps[0:r, 5:7, 0:3 * GI * wide].rearrange("p a (i w) -> p a i w", i=GI)
                s4 = ctxsum[0:r, :, :].rearrange("p (a w) d -> p a (w d)", a=2)
                if i < g.images:
                    dve.wait_ge((sum_a, sum_b)[i - 1], g.q + 1)
                    V.scalar_tensor_tensor(out=s4, in0=o[:, :, i, :], scalar=third[0:r, 0, i:i + 1], in1=s4,
                                           op0=ALU.mult, op1=ALU.add).then_inc((sum_b, sum_ready)[i - 1], 1)
                elif i == GI - 1:
                    dve.wait_ge(sum_a, g.q + 1)
                    V.tensor_copy(rden[0:r, 0:1], ctxsum[0:r, 0:1, 0]).then_inc(sum_ready, 1)

            def divide_context(g):
                r = g.rows
                dve.wait_ge(sum_ready, g.q + 1)
                V.reciprocal(rden[0:r, :], ctxsum[0:r, 0:H, HD]).then_inc(rden_ready, 1)
                dve.wait_ge(rden_ready, g.q + 1)
                if not (isinstance(g.q, int) and g.q == 0):
                    dve.wait_ge(cx_turned, g.q)
                V.tensor_tensor(cx[0:r, :, :], ctxsum[0:r, 0:H, 0:HD], rden[0:r, :].unsqueeze(2).broadcast_to([r, H, HD]),
                                ALU.mult).then_inc(cx_ready, 1)

            def residual(g):
                r = g.rows
                dve.wait_ge(wo_done, g.q + 1)
                dve.wait_ge(hb_ready, g.q + 1)
                V.tensor_tensor(h2[g.u][0:r, :], ps[0:r, 4, 0:D], hb[g.u][0:r, :], ALU.add).then_inc(h2_ready, 1)

            def residual_norm(g):
                r = g.rows
                dve.wait_ge(h2_ready, g.q + 1)
                norm(g, h2[g.u][0:r, :], st2, mv2, ve2, ln2_stats, ln2_mean, ln2_var)

            def normed_two(g):
                r = g.rows
                if not (isinstance(g.q, int) and g.q < 2):
                    dve.wait_ge(scattered[g.u], 16 * TOPK * g.pair)
                V.tensor_scalar(number[g.u][:, :], number[g.u][:, :], 2.0 * R, None, ALU.add).then_inc(number_ready, 1)
                if not (isinstance(g.q, int) and g.q < 2):
                    dve.wait_ge(row_stored[g.u], 16 * g.pair)
                dve.wait_ge(ln2_rstd, g.q + 1)
                V.tensor_scalar(xs[g.u][0:r, 0:D], h2[g.u][0:r, :], mv2[0:r, 0:1], rs2[0:r, 0:1], ALU.subtract,
                                ALU.mult).then_inc(xn2_ready, 1)

            def choose(g):
                r = g.rows
                dve.wait_ge(router_done, g.q + 1)
                V.tensor_copy(lg[0:r, :], ps[0:r, 4, 0:E]).then_inc(logits_ready, 1)
                constant_wait()
                dve.wait_ge(logits_ready, g.q + 1)
                V.max(top[0:r, :], lg[0:r, :]).then_inc(top_ready, 1)
                constant_wait()
                dve.wait_ge(top_ready, g.q + 1)
                V.match_replace(cut[0:r, :], top[0:r, :], lg[0:r, :], NEG).then_inc(cut_ready, 1)
                if not (isinstance(g.q, int) and g.q == 0):
                    dve.wait_ge(ex_ready, g.q)
                V.tensor_scalar(shifted[0:r, :], lg[0:r, :], top[0:r, 0:1], None, ALU.subtract).then_inc(shifted_ready, 1)
                dve.wait_ge(cut_ready, g.q + 1)
                V.tensor_tensor(chosen[g.u][0:r, :], lg[0:r, :], cut[0:r, :], ALU.not_equal).then_inc(chosen_ready, 1)
                dve.wait_ge(chosen_ready, g.q + 1)
                if not (isinstance(g.q, int) and g.q == GROUPS - 1):
                    if not (isinstance(g.q, int) and g.q == 0):
                        dve.wait_ge(places_done, g.q)
                    V.tensor_tensor(earlier[1 - g.u][0:R, :], earlier[g.u][0:R, :], chosen[g.u][0:R, :],
                                    ALU.add).then_inc(earlier_ready, 1)

            def weigh(g):
                r = g.rows
                dve.wait_ge(ex_ready, g.q + 1)
                V.tensor_tensor_reduce(em[0:r, :], ex[0:r, :], chosen[g.u][0:r, :], 1.0, 0.0, ALU.mult, ALU.add,
                                       wsum[0:r, :]).then_inc(em_ready, 1)

            def weigh_sum(g):
                r = g.rows
                dve.wait_ge(em_ready, g.q + 1)
                V.reciprocal(wrec[0:r, :], wsum[0:r, :]).then_inc(wrec_ready, 1)

            def weigh_row(g):
                r = g.rows
                dve.wait_ge(wrec_ready, g.q + 1)
                V.tensor_scalar(xs[g.u][0:r, D:D + E], em[0:r, :], wrec[0:r, 0:1], None, ALU.mult).then_inc(row_ready, 1)

            def place(g):
                r = g.rows
                dve.wait_ge(places_done, g.q + 1)
                V.scalar_tensor_tensor(out=room[0:r, :], in0=ps[0:r, 4, 0:E], scalar=float(-E), in1=base[0:r, :],
                                       op0=ALU.mult, op1=ALU.add)
                V.scalar_tensor_tensor(out=fits[0:r, :], in0=ps[0:r, 4, 0:E], scalar=float(CAP),
                                       in1=chosen[g.u][0:r, :], op0=ALU.is_lt, op1=ALU.mult).then_inc(room_ready, 1)

            def name_slots(g):
                r = g.rows
                dve.wait_ge(room_ready, g.q + 1)
                V.tensor_tensor(code[0:r, :], room[0:r, :], fits[0:r, :], ALU.mult).then_inc(code_ready, 1)

            def name_largest(g):
                r = g.rows
                constant_wait()
                dve.wait_ge(code_ready, g.q + 1)
                V.max(top2[0:r, :], code[0:r, :]).then_inc(top2_ready, 1)

            def name_index(g):
                r = g.rows
                dve.wait_ge(top2_ready, g.q + 1)
                V.tensor_scalar(idx[g.u][0:r, :], top2[0:r, :], -1.0, float(SLOTS), ALU.mult, ALU.add).then_inc(idx_ready, 1)

            def shared_gate(g):
                r = g.rows
                gu = ps[0:FP, 0, 0:4 * R].rearrange("p (k r) -> p k r", k=4)
                dve.wait_ge(tanh_ready, g.q + 1)
                V.scalar_tensor_tensor(out=g1[:, :, 0:r], in0=th[:, :, 0:r], scalar=1.0, in1=gu[:, 0:2, 0:r],
                                       op0=ALU.add, op1=ALU.mult).then_inc(g1_ready, 1)
                dve.wait_ge(g1_ready, g.q + 1)
                if not (isinstance(g.q, int) and g.q == 0):
                    dve.wait_ge(down_done, g.q)
                V.scalar_tensor_tensor(out=hs[:, :, 0:r], in0=g1[:, :, 0:r], scalar=0.5, in1=gu[:, 2:4, 0:r],
                                       op0=ALU.mult, op1=ALU.mult).then_inc(hs_ready, 1)

            def shared_add(g):
                r = g.rows
                dve.wait_ge(down_done, g.q + 1)
                if not (isinstance(g.q, int) and g.q < 2):
                    dve.wait_ge(res_stored[g.u], 16 * g.pair)
                V.tensor_tensor(res[g.u][0:r, :], ps[0:r, 7, 0:D], h2[g.u][0:r, :], ALU.add).then_inc(res_ready, 1)

            def turn(b, c):
                here = 2 * b + c
                known = isinstance(here, int)
                front = not known or 0 <= here + 1 < GROUPS
                mid = not known or 0 <= here < GROUPS
                back = not known or 0 <= here - 1 < GROUPS
                placing = not known or 0 <= here - 2 < GROUPS
                pair, half = b + (c + 2) // 2, c % 2
                images = 2 * GI if not known else min(2 * GI, IMAGES - 2 * GI * pair)
                turning = images > 0
                if placing:
                    place(Group(b, c - 2))
                if mid:
                    more_keys(Group(b, c))
                if placing:
                    name_slots(Group(b, c - 2))
                    shared_add(Group(b, c - 2))
                if back:
                    residual(Group(b, c - 1))
                if placing:
                    name_largest(Group(b, c - 2))
                if back:
                    residual_norm(Group(b, c - 1))
                if placing:
                    name_index(Group(b, c - 2))
                if mid:
                    softmax(Group(b, c), 0)
                if back:
                    normed_two(Group(b, c - 1))
                if turning and half == 1:
                    patches_low(pair, 1)
                if mid:
                    softmax(Group(b, c), 1)
                if front:
                    tokens(Group(b, c + 1))
                if back:
                    choose(Group(b, c - 1))
                if front:
                    normed(Group(b, c + 1))
                if turning and half == 0:
                    patches_low(pair, 0)
                if back:
                    shared_gate(Group(b, c - 1))
                if mid:
                    gather_context(Group(b, c))
                if back:
                    weigh(Group(b, c - 1))
                if mid:
                    gather_image(Group(b, c), 1)
                if back:
                    weigh_sum(Group(b, c - 1))
                if mid:
                    gather_image(Group(b, c), 2)
                if back:
                    weigh_row(Group(b, c - 1))
                if mid:
                    divide_context(Group(b, c))
                if front:
                    copy_keys(Group(b, c + 1))

            turn(0, -2)
            for n in range(3):
                dve.wait_ge(wT_copied, n + 1)
                V.tensor_tensor(wT_lo[:, 2 * n:2 * n + 2, :].rearrange("p a b -> p (a b)"), ps[:, n, 0:2 * D],
                                wT_hi[:, 2 * n:2 * n + 2, :].rearrange("p a b -> p (a b)").bitcast(F32),
                                ALU.subtract).then_inc(wT_low, 1)
            for i in range(-1, 3):
                turn(0, i)
            with dve.Fori(1, PAIRS - 2) as b:
                turn(b, 1)
                turn(b, 2)
            for i in range(GROUPS - 3, GROUPS):
                turn(0, i)
            behind, last = Group(0, GROUPS - 2), Group(0, GROUPS - 1)
            place(behind)
            name_slots(behind)
            name_largest(behind)
            name_index(behind)
            residual(last)
            residual_norm(last)
            shared_add(behind)
            normed_two(last)
            choose(last)
            place(last)
            name_slots(last)
            name_largest(last)
            name_index(last)
            shared_gate(last)
            weigh(last)
            weigh_sum(last)
            weigh_row(last)
            shared_add(last)

            def hidden(e, u):
                dve.wait_ge(silu_ready, e + 1)
                if not isinstance(e, int) or e >= 2:
                    dve.wait_ge(hh_turned, e - 1)
                V.tensor_tensor(hh[u][:, :], sg[u][:, :], ps[:, u, F:2 * F], ALU.mult).then_inc(hh_ready, 1)

            def x_low(e, u):
                dve.wait_ge(x_hi_ready, e + 1)
                if not isinstance(e, int) or e >= 2:
                    dve.wait_ge(e_gu_done, e - 1)
                V.tensor_tensor(x_lo[u][:, :], ps[:, 2 + u, 0:KD * P], x_hi[u][:, :].bitcast(F32), ALU.subtract).then_inc(x_lo_ready, 1)

            def w_low(e, c):
                dve.wait_ge(w_hi_ready, e + 1)
                if not isinstance(e, int) or e >= 2:
                    dve.wait_ge(e_gu_done, e - 1)
                V.tensor_tensor(w_lo[c % 2][:, :], ew[:, bass.ds(e % RING, 1), 0:GU].rearrange("p a b -> p (a b)"),
                                w_hi[c % 2][:, :].bitcast(F32), ALU.subtract).then_inc(w_lo_ready, 1)

            def weighed(e, u, c):
                dve.wait_ge(e_down_done, e + 1)
                if not isinstance(e, int) or e >= 4:
                    dve.wait_ge(added[u], 8 * (e - u) - 16)
                V.tensor_scalar(ysc[c % 4][:, :], ps[:, 6 + u, 0:D], xrow[c][:, bass.ds(D + e, 1)], None,
                                ALU.mult).then_inc(ysc_ready, 1)

            def experts(m, first=False, last=False):
                for c in range(8):
                    e = 8 * m + c
                    hidden(e, c % 2)
                    if not (first and c == 0):
                        weighed(e - 1, (c - 1) % 2, (c - 1) % 8)
                    if not (last and c >= 6):
                        w_low(e + 2, c + 2)
                        x_low(e + 2, c % 2)

            for e in range(2):
                w_low(e, e)
                x_low(e, e)
            experts(0, first=True)
            with dve.Fori(1, E // 8 - 1) as m:
                experts(m)
            experts(E // 8 - 1, last=True)
            weighed(E - 1, 1, 7)


_INS = ['x', 'L0_tok_W', 'L0_tok_b', 'L0_tok_cls_token', 'L0_tok_pos_embedding', 'L0_attn_Wq', 'L0_attn_Wk',
        'L0_attn_Wv', 'L0_attn_Wo', 'L0_attn_bo', 'L0_ffn_router_w', 'L0_ffn_w_gate', 'L0_ffn_w_up',
        'L0_ffn_w_down', 'L0_ffn_ws_gate_up', 'L0_ffn_ws_down']
_OUTS = [((IMAGES, S, D), 'float32')]


def kernel(**inputs):
    import numpy as _np
    import concourse.bacc as _bacc
    from concourse import mybir as _mybir
    from concourse.bass_utils import run_bass_kernel_spmd as _run

    nc = _bacc.Bacc("TRN2", target_bir_lowering=False, num_devices=1)
    arrays, args = {}, []
    for name in _INS:
        a = _np.ascontiguousarray(inputs[name])
        arrays[f"in_{name}_dram"] = a
        args.append(nc.dram_tensor(f"in_{name}_dram", a.shape, _mybir.dt.from_np(a.dtype), kind="ExternalInput").ap())
    for i, (shape, dtype) in enumerate(_OUTS):
        dt = _mybir.dt.from_np(_np.dtype(dtype))
        args.append(nc.dram_tensor(f"out_{i}_dram", shape, dt, kind="ExternalOutput").ap())
    vit_kernel(nc, *args)
    r = _run(nc, [arrays], core_ids=[0])
    got = tuple(r.results[0][f"out_{i}_dram"] for i in range(len(_OUTS)))
    return got[0]
```
